# Optimizing a Trainium2 kernel written in Bass

```python
import numpy as np
import jax
import jax.numpy as jnp

def _softmax(x, axis=-1):
    return jax.nn.softmax(x, axis=axis)

def _gelu(x):
    return jax.nn.gelu(x, approximate=True)

def _silu(x):
    return jax.nn.silu(x)

def _sigmoid(x):
    return jax.nn.sigmoid(x)

def _layernorm(x, axis=-1, eps=1e-05):
    m = jnp.mean(x, axis=axis, keepdims=True)
    v = jnp.var(x, axis=axis, keepdims=True)
    return (x - m) / jnp.sqrt(v + eps)

def _scatter_add(tgt, idx, src, axis=0):
    return tgt.at[idx].add(src)

def _segment_sum(src, seg, n):
    return jax.ops.segment_sum(src, seg, n)
kernel_name = 'mk_macaron_d2_jaxref_r8_ea7215'

def setup_inputs(seed: int=0):
    np.random.seed(seed)
    _w = jnp.asarray

    def _L0_attn_setup():
        import jax, jax.numpy as jnp
        import numpy as np
        B, S, D_IN, D_OUT, H = (2, 256, 128, 128, 16)
        HD = D_OUT // H
        key = jax.random.key(seed)
        ks = jax.random.split(key, 6)
        x = jax.random.normal(ks[0], (B, S, D_IN), jnp.float32)
        Wq = jax.random.normal(ks[1], (D_IN, D_OUT), jnp.float32) * 0.02
        Wk = jax.random.normal(ks[2], (D_IN, D_OUT), jnp.float32) * 0.02
        Wv = jax.random.normal(ks[3], (D_IN, D_OUT), jnp.float32) * 0.02
        Wo = jax.random.normal(ks[4], (D_OUT, D_OUT), jnp.float32) * 0.02
        bo = jax.random.normal(ks[5], (D_OUT,), jnp.float32) * 0.02
        return {'x': x, 'Wq': Wq, 'Wk': Wk, 'Wv': Wv, 'Wo': Wo, 'bo': bo}
    _L0_attn_in = _L0_attn_setup()

    def _L0_ffn_setup():
        import jax, jax.numpy as jnp
        import numpy as np
        H, I, E, K = (128, 64, 32, 8)
        B, S = (4, 128)

        def silu(x):
            return x * jax.nn.sigmoid(x)
        key = jax.random.key(seed)
        ks = jax.random.split(key, 14)

        def w(k, shape, fan_in):
            return jax.random.normal(k, shape, jnp.float32) / np.float32(np.sqrt(fan_in))
        return {'hidden_states': jax.random.normal(ks[0], (B, S, H), jnp.float32), 'Wr': w(ks[1], (H, E), H), 'br': jnp.zeros((E,), jnp.float32), 'Wg_s': w(ks[2], (H, I), H), 'bg_s': jnp.zeros((I,), jnp.float32), 'Wu_s': w(ks[3], (H, I), H), 'bu_s': jnp.zeros((I,), jnp.float32), 'Wd_s': w(ks[4], (I, H), I), 'bd_s': jnp.zeros((H,), jnp.float32), 'Wg': w(ks[5], (E, H, I), H), 'bg': jnp.zeros((E, I), jnp.float32), 'Wu': w(ks[6], (E, H, I), H), 'bu': jnp.zeros((E, I), jnp.float32), 'Wd': w(ks[7], (E, I, H), I), 'bd': jnp.zeros((E, H), jnp.float32)}
    _L0_ffn_in = _L0_ffn_setup()

    def _L1_attn_setup():
        import jax, jax.numpy as jnp
        import numpy as np
        B, S, D, H = (4, 256, 128, 16)
        HD = D // H
        LN_EPS = 1e-05
        KERN_EPS = 1e-06

        def kernel_func(q, k):
            scores = jnp.einsum('bhqd,bhkd->bhqk', q, k) / jnp.sqrt(jnp.asarray(HD, q.dtype))
            w = jax.nn.relu(scores)
            return w / (jnp.sum(w, axis=-1, keepdims=True) + KERN_EPS)
        key = jax.random.key(seed)
        k1, k2, k3 = jax.random.split(key, 3)
        scale = 1.0 / np.sqrt(D)
        return {'x': jax.random.normal(k1, (B, S, D), dtype=jnp.float32), 'w_qkv': jax.random.normal(k2, (D, 3 * D), dtype=jnp.float32) * scale, 'w_out': jax.random.normal(k3, (D, D), dtype=jnp.float32) * scale, 'b_out': jnp.zeros((D,), dtype=jnp.float32), 'gamma': jnp.ones((D,), dtype=jnp.float32), 'beta': jnp.zeros((D,), dtype=jnp.float32)}
    _L1_attn_in = _L1_attn_setup()

    def _L1_ffn_setup():
        import jax, jax.numpy as jnp
        import numpy as np
        EMBED = 128
        NUM_EXPERTS = 8
        ACTIVE = 2
        HIDDEN = 4 * EMBED
        key = jax.random.key(seed)
        ks = jax.random.split(key, 7)
        B, T = (4, 128)
        s1 = 1.0 / np.sqrt(EMBED)
        s2 = 1.0 / np.sqrt(HIDDEN)
        return {'x': jax.random.normal(ks[0], (B, T, EMBED), dtype=jnp.float32), 'W1': jax.random.uniform(ks[1], (NUM_EXPERTS, EMBED, HIDDEN), jnp.float32, -s1, s1), 'b1': jax.random.uniform(ks[2], (NUM_EXPERTS, HIDDEN), jnp.float32, -s1, s1), 'W2': jax.random.uniform(ks[3], (NUM_EXPERTS, HIDDEN, EMBED), jnp.float32, -s2, s2), 'b2': jax.random.uniform(ks[4], (NUM_EXPERTS, EMBED), jnp.float32, -s2, s2), 'Wr': jax.random.uniform(ks[5], (EMBED, NUM_EXPERTS), jnp.float32, -s1, s1), 'br': jax.random.uniform(ks[6], (NUM_EXPERTS,), jnp.float32, -s1, s1)}
    _L1_ffn_in = _L1_ffn_setup()
    _d = {'L0_attn_x': _L0_attn_in['x'], 'L0_attn_Wq': _L0_attn_in['Wq'], 'L0_attn_Wk': _L0_attn_in['Wk'], 'L0_attn_Wv': _L0_attn_in['Wv'], 'L0_attn_Wo': _L0_attn_in['Wo'], 'L0_attn_bo': _L0_attn_in['bo'], 'L0_ffn_Wr': _L0_ffn_in['Wr'], 'L0_ffn_br': _L0_ffn_in['br'], 'L0_ffn_Wg_s': _L0_ffn_in['Wg_s'], 'L0_ffn_bg_s': _L0_ffn_in['bg_s'], 'L0_ffn_Wu_s': _L0_ffn_in['Wu_s'], 'L0_ffn_bu_s': _L0_ffn_in['bu_s'], 'L0_ffn_Wd_s': _L0_ffn_in['Wd_s'], 'L0_ffn_bd_s': _L0_ffn_in['bd_s'], 'L0_ffn_Wg': _L0_ffn_in['Wg'], 'L0_ffn_bg': _L0_ffn_in['bg'], 'L0_ffn_Wu': _L0_ffn_in['Wu'], 'L0_ffn_bu': _L0_ffn_in['bu'], 'L0_ffn_Wd': _L0_ffn_in['Wd'], 'L0_ffn_bd': _L0_ffn_in['bd'], 'L1_attn_w_qkv': _L1_attn_in['w_qkv'], 'L1_attn_w_out': _L1_attn_in['w_out'], 'L1_attn_b_out': _L1_attn_in['b_out'], 'L1_attn_gamma': _L1_attn_in['gamma'], 'L1_attn_beta': _L1_attn_in['beta'], 'L1_ffn_W1': _L1_ffn_in['W1'], 'L1_ffn_b1': _L1_ffn_in['b1'], 'L1_ffn_W2': _L1_ffn_in['W2'], 'L1_ffn_b2': _L1_ffn_in['b2'], 'L1_ffn_Wr': _L1_ffn_in['Wr'], 'L1_ffn_br': _L1_ffn_in['br']}
    _x0 = _d['L0_attn_x']
    _d['L0_attn_x'] = jax.random.normal(jax.random.fold_in(jax.random.key(seed), 1), (8, 512, 128), dtype=_x0.dtype)
    del _x0
    return _d

def reference(L0_attn_x, L0_attn_Wq, L0_attn_Wk, L0_attn_Wv, L0_attn_Wo, L0_attn_bo, L0_ffn_Wr, L0_ffn_br, L0_ffn_Wg_s, L0_ffn_bg_s, L0_ffn_Wu_s, L0_ffn_bu_s, L0_ffn_Wd_s, L0_ffn_bd_s, L0_ffn_Wg, L0_ffn_bg, L0_ffn_Wu, L0_ffn_bu, L0_ffn_Wd, L0_ffn_bd, L1_attn_w_qkv, L1_attn_w_out, L1_attn_b_out, L1_attn_gamma, L1_attn_beta, L1_ffn_W1, L1_ffn_b1, L1_ffn_W2, L1_ffn_b2, L1_ffn_Wr, L1_ffn_br):

    def _L0_attn_ref(x, Wq, Wk, Wv, Wo, bo):
        import jax, jax.numpy as jnp
        import numpy as np
        B, S, D_IN, D_OUT, H = (2, 256, 128, 128, 16)
        HD = D_OUT // H
        b, s, _ = x.shape

        def to_heads(t):
            return t.reshape(b, s, H, HD).transpose(0, 2, 1, 3)
        Q = to_heads(x @ Wq)
        K = to_heads(x @ Wk)
        V = to_heads(x @ Wv)
        scale = 1.0 / jnp.sqrt(jnp.asarray(HD, x.dtype))
        scores = jnp.einsum('bhqd,bhkd->bhqk', Q, K) * scale
        causal_mask = jnp.triu(jnp.ones((s, s), dtype=bool), k=1)
        scores = jnp.where(causal_mask, jnp.asarray(-1000000.0, scores.dtype), scores)
        weights = jax.nn.softmax(scores, axis=-1)
        attn = jnp.einsum('bhqk,bhkd->bhqd', weights, V)
        attn = attn.reshape(b, s, D_OUT)
        return attn @ Wo + bo

    def _L0_ffn_ref(hidden_states, Wr, br, Wg_s, bg_s, Wu_s, bu_s, Wd_s, bd_s, Wg, bg, Wu, bu, Wd, bd):
        import jax, jax.numpy as jnp
        import numpy as np
        H, I, E, K = (128, 64, 32, 8)
        B, S = (4, 128)

        def silu(x):
            return x * jax.nn.sigmoid(x)
        b, s, h = hidden_states.shape
        T = b * s
        x = hidden_states.reshape(T, h)
        logits = jnp.dot(x.astype(jnp.float32), Wr) + br
        aff = jax.nn.sigmoid(logits)
        top_v, top_i = jax.lax.top_k(aff, K)
        top_w = top_v / (jnp.sum(top_v, axis=-1, keepdims=True) + 1e-09)
        top_w = top_w.astype(hidden_states.dtype)
        e_total = Wr.shape[1]
        w_full = jnp.zeros((T, e_total), hidden_states.dtype)
        w_full = w_full.at[jnp.arange(T)[:, None], top_i].set(top_w)
        shared = jnp.dot(silu(jnp.dot(x, Wg_s) + bg_s) * (jnp.dot(x, Wu_s) + bu_s), Wd_s) + bd_s
        gate = silu(jnp.einsum('th,ehi->eti', x, Wg) + bg[:, None, :])
        up = jnp.einsum('th,ehi->eti', x, Wu) + bu[:, None, :]
        down = jnp.einsum('eti,eih->eth', gate * up, Wd) + bd[:, None, :]
        routed = jnp.einsum('te,eth->th', w_full, down)
        return (shared + routed).reshape(b, s, h)

    def _L1_attn_ref(x, w_qkv, w_out, b_out, gamma, beta):
        import jax, jax.numpy as jnp
        import numpy as np
        B, S, D, H = (4, 256, 128, 16)
        HD = D // H
        LN_EPS = 1e-05
        KERN_EPS = 1e-06

        def kernel_func(q, k):
            scores = jnp.einsum('bhqd,bhkd->bhqk', q, k) / jnp.sqrt(jnp.asarray(HD, q.dtype))
            w = jax.nn.relu(scores)
            return w / (jnp.sum(w, axis=-1, keepdims=True) + KERN_EPS)
        Bx, Sx, _ = x.shape
        qkv = (x @ w_qkv).reshape(Bx, Sx, H, 3 * HD)
        q, k, v = jnp.split(qkv, 3, axis=-1)
        q = q.transpose(0, 2, 1, 3)
        k = k.transpose(0, 2, 1, 3)
        v = v.transpose(0, 2, 1, 3)
        attn = kernel_func(q, k)
        out = jnp.einsum('bhqk,bhkd->bhqd', attn, v)
        out = out.transpose(0, 2, 1, 3).reshape(Bx, Sx, D)
        out = out @ w_out + b_out
        y = x + out
        mu = jnp.mean(y, axis=-1, keepdims=True)
        var = jnp.var(y, axis=-1, keepdims=True)
        return (y - mu) * jax.lax.rsqrt(var + LN_EPS) * gamma + beta

    def _L1_ffn_ref(x, W1, b1, W2, b2, Wr, br):
        import jax, jax.numpy as jnp
        import numpy as np
        EMBED = 128
        NUM_EXPERTS = 8
        ACTIVE = 2
        HIDDEN = 4 * EMBED
        scores = x @ Wr + br
        topk_scores, indices = jax.lax.top_k(scores, ACTIVE)
        one_hot = jax.nn.one_hot(indices, NUM_EXPERTS, dtype=scores.dtype)
        mask = jnp.einsum('btke,btk->bte', one_hot, topk_scores)
        router_output = jax.nn.softmax(mask, axis=-1)
        h = jax.nn.relu(jnp.einsum('btd,edh->bteh', x, W1) + b1)
        expert_outputs = jnp.einsum('bteh,ehd->bted', h, W2) + b2
        return jnp.einsum('bte,bted->btd', router_output, expert_outputs)
    x = L0_attn_x
    x = x + 0.5 * _L0_ffn_ref(_layernorm(x, axis=-1), L0_ffn_Wr, L0_ffn_br, L0_ffn_Wg_s, L0_ffn_bg_s, L0_ffn_Wu_s, L0_ffn_bu_s, L0_ffn_Wd_s, L0_ffn_bd_s, L0_ffn_Wg, L0_ffn_bg, L0_ffn_Wu, L0_ffn_bu, L0_ffn_Wd, L0_ffn_bd)
    x = x + _L0_attn_ref(_layernorm(x, axis=-1), L0_attn_Wq, L0_attn_Wk, L0_attn_Wv, L0_attn_Wo, L0_attn_bo)
    x = x + 0.5 * _L0_ffn_ref(_layernorm(x, axis=-1), L0_ffn_Wr, L0_ffn_br, L0_ffn_Wg_s, L0_ffn_bg_s, L0_ffn_Wu_s, L0_ffn_bu_s, L0_ffn_Wd_s, L0_ffn_bd_s, L0_ffn_Wg, L0_ffn_bg, L0_ffn_Wu, L0_ffn_bu, L0_ffn_Wd, L0_ffn_bd)
    x = x + 0.5 * _L1_ffn_ref(_layernorm(x, axis=-1), L1_ffn_W1, L1_ffn_b1, L1_ffn_W2, L1_ffn_b2, L1_ffn_Wr, L1_ffn_br)
    x = x + _L1_attn_ref(_layernorm(x, axis=-1), L1_attn_w_qkv, L1_attn_w_out, L1_attn_b_out, L1_attn_gamma, L1_attn_beta)
    x = x + 0.5 * _L1_ffn_ref(_layernorm(x, axis=-1), L1_ffn_W1, L1_ffn_b1, L1_ffn_W2, L1_ffn_b2, L1_ffn_Wr, L1_ffn_br)
    return x

_drawn_inputs = setup_inputs


def setup_inputs(seed=0):
    import zlib

    import numpy as np

    out = dict(_drawn_inputs(seed))
    spreads = {'L0_ffn_br': (0.0, 0.1),
     'L0_ffn_bg_s': (0.0, 0.1),
     'L0_ffn_bu_s': (0.0, 0.1),
     'L0_ffn_bd_s': (0.0, 0.1),
     'L0_ffn_bg': (0.0, 0.385),
     'L0_ffn_bu': (0.0, 0.4),
     'L0_ffn_bd': (0.0, 0.1),
     'L1_attn_b_out': (0.0, 0.1),
     'L1_attn_gamma': (1.0, 0.2),
     'L1_attn_beta': (0.0, 0.1)}
    factors = {'L0_attn_Wq': 8.0,
     'L0_attn_Wk': 8.0,
     'L0_attn_Wv': 7.258,
     'L0_attn_Wo': 7.002,
     'L1_ffn_b1': 8.0,
     'L1_ffn_b2': 8.0,
     'L1_ffn_br': 8.0,
     'L0_attn_bo': 3.555}
    for name, (base, spread) in spreads.items():
        noise = np.random.default_rng([zlib.crc32(name.encode()), seed]).standard_normal(out[name].shape)
        drawn = base * np.exp(spread * noise) if base else spread * noise
        out[name] = jnp.asarray(drawn.astype(out[name].dtype))
    for name, factor in factors.items():
        out[name] = (out[name] * factor).astype(out[name].dtype)
    return out
```

```python
from contextlib import ExitStack

import numpy as np
import concourse.bass as bass
from concourse import mybir

ALU = mybir.AluOpType
ACT = mybir.ActivationFunctionType
AX_X = mybir.AxisListType.X
F32 = mybir.dt.float32
F32R = mybir.dt.float32r
BF16 = mybir.dt.bfloat16
U32 = mybir.dt.uint32

P = 128
D = 128
NB, S = 8, 512
NT = S // P
H, HD = 16, 8
E0, K0, I0 = 32, 8, 64
NP = E0 // 2
NPS = NP + 1
E1, I1 = 8, 512
HC = I1 // P
NJ = E1 * HC
LN_EPS = 1e-5
KERN_EPS = 1e-6
SCALE = float(HD) ** -0.5
NPART = 3
PAIRS = 6
Q_PART = (0, 0, 1, 1, 0, 2)
K_PART = (0, 1, 0, 1, 2, 0)
QK_ROWS = PAIRS * HD
MAX_ROW = QK_ROWS
STACK = 64
HALF = H // 2
GQ = D // HD

GATE0, UP0, DOWN0, WR0 = 0, NPS, 2 * NPS, 3 * NPS
NW0 = 3 * NPS + 1
UP1, DOWN1, WR1 = 0, NJ, 2 * NJ
NW1 = 2 * NJ + 1
WQ, WK, WV, WO = range(4)
BG, BU, BDS, BR0, B1, B2, BR1 = 0, NPS, 2 * NPS, 2 * NPS + 1, 2 * NPS + 2, 2 * NPS + 2 + NJ, 2 * NPS + 2 + NJ + E1
NBIAS = BR1 + 1
C_ID, C_NEG, C_NEGT, C_SEL0, C_SEL1 = 0, P, 2 * P, 3 * P, 3 * P + NP * P
NCONST = C_SEL1 + E1 * P

STAGES = ("ffn0", "attn0", "ffn0", "ffn1", "attn1", "ffn1")
LAG = 3
NH = 4
ONE = 1
LOAD = 1024


class Steps:

    def __init__(self, sem, per):
        self.sem, self.per = sem, per

    def begin(self, visit):
        self.base, self.k = visit * self.per, 0

    def mark(self, ins):
        ins.then_inc(self.sem, 1)
        self.k += 1
        return self.base + self.k

    def end(self):
        assert self.k == self.per, (self.k, self.per)


def build(nc, x_in, w0, w1, wa, biases, bd3, rows, consts, out, scratch, mixed):
    nc.disable_value_cache = True
    ctx = ExitStack()
    with ctx:
        def sb(name, shape, dt, stack=ctx):
            return stack.enter_context(nc.sbuf_tensor(name, shape, dt))

        def sem(name):
            return ctx.enter_context(nc.semaphore(name))

        x = sb("x", [P, NB * NT, D], F32)
        w0_hi, w0_lo = sb("w0_hi", [P, NW0, P], F32R), sb("w0_lo", [P, NW0, P], F32R)
        w1_hi, w1_lo = sb("w1_hi", [P, NW1, P], F32R), sb("w1_lo", [P, NW1, P], F32R)
        wa_hi, wa_lo = sb("wa_hi", [P, 2, 4, P], F32R), sb("wa_lo", [P, 2, 4, P], F32R)
        bias = sb("bias", [P, NBIAS], F32)
        row = sb("row", [P, 4, D], F32)
        ident = sb("ident", [P, P], F32)
        cbf = sb("cbf", [P, NCONST], BF16)
        bd_parts = sb("bd_parts", [96, NPART, D], BF16)
        xn = sb("xn", [P, NT, D], F32)
        xnT_hi, xnT_lo = sb("xnT_hi", [P, S], F32R), sb("xnT_lo", [P, S], F32R)
        stats, mv = sb("stats", [P, NT, 6], F32), sb("mv", [P, NT, 2], F32)
        ve, rstd = sb("ve", [P, NT], F32), sb("rstd", [P, NT], F32)
        mhalf = sb("mhalf", [P, NT], F32)

        with ExitStack() as part:
            stage_w = sb("stage_w", [P, 4, LOAD], F32, part)
            stage_c = sb("stage_c", [P, NCONST], F32, part)
            stage_bd = sb("stage_bd", [96, 2, D], F32, part)
        with ExitStack() as part:
            gate = sb("gate", [P, 2, S], F32, part)
            prod = sb("prod", [P, 2, S], F32, part)
            hid = sb("hid", [P, 3, S], F32, part)
            h_hi, h_lo = sb("h_hi", [P, NH, S], F32R, part), sb("h_lo", [P, NH, S], F32R, part)
            wT = sb("wT", [96, S], BF16, part)
            yT = sb("yT", [P, S], F32, part)
            lgT = sb("lgT", [E0, S], F32, part)
            aff, sel, wgt = (sb(n, [P, NT, E0], F32, part) for n in ("aff", "sel", "wgt"))
            m8 = sb("m8", [P, NT, 8], F32, part)
            i8 = sb("i8", [P, NT, 8], U32, part)
            i8f = sb("i8f", [P, NT, 8], F32, part)
            iota8 = sb("iota8", [P, NT, 8], F32, part)
            den = sb("den", [P, 2, NT], F32, part)
            wparts = sb("wparts", [P, NT, NPART * E0], BF16, part)
        rb, zed = gate, prod
        with ExitStack() as part:
            q_st = sb("q_st", [P, H // 2, S], BF16, part)
            k_st = sb("k_st", [P, H // 2, S], BF16, part)
            probs = sb("probs", [P, 2, NT, S], F32, part)
            parts = sb("parts", [P, 2, NPART, S], BF16, part)
            v9 = sb("v9", [P, NT, H, HD + 1], F32, part)
            rmax = sb("rmax", [P, NT, H], F32, part)
            nmax = sb("nmax", [P, 2, NT, HALF], F32, part)
            mparts = sb("mparts", [P, NT, NPART, HALF], BF16, part)
            mT = sb("mT", [NPART * HALF, 2, S], BF16, part)
            rden = sb("rden", [P, 2, NT * HALF], F32, part)
            attn = sb("attn", [P, NT, H, HD], F32, part)
            aT_hi, aT_lo = sb("aT_hi", [P, S], F32R, part), sb("aT_lo", [P, S], F32R, part)

        qkv, res = probs[:, 0, 0:3, :], probs[:, 1, 0:2, :]
        aT_perm, aT_mix = probs[:, 0, 0, :], probs[:, 0, 1, :]

        bank = [ctx.enter_context(nc.psum_tensor(f"bank{i}", [P, S], F32)) for i in range(8)]
        bank6, bank7 = bank[6], bank[7]
        bank7h = bank7[:, :].bitcast(BF16)
        identb = cbf[:, C_ID:C_ID + P]
        neg, negT = cbf[:, C_NEG:C_NEG + P], cbf[:, C_NEGT:C_NEGT + P]

        x_in_sem, small_in = sem("x_in_sem"), sem("small_in")
        w_in = [sem(f"w_in{i}") for i in range(4)]
        w_hi_done, w_lo_done = sem("w_hi_done"), sem("w_lo_done")
        const_ready, pool_init = sem("const_ready"), sem("pool_init")
        ln_steps = Steps(sem("ln_steps"), 13)
        rstd_ready, xn_ready, xnT_ps, xnT_hi_ready, xnT_lo_ready = map(sem, (
            "rstd_ready", "xn_ready", "xnT_ps", "xnT_hi_ready", "xnT_lo_ready"))
        lgT_ps, lgT_ready, lg_ps, aff_ready, wparts_ready, wT_ps, wT_ready = map(sem, (
            "lgT_ps", "lgT_ready", "lg_ps", "aff_ready", "wparts_ready", "wT_ps", "wT_ready"))
        top0 = Steps(sem("top0_steps"), 18)
        top1 = Steps(sem("top1_steps"), 22)
        mx_ready, e_ready = sem("mask_ready"), sem("exp_ready")
        g_ready, u_ready, wb_ready = sem("g_ready"), sem("u_ready"), sem("wb_ready")
        silu_ready, prod_ready, hid_ready = sem("silu_ready"), sem("prod_ready"), sem("hid_ready")
        hi_ready, lo_ready, h_used = sem("hi_ready"), sem("lo_ready"), sem("h_used")
        y_ps, yT_ready, y_tok = sem("y_ps"), sem("yT_ready"), sem("y_tok")
        x_done = sem("x_done")
        u1_ready, hid1_ready, hi1a_ready, hi1v_ready, lo1p_ready, lo1v_ready, h1_used = map(sem, (
            "u1_ready", "hid1_ready", "hi1a_ready", "hi1v_ready", "lo1p_ready", "lo1v_ready", "h1_used"))
        rb_ps, rb_ready, ze_ready, acc_ready = map(sem, ("rb_ps", "rb_ready", "ze_ready", "acc_ready"))
        y1_tok = sem("y1_tok")
        qkv_ps, qkv_ready, vT_ps, v9_ready = map(sem, ("qkv_ps", "qkv_ready", "vT_ps", "v9_ready"))
        q_steps, k_steps = Steps(sem("q_steps"), 5), Steps(sem("k_steps"), 5)
        scr_w, st_in = sem("scratch_written"), [sem("stack_in0"), sem("stack_in1")]
        s_ready, s_used, m_steps = sem("s_ready"), sem("s_used"), Steps(sem("m_steps"), 10)
        mT_ps, mT_ready = sem("mT_ps"), sem("mT_ready")
        m_in = [sem("m_in0"), sem("m_in1")]
        st_ready, p_ready, pv_done = sem("st_ready"), sem("p_ready"), sem("pv_done")
        attn_steps = Steps(sem("attn_steps"), 4)
        aT_ps, aT_hi_ready, aT_lo_ready, o_ps = map(sem, ("aT_ps", "aT_hi_ready", "aT_lo_ready", "o_ps"))
        tail = Steps(sem("tail_steps"), 17)
        x_mid = sem("x_mid")
        tail_var, tail_rstd, tail_eps = sem("tail_var"), sem("tail_rstd"), sem("tail_eps")
        perm_ready, perm_out, mix_in = sem("perm_ready"), sem("perm_out"), sem("mix_in")
        out_sem = sem("out_sem")

        loads = []
        for src, hi, lo, n in ((w0, w0_hi, w0_lo, NW0 * P), (wa, wa_hi, wa_lo, 8 * P), (w1, w1_hi, w1_lo, NW1 * P)):
            hif = hi.rearrange("p a b -> p (a b)") if len(hi.shape) == 3 else hi.rearrange("p a b c -> p (a b c)")
            lof = lo.rearrange("p a b -> p (a b)") if len(lo.shape) == 3 else lo.rearrange("p a b c -> p (a b c)")
            for a in range(0, n, LOAD):
                b = min(n, a + LOAD)
                loads.append((src[:, a:b], hif[:, a:b], lof[:, a:b], b - a))

        passed = {}

        def settle(eng):
            if eng.engine not in passed:
                passed[eng.engine] = sem(f"passed{len(passed)}")
            eng.sem_inc(passed[eng.engine], 1)

        def products(eng, o, w_hi_, w_lo_, v_hi, v_lo, start=True, stop=True, **kw):
            eng.matmul(o, w_hi_, v_hi, start=start, stop=False, **kw)
            eng.matmul(o, w_hi_, v_lo, start=False, stop=False, **kw)
            return eng.matmul(o, w_lo_, v_hi, start=False, stop=stop, **kw)

        nth = [STAGES[:s].count(STAGES[s]) for s in range(len(STAGES))]
        nffn = [sum(a[:3] == "ffn" for a in STAGES[:s]) for s in range(len(STAGES))]
        nattn = [sum(a[:4] == "attn" for a in STAGES[:s]) for s in range(len(STAGES))]
        ph_s = lambda: 0

        def chunks(eng, body):
            for s, kind in enumerate(STAGES):
                with eng.Fori(0, NB) as c:
                    body(s, kind, c)

        def split_parts(eng, steps, ga, i):
            steps.begin(ga)
            settle(eng)
            v = steps.mark(eng.tensor_copy(parts[:, i, 0, :], qkv[:, i, :]))
            eng.wait_ge(steps.sem, v)
            v = steps.mark(eng.tensor_tensor(res[:, i, :], qkv[:, i, :], parts[:, i, 0, :], ALU.subtract))
            eng.wait_ge(steps.sem, v)
            settle(eng)
            v = steps.mark(eng.tensor_copy(parts[:, i, 1, :], res[:, i, :]))
            eng.wait_ge(steps.sem, v)
            v = steps.mark(eng.tensor_tensor(res[:, i, :], res[:, i, :], parts[:, i, 1, :], ALU.subtract))
            eng.wait_ge(steps.sem, v)
            settle(eng)
            steps.mark(eng.tensor_copy(parts[:, i, 2, :], res[:, i, :]))
            steps.end()

        def router_act(eng, s, kind, c):
            gr = nffn[s] * NB + c
            ne, br = (E0, BR0) if kind == "ffn0" else (E1, BR1)
            eng.wait_ge(lgT_ps, gr + 1)
            eng.activation(lgT[0:ne, :], bank7[0:ne, :], ACT.Identity, bias=bias[0:ne, br:br + 1]).then_inc(lgT_ready, 1)
            eng.wait_ge(lg_ps, gr + 1)
            src = bank7[:, 0:NT * ne].rearrange("p (t e) -> p t e", e=ne)
            eng.activation(aff[:, :, 0:ne], src, ACT.Sigmoid if kind == "ffn0" else ACT.Copy).then_inc(aff_ready, 1)
            if kind == "ffn1":
                g = nth[s] * NB + c
                eng.wait_ge(mx_ready, g + 1)
                eng.activation(wgt[:, :, 0:E1], sel[:, :, 0:E1], ACT.Exp).then_inc(e_ready, 1)
            eng.wait_ge(wT_ps, gr + 1)
            eng.activation(wT[0:NPART * ne, :], bank7h[0:NPART * ne, 0:S], ACT.Copy).then_inc(wT_ready, 1)

        def ffn0_act(eng, g):
            def hi_part(p):
                eng.wait_ge(hid_ready, ONE + g * NPS + p + 1)
                if p >= NH:
                    eng.wait_ge(h_used, ONE + g * NPS + p - NH + 1)
                else:
                    eng.wait_ge(h_used, ONE + g * NPS)
                eng.activation(h_hi[:, p % NH, :], hid[:, p % 3, :], ACT.Copy).then_inc(hi_ready, 1)

            for p in range(NPS):
                eng.wait_ge(g_ready, g * NPS + p + 1)
                if p >= 2:
                    eng.wait_ge(prod_ready, ONE + g * NPS + p - 1)
                else:
                    eng.wait_ge(prod_ready, ONE + g * NPS)
                eng.activation(gate[:, p % 2, :], bank[p % 2][:, :], ACT.Silu, bias=bias[:, BG + p:BG + p + 1]).then_inc(silu_ready, 1)
                if p >= 1:
                    hi_part(p - 1)
            hi_part(NPS - 1)
            eng.wait_ge(y_ps, g + 1)
            eng.activation(yT[:, :], bank[5][:, :], ACT.Identity, bias=bias[:, BDS:BDS + 1]).then_inc(yT_ready, 1)

        def ffn1_act(eng, g):
            def hi_part(j):
                eng.wait_ge(hid1_ready, ONE + g * NJ + j + 1)
                eng.wait_ge(h1_used, ONE + g * NJ + (j - NH + 1 if j >= NH else 0))
                eng.activation(h_hi[:, j % NH, :], hid[:, j % 3, :], ACT.Copy).then_inc(hi1a_ready, 1)

            for j in range(NJ):
                if j % HC == 0:
                    e = j // HC
                    eng.wait_ge(rb_ps, g * E1 + e + 1)
                    eng.wait_ge(ze_ready, ONE + g * E1 + (e - 1 if e >= 2 else 0))
                    eng.activation(rb[:, e % 2, :], bank[4][:, :], ACT.Copy).then_inc(rb_ready, 1)
                eng.wait_ge(u1_ready, g * NJ + j + 1)
                if j >= 3:
                    q = j - 3
                    if q % 2 == 0:
                        eng.wait_ge(lo1p_ready, ONE + g * (NJ // 2) + q // 2 + 1)
                    else:
                        eng.wait_ge(lo1v_ready, ONE + g * (NJ // 2) + q // 2 + 1)
                else:
                    eng.wait_ge(lo1p_ready, ONE + g * (NJ // 2))
                    eng.wait_ge(lo1v_ready, ONE + g * (NJ // 2))
                eng.activation(hid[:, j % 3, :], bank[j % 3][:, :], ACT.Relu, bias=bias[:, B1 + j:B1 + j + 1]).then_inc(hid1_ready, 1)
                if j % 2 == 0:
                    hi_part(j)

        def attn_act(eng, kind, ga, gk):
            causal = kind == "attn0"
            for i in range(3):
                eng.wait_ge(qkv_ps, 3 * ga + i + 1)
                eng.activation(qkv[:, i, :], bank[i][:, :], ACT.Copy, scale=SCALE if i == 0 else 1.0).then_inc(qkv_ready, 1)
            eng.wait_ge(vT_ps, ga + 1)
            for t in range(NT):
                ins = eng.activation(v9[:, t, :, 0:HD], bank7[:, t * P:(t + 1) * P].rearrange("p (h d) -> p h d", d=HD), ACT.Copy)
                ins.then_inc(v9_ready, 1)
            if causal:
                for half in range(2):
                    eng.wait_ge(mT_ps, ONE + 2 * gk + half + 1)
                    eng.activation(mT[:, half, :], bank7h[0:NPART * HALF, 0:S], ACT.Copy).then_inc(mT_ready, 1)
            for h in range(H):
                for kb in range(NT):
                    n = (ga * H + h) * NT + kb
                    q0 = kb * P if causal else 0
                    eng.wait_ge(st_ready, n + 1)
                    if kb == 0:
                        eng.wait_ge(pv_done, ONE + ga * H + (h - 1 if h >= 2 else 0))
                    eng.activation(probs[:, h % 2, kb, q0:S], bank[kb][:, 0:S - q0], ACT.Exp if causal else ACT.Relu).then_inc(p_ready, 1)
            eng.wait_ge(aT_ps, ONE + ga + 1)
            if causal:
                eng.activation(aT_perm[:, :].rearrange("p (q r) -> p r q", q=GQ),
                               bank6[:, :].rearrange("p (r q) -> p r q", q=GQ), ACT.Copy).then_inc(perm_ready, 1)
                eng.wait_ge(mix_in, 16 * GQ * (gk + 1))
                eng.activation(aT_hi[:, :], aT_mix[:, :], ACT.Copy).then_inc(aT_hi_ready, 1)
            else:
                eng.activation(aT_hi[:, :], bank6[:, :], ACT.Copy).then_inc(aT_hi_ready, 1)

        def layernorm(eng, steps, visit, src):
            steps.begin(visit)
            for t in range(NT):
                v = steps.mark(eng.bn_stats(stats[:, t, :], src[:, t, :]))
            eng.wait_ge(steps.sem, v)
            settle(eng)
            for t in range(NT):
                v = steps.mark(eng.bn_aggr(mv[:, t, :], stats[:, t, :]))
            eng.wait_ge(steps.sem, v)
            steps.mark(eng.tensor_scalar(ve[:, :], mv[:, :, 1], LN_EPS, None, ALU.add))
            eng.wait_ge(rstd_ready, visit + 1)
            eng.wait_ge(xnT_ps, ONE + visit)
            for t in range(NT):
                v = steps.mark(eng.tensor_scalar(xn[:, t, :], src[:, t, :], mv[:, t, 0:1], rstd[:, t:t + 1],
                                                 ALU.subtract, ALU.mult))
            steps.end()

        def split3(eng, steps, ne):
            for i in range(NPART):
                src = wgt if i == 0 else sel
                v = steps.mark(eng.tensor_copy(wparts[:, :, i * ne:(i + 1) * ne], src[:, :, 0:ne]))
                eng.wait_ge(steps.sem, v)
                if i < 2:
                    v = steps.mark(eng.tensor_tensor(sel[:, :, 0:ne], src[:, :, 0:ne], wparts[:, :, i * ne:(i + 1) * ne], ALU.subtract))
                    eng.wait_ge(steps.sem, v)

        def router0_dve(eng, s, c):
            st = top0
            st.begin(nth[s] * NB + c)
            eng.wait_ge(aff_ready, nffn[s] * NB + c + 1)
            settle(eng)
            for t in range(NT):
                v = st.mark(eng.max(m8[:, t, :], aff[:, t, :]))
            eng.wait_ge(st.sem, v)
            settle(eng)
            for t in range(NT):
                st.mark(eng.match_replace(sel[:, t, :], m8[:, t, :], aff[:, t, :], -1.0))
            v = st.mark(eng.tensor_reduce(den[:, 0, :], m8[:, :, :], AX_X, ALU.add))
            eng.wait_ge(st.sem, v)
            v = st.mark(eng.tensor_scalar(den[:, 0, :], den[:, 0, :], 1e-9, None, ALU.add))
            eng.wait_ge(st.sem, v)
            v = st.mark(eng.reciprocal(den[:, 1, :], den[:, 0, :]))
            v = st.mark(eng.tensor_tensor(sel[:, :, :], sel[:, :, :], aff[:, :, :], ALU.not_equal))
            eng.wait_ge(st.sem, v)
            v = st.mark(eng.tensor_tensor(aff[:, :, :], aff[:, :, :], den[:, 1, :].unsqueeze(2).broadcast_to([P, NT, E0]), ALU.mult))
            eng.wait_ge(st.sem, v)
            v = st.mark(eng.tensor_tensor(wgt[:, :, :], aff[:, :, :], sel[:, :, :], ALU.mult))
            eng.wait_ge(st.sem, v)
            split_tail(eng, st, E0)
            st.end()

        def split_tail(eng, st, ne):
            v = st.mark(eng.tensor_copy(wparts[:, :, 0:ne], wgt[:, :, 0:ne]))
            eng.wait_ge(st.sem, v)
            v = st.mark(eng.tensor_tensor(sel[:, :, 0:ne], wgt[:, :, 0:ne], wparts[:, :, 0:ne], ALU.subtract))
            eng.wait_ge(st.sem, v)
            v = st.mark(eng.tensor_copy(wparts[:, :, ne:2 * ne], sel[:, :, 0:ne]))
            eng.wait_ge(st.sem, v)
            v = st.mark(eng.tensor_tensor(wparts[:, :, 2 * ne:3 * ne], sel[:, :, 0:ne], wparts[:, :, ne:2 * ne], ALU.subtract))

        def router1_dve(eng, s, c):
            st = top1
            g = nth[s] * NB + c
            st.begin(g)
            a, r, w = aff[:, :, 0:E1], sel[:, :, 0:E1], wgt[:, :, 0:E1]
            bc = lambda v1: v1.broadcast_to([P, NT, E1])
            eng.wait_ge(aff_ready, nffn[s] * NB + c + 1)
            settle(eng)
            for t in range(NT):
                v = st.mark(eng.max(m8[:, t, :], aff[:, t, 0:E1]))
            eng.wait_ge(st.sem, v)
            settle(eng)
            for t in range(NT):
                v = st.mark(eng.max_index(i8[:, t, :], m8[:, t, :], aff[:, t, 0:E1]))
            eng.wait_ge(st.sem, v)
            v = st.mark(eng.tensor_copy(i8f[:, :, :], i8[:, :, :]))
            eng.wait_ge(st.sem, v)
            v = st.mark(eng.tensor_tensor(r, iota8[:, :, :], bc(i8f[:, :, 0:1]), ALU.is_equal))
            v = st.mark(eng.tensor_tensor(w, iota8[:, :, :], bc(i8f[:, :, 1:2]), ALU.is_equal))
            eng.wait_ge(st.sem, v)
            v = st.mark(eng.tensor_tensor(r, r, bc(m8[:, :, 0:1]), ALU.mult))
            v = st.mark(eng.tensor_tensor(w, w, bc(m8[:, :, 1:2]), ALU.mult))
            eng.wait_ge(st.sem, v)
            v = st.mark(eng.tensor_tensor(r, r, w, ALU.add))
            eng.wait_ge(st.sem, v)
            v = st.mark(eng.tensor_scalar(den[:, 0, :], m8[:, :, 0], 0.0, None, ALU.max))
            eng.wait_ge(st.sem, v)
            eng.tensor_tensor(r, r, bc(den[:, 0, :].unsqueeze(2)), ALU.subtract).then_inc(mx_ready, 1)
            eng.wait_ge(e_ready, g + 1)
            v = st.mark(eng.tensor_reduce(den[:, 0, :], w, AX_X, ALU.add))
            eng.wait_ge(st.sem, v)
            v = st.mark(eng.reciprocal(den[:, 1, :], den[:, 0, :]))
            eng.wait_ge(st.sem, v)
            v = st.mark(eng.tensor_tensor(w, w, bc(den[:, 1, :].unsqueeze(2)), ALU.mult))
            eng.wait_ge(st.sem, v)
            split_tail(eng, st, E1)
            assert st.k == 22, st.k

        def ffn0_dve(eng, g):
            for p in range(NPS):
                n = g * NPS + p
                eng.wait_ge(silu_ready, ONE + n + 1)
                eng.wait_ge(u_ready, n + 1)
                eng.wait_ge(hid_ready, ONE + g * NPS + (p - 1 if p >= 2 else 0))
                settle(eng)
                eng.scalar_tensor_tensor(prod[:, p % 2, :], bank[2 + p % 2][:, :], bias[:, BU + p:BU + p + 1],
                                         gate[:, p % 2, :], ALU.add, ALU.mult).then_inc(prod_ready, 1)
                eng.wait_ge(prod_ready, ONE + n + 1)
                eng.wait_ge(lo_ready, ONE + g * NPS + (p - 2 if p >= 3 else 0))
                if p < NP:
                    eng.wait_ge(wb_ready, g * NP + p + 1)
                    eng.tensor_tensor(hid[:, p % 3, :], bank[4][:, :], prod[:, p % 2, :], ALU.mult).then_inc(hid_ready, 1)
                else:
                    eng.tensor_copy(hid[:, p % 3, :], prod[:, p % 2, :]).then_inc(hid_ready, 1)

        def ffn1_dve(eng, g):
            def combine(e):
                n = g * E1 + e
                eng.wait_ge(h1_used, ONE + (n + 1) * HC)
                eng.wait_ge(rb_ready, ONE + n + 1)
                eng.wait_ge(acc_ready, ONE + g * E1 + e)
                ybank = bank[5 if e % 2 == 0 else 3]
                dst = yT[:, :] if e == 0 else zed[:, e % 2, :]
                if e == 0:
                    eng.wait_ge(y1_tok, ONE + g)
                settle(eng)
                eng.scalar_tensor_tensor(dst, ybank[:, :], bias[:, B2 + e:B2 + e + 1], rb[:, e % 2, :],
                                         ALU.add, ALU.mult).then_inc(ze_ready, 1)
                eng.wait_ge(ze_ready, ONE + n + 1)
                if e == 0:
                    eng.tensor_copy(den[:, 0, 0:1], yT[:, 0:1]).then_inc(acc_ready, 1)
                else:
                    eng.tensor_tensor(yT[:, :], yT[:, :], dst, ALU.add).then_inc(acc_ready, 1)

            for j in range(NJ + LAG + 1):
                if j < NJ and j % 2 == 1:
                    eng.wait_ge(hid1_ready, ONE + g * NJ + j + 1)
                    eng.wait_ge(h1_used, ONE + g * NJ + (j - NH + 1 if j >= NH else 0))
                    eng.tensor_copy(h_hi[:, j % NH, :], hid[:, j % 3, :]).then_inc(hi1v_ready, 1)
                    eng.wait_ge(hi1v_ready, g * (NJ // 2) + j // 2 + 1)
                    eng.tensor_tensor(h_lo[:, j % NH, :], hid[:, j % 3, :], h_hi[:, j % NH, :].bitcast(F32),
                                      ALU.subtract).then_inc(lo1v_ready, 1)
                d = j - LAG - 1
                if d >= 0 and d % HC == HC - 1:
                    combine(d // HC)

        def attn_dve(eng, kind, s, c, xs):
            causal = kind == "attn0"
            ga, gk = nattn[s] * NB + c, nth[s] * NB + c
            eng.wait_ge(qkv_ready, 3 * ga + 1)
            split_parts(eng, q_steps, ga, 0)
            if causal:
                m_steps.begin(gk)
                for half in range(2):
                    for hh in range(HALF):
                        h = half * HALF + hh
                        for qt in range(NT):
                            n = (gk * H + h) * NT + qt
                            eng.wait_ge(s_ready, n + 1)
                            eng.tensor_reduce(rmax[:, qt, h:h + 1], bank[qt][:, 0:(qt + 1) * P], AX_X, ALU.max).then_inc(s_used, 1)
                    eng.wait_ge(s_used, (gk * H + (half + 1) * HALF) * NT)
                    eng.wait_ge(mT_ps, ONE + 2 * gk + half)
                    hs = slice(half * HALF, (half + 1) * HALF)
                    v = m_steps.mark(eng.tensor_scalar(nmax[:, 0, :, :], rmax[:, :, hs], -1.0, None, ALU.mult))
                    eng.wait_ge(m_steps.sem, v)
                    v = m_steps.mark(eng.tensor_copy(mparts[:, :, 0, :], nmax[:, 0, :, :]))
                    eng.wait_ge(m_steps.sem, v)
                    v = m_steps.mark(eng.tensor_tensor(nmax[:, 1, :, :], nmax[:, 0, :, :], mparts[:, :, 0, :], ALU.subtract))
                    eng.wait_ge(m_steps.sem, v)
                    v = m_steps.mark(eng.tensor_copy(mparts[:, :, 1, :], nmax[:, 1, :, :]))
                    eng.wait_ge(m_steps.sem, v)
                    v = m_steps.mark(eng.tensor_tensor(mparts[:, :, 2, :], nmax[:, 1, :, :], mparts[:, :, 1, :], ALU.subtract))
                m_steps.end()
            attn_steps.begin(ga)
            for half in range(2):
                o = bank[4 + half][:, 0:NT * HALF * (HD + 1)].rearrange("p (n c) -> p n c", c=HD + 1)
                if half:
                    eng.wait_ge(attn_steps.sem, 4 * ga + 2)
                eng.wait_ge(pv_done, ONE + ga * H + (half + 1) * HALF)
                if causal:
                    v = attn_steps.mark(eng.reciprocal(rden[:, 1, :], o[:, :, HD]))
                else:
                    eng.tensor_scalar(rden[:, 0, :], o[:, :, HD], KERN_EPS, None, ALU.add).then_inc(tail_eps, 1)
                    eng.wait_ge(tail_eps, 2 * gk + half + 1)
                    v = attn_steps.mark(eng.reciprocal(rden[:, 1, :], rden[:, 0, :]))
                eng.wait_ge(attn_steps.sem, v)
                if half == 0:
                    eng.wait_ge(aT_ps, ONE + ga)
                attn_steps.mark(eng.tensor_tensor(
                    attn[:, :, half * HALF:(half + 1) * HALF, :],
                    o[:, :, 0:HD].rearrange("p (t h) d -> p t h d", h=HALF),
                    rden[:, 1, :].rearrange("p (t h) -> p t h", h=HALF).unsqueeze(3).broadcast_to([P, NT, HALF, HD]), ALU.mult))
            attn_steps.end()
            eng.wait_ge(aT_hi_ready, ga + 1)
            eng.tensor_tensor(aT_lo[:, :], aT_mix[:, :] if causal else bank6[:, :], aT_hi[:, :].bitcast(F32), ALU.subtract).then_inc(aT_lo_ready, 1)
            eng.wait_ge(o_ps, ga + 1)
            ob = bank7[:, :].rearrange("p (t d) -> p t d", d=D)
            rbc = lambda i: row[:, i, :].unsqueeze(1).broadcast_to([P, NT, D])
            if causal:
                eng.tensor_tensor(xs, ob, xs, ALU.add).then_inc(x_mid, 1)
                eng.wait_ge(x_mid, gk + 1)
                eng.tensor_tensor(xs, xs, rbc(0), ALU.add).then_inc(x_done, 1)
            else:
                st = tail
                st.begin(gk)
                v = st.mark(eng.tensor_tensor(xn[:, :, :], ob, xn[:, :, :], ALU.add))
                eng.wait_ge(st.sem, v)
                v = st.mark(eng.tensor_tensor(xn[:, :, :], xn[:, :, :], rbc(1), ALU.add))
                eng.wait_ge(st.sem, v)
                for t in range(NT):
                    v = st.mark(eng.bn_stats(stats[:, t, :], xn[:, t, :]))
                eng.wait_ge(st.sem, v)
                settle(eng)
                for t in range(NT):
                    v = st.mark(eng.bn_aggr(mv[:, t, :], stats[:, t, :]))
                eng.wait_ge(st.sem, v)
                eng.tensor_scalar(ve[:, :], mv[:, :, 1], LN_EPS, None, ALU.add).then_inc(tail_var, 1)
                eng.wait_ge(tail_rstd, gk + 1)
                for t in range(NT):
                    v = st.mark(eng.tensor_scalar(xn[:, t, :], xn[:, t, :], mv[:, t, 0:1], rstd[:, t:t + 1],
                                                  ALU.subtract, ALU.mult))
                eng.wait_ge(st.sem, v)
                v = st.mark(eng.tensor_tensor(xn[:, :, :], xn[:, :, :], rbc(2), ALU.mult))
                eng.wait_ge(st.sem, v)
                v = st.mark(eng.tensor_tensor(xn[:, :, :], xn[:, :, :], rbc(3), ALU.add))
                eng.wait_ge(st.sem, v)
                v = st.mark(eng.tensor_tensor(xs, xs, xn[:, :, :], ALU.add))
                eng.wait_ge(st.sem, v)
                eng.tensor_copy(ve[:, 0:1], rstd[:, 0:1]).then_inc(x_done, 1)
                assert st.k == 17, st.k

        def router_pe(eng, s, kind, c):
            gr = nffn[s] * NB + c
            w_hi_, w_lo_, blk, ne = (w0_hi, w0_lo, WR0, E0) if kind == "ffn0" else (w1_hi, w1_lo, WR1, E1)
            products(eng, bank7[:, :], w_hi_[:, blk, :], w_lo_[:, blk, :], xnT_hi[:, :], xnT_lo[:, :]).then_inc(lgT_ps, 1)
            eng.wait_ge(lgT_ready, gr + 1)
            settle(eng)
            for t in range(NT):
                ins = eng.transpose(bank7[:, t * ne:(t + 1) * ne], lgT[0:ne, t * P:(t + 1) * P], ident[0:ne, 0:ne])
            ins.then_inc(lg_ps, 1)

        def router_pe2(eng, kind, gr):
            ne, st, per = (E0, top0, 18) if kind == "ffn0" else (E1, top1, 22)
            eng.wait_ge(st.sem, gr * per + per)
            for t in range(NT):
                ins = eng.transpose(bank7h[0:NPART * ne, t * P:(t + 1) * P], wparts[:, t, 0:NPART * ne], identb)
            ins.then_inc(wT_ps, 1)

        def ffn0_pe(eng, g, gr):
            def down(p):
                eng.wait_ge(hi_ready, g * NPS + p + 1)
                eng.wait_ge(lo_ready, ONE + g * NPS + p + 1)
                products(eng, bank[5][:, :], w0_hi[:, DOWN0 + p, :], w0_lo[:, DOWN0 + p, :],
                         h_hi[:, p % NH, :], h_lo[:, p % NH, :], start=(p == 0), stop=False).then_inc(h_used, 1)

            for p in range(NPS + LAG):
                if p < NPS:
                    eng.wait_ge(silu_ready, ONE + g * NPS + (p - 1 if p >= 2 else 0))
                    products(eng, bank[p % 2][:, :], w0_hi[:, GATE0 + p, :], w0_lo[:, GATE0 + p, :],
                             xnT_hi[:, :], xnT_lo[:, :]).then_inc(g_ready, 1)
                    eng.wait_ge(prod_ready, ONE + g * NPS + (p - 1 if p >= 2 else 0))
                    products(eng, bank[2 + p % 2][:, :], w0_hi[:, UP0 + p, :], w0_lo[:, UP0 + p, :],
                             xnT_hi[:, :], xnT_lo[:, :]).then_inc(u_ready, 1)
                if p == 1:
                    router_pe2(eng, "ffn0", g)
                    eng.wait_ge(wT_ready, gr + 1)
                    weight(eng, g, 0)
                    weight(eng, g, 1)
                if 1 < p < NP:
                    weight(eng, g, p)
                if p >= LAG:
                    down(p - LAG)
            for j in range(NPART):
                ins = eng.matmul(bank[5][:, :], bd_parts[:, j, :], wT[:, :], start=False, stop=(j == NPART - 1))
            ins.then_inc(y_ps, 1)
            eng.wait_ge(yT_ready, g + 1)
            for t in range(NT):
                ins = eng.transpose(bank6[:, t * P:(t + 1) * P], yT[:, t * P:(t + 1) * P], ident[:, :])
            ins.then_inc(y_tok, 1)

        def weight(eng, g, p):
            eng.wait_ge(hid_ready, ONE + g * NPS + p)
            eng.matmul(bank[4][:, :], cbf[0:NPART * E0, C_SEL0 + p * P:C_SEL0 + (p + 1) * P], wT[:, :],
                       start=True, stop=True).then_inc(wb_ready, 1)

        def ffn1_pe(eng, g, gr):
            def down(j):
                e = j // HC
                if j % 2 == 0:
                    eng.wait_ge(lo1p_ready, ONE + g * (NJ // 2) + j // 2 + 1)
                else:
                    eng.wait_ge(lo1v_ready, ONE + g * (NJ // 2) + j // 2 + 1)
                if j % HC == 0:
                    eng.wait_ge(ze_ready, ONE + g * E1 + (e - 1 if e >= 2 else 0))
                ybank = bank[5 if e % 2 == 0 else 3]
                ins = products(eng, ybank[:, :], w1_hi[:, DOWN1 + j, :], w1_lo[:, DOWN1 + j, :],
                               h_hi[:, j % NH, :], h_lo[:, j % NH, :], start=(j % HC == 0), stop=(j % HC == HC - 1))
                ins.then_inc(h1_used, 1)

            def spread(e):
                eng.wait_ge(rb_ready, ONE + g * E1 + e)
                eng.matmul(bank[4][:, :], cbf[0:NPART * E1, C_SEL1 + e * P:C_SEL1 + (e + 1) * P],
                           wT[0:NPART * E1, :], start=True, stop=True).then_inc(rb_ps, 1)

            for j in range(NJ + LAG):
                if j == 0:
                    router_pe2(eng, "ffn1", g)
                    eng.wait_ge(wT_ready, gr + 1)
                if j < NJ and j % HC == 0:
                    spread(j // HC)
                if j < NJ:
                    eng.wait_ge(hid1_ready, ONE + g * NJ + (j - 2 if j >= 3 else 0))
                    products(eng, bank[j % 3][:, :], w1_hi[:, UP1 + j, :], w1_lo[:, UP1 + j, :],
                             xnT_hi[:, :], xnT_lo[:, :]).then_inc(u1_ready, 1)
                if j >= LAG:
                    down(j - LAG)
            eng.wait_ge(acc_ready, ONE + g * E1 + E1)
            for t in range(NT):
                ins = eng.transpose(bank6[:, t * P:(t + 1) * P], yT[:, t * P:(t + 1) * P], ident[:, :])
            ins.then_inc(y1_tok, 1)

        def attn_pe(eng, kind, ga, gk, G):
            causal = kind == "attn0"
            layer = 0 if causal else 1
            for i in range(3):
                products(eng, bank[i][:, :], wa_hi[:, layer, i, :], wa_lo[:, layer, i, :],
                         xnT_hi[:, :], xnT_lo[:, :]).then_inc(qkv_ps, 1)
            eng.wait_ge(qkv_ready, 3 * ga + 3)
            for t in range(NT):
                ins = eng.transpose(bank7[:, t * P:(t + 1) * P], qkv[:, 2, t * P:(t + 1) * P], ident[:, :])
            ins.then_inc(vT_ps, 1)

            def head(st, h, rows):
                p0 = (h % 2) * STACK
                return st[p0:p0 + rows, h // 2, :]

            def maxima(half):
                eng.wait_ge(m_steps.sem, gk * 10 + 5 * half + 5)
                if half:
                    eng.wait_ge(mT_ready, 2 * gk + 1)
                else:
                    eng.wait_ge(v9_ready, 4 * ga + 4)
                for t in range(NT):
                    ins = eng.transpose(bank7h[0:NPART * HALF, t * P:(t + 1) * P],
                                        mparts[:, t, :, :].rearrange("p a b -> p (a b)"), identb)
                ins.then_inc(mT_ps, 1)

            if causal:
                for half in range(2):
                    eng.wait_ge(st_in[half], 16 * 24 * (ga + 1))
                    for h in range(half * HALF, (half + 1) * HALF):
                        qs, ks = head(q_st, h, QK_ROWS), head(k_st, h, QK_ROWS)
                        for qt in range(NT):
                            n = (gk * H + h) * NT + qt
                            if h:
                                eng.wait_ge(s_used, n - NT + 1)
                            eng.matmul(bank[qt][:, 0:(qt + 1) * P], qs[:, qt * P:(qt + 1) * P], ks[:, 0:(qt + 1) * P],
                                       start=True, stop=True)
                            eng.matmul(bank[qt][:, qt * P:(qt + 1) * P], identb, neg, start=False, stop=True,
                                       skip_group_check=True).then_inc(s_ready, 1)
                    if half == 1:
                        maxima(0)
                maxima(1)
                rows_ = QK_ROWS + NPART
            else:
                rows_ = QK_ROWS

            def pv(h):
                half, hh = h // HALF, h % HALF
                for qt in range(NT):
                    kbs = range(qt + 1) if causal else range(NT)
                    o = bank[4 + half][:, (qt * HALF + hh) * (HD + 1):(qt * HALF + hh + 1) * (HD + 1)]
                    for kb in kbs:
                        if qt == 0:
                            eng.wait_ge(p_ready, (ga * H + h) * NT + (NT if kb == 0 else NT))
                        ins = eng.matmul(o, probs[:, h % 2, kb, qt * P:(qt + 1) * P], v9[:, kb, h, :],
                                         start=(kb == 0), stop=(kb == kbs[-1]))
                ins.then_inc(pv_done, 1)

            for h in range(H + 1):
                if h < H:
                    half = h // HALF
                    if h % HALF == 0:
                        if causal:
                            eng.wait_ge(m_in[half], 96 * (gk + 1))
                        else:
                            eng.wait_ge(st_in[half], 16 * 24 * (ga + 1))
                    qs, ks = head(q_st, h, rows_), head(k_st, h, rows_)
                    for kb in range(NT):
                        n = (ga * H + h) * NT + kb
                        q0 = kb * P if causal else 0
                        if h:
                            eng.wait_ge(p_ready, n - NT + 1)
                        elif causal:
                            eng.wait_ge(s_used, (gk + 1) * H * NT)
                        ins = eng.matmul(bank[kb][:, 0:S - q0], ks[:, kb * P:(kb + 1) * P], qs[:, q0:S],
                                         start=True, stop=True)
                        if causal:
                            ins = eng.matmul(bank[kb][:, 0:P], identb, negT, start=False, stop=True, skip_group_check=True)
                        ins.then_inc(st_ready, 1)
                if h >= 1:
                    pv(h - 1)
            eng.wait_ge(attn_steps.sem, 4 * ga + 4)
            for t in range(NT):
                ins = eng.transpose(bank6[:, t * P:(t + 1) * P], attn[:, t, :, :].rearrange("p h d -> p (h d)"), ident[:, :])
            ins.then_inc(aT_ps, 1)
            eng.wait_ge(aT_lo_ready, ga + 1)
            for t in range(NT):
                ts = slice(t * P, (t + 1) * P)
                ins = products(eng, bank7[:, ts], aT_hi[:, ts], aT_lo[:, ts], wa_hi[:, layer, WO, :], wa_lo[:, layer, WO, :])
            ins.then_inc(o_ps, 1)

        block = ctx.enter_context(nc.Block())

        @block.sync
        def _(eng):
            eng.dma_start(x[:, :, :], x_in).then_inc(x_in_sem, 16)
            eng.dma_start(stage_c[:, :], consts).then_inc(small_in, 16)
            eng.dma_start(bias[:, :], biases).then_inc(small_in, 16)
            eng.dma_start(row[:, :, :], rows).then_inc(small_in, 16)
            eng.dma_start(stage_bd[:, 0, :], bd3).then_inc(small_in, 16)
            for n, (src, _, _, cols) in enumerate(loads):
                if n >= 4:
                    eng.wait_ge(w_lo_done, n - 3)
                eng.dma_start(stage_w[:, n % 4, 0:cols], src).then_inc(w_in[n % 4], 16)

            for s, kind in enumerate(STAGES):
                if kind[:4] != "attn":
                    continue
                a = nattn[s]
                with eng.Fori(0, NB) as c:
                    ga = a * NB + c
                    eng.wait_ge(q_steps.sem, ga * 5 + 5)
                    eng.wait_ge(k_steps.sem, ga * 5 + 5)
                    for i in range(2):
                        eng.dma_start(scratch[bass.ds(ga, 1), i, :, :, :].rearrange("g n p s -> (g p) n s"),
                                      parts[:, i, :, :]).then_inc(scr_w, 16)
                    eng.wait_ge(scr_w, ga * 32 + 32)
                    for half in range(2):
                        for i, (st, part_of) in enumerate(((q_st, Q_PART), (k_st, K_PART))):
                            for par in range(2):
                                for r in range(PAIRS):
                                    src = scratch[bass.ds(ga, 1), i, part_of[r], :, :].rearrange(
                                        "g (hf j two d) s -> g hf two d j s", hf=2, two=2, d=HD)[0, half, par]
                                    p0 = par * STACK + r * HD
                                    eng.dma_start(st[p0:p0 + HD, half * 4:half * 4 + 4, :], src).then_inc(st_in[half], 16)
                    if kind == "attn0":
                        for half in range(2):
                            eng.wait_ge(mT_ready, 2 * ga + half + 1)
                            for i in range(NPART):
                                for par in range(2):
                                    p0 = par * STACK + MAX_ROW + i
                                    eng.dma_start(q_st[p0:p0 + 1, half * 4:half * 4 + 4, :],
                                                  mT[i * HALF + par:i * HALF + HALF:2, half, :]).then_inc(m_in[half], 16)
                        eng.wait_ge(perm_ready, ga + 1)
                        eng.dma_start(mixed[bass.ds(ga, 1), :, :].rearrange("g p s -> (g p) s"), aT_perm[:, :]).then_inc(perm_out, 16)
                        eng.wait_ge(perm_out, 16 * (ga + 1))
                        src = mixed[bass.ds(ga, 1), :, :].rearrange("g (h d) (q r) -> g q d h r", d=HD, q=GQ)[0]
                        for q in range(GQ):
                            eng.dma_start(aT_mix[q * HD:(q + 1) * HD, :].rearrange("d (h r) -> d h r", h=H), src[q]).then_inc(mix_in, 16)
            s = len(STAGES) - 1
            with eng.Fori(0, NB) as c:
                eng.wait_ge(x_done, ONE + s * NB + c + 1)
                eng.dma_start(out[:, bass.ds(c * NT, NT), :], x[:, bass.ds(c * NT, NT), :]).then_inc(out_sem, 16)
            eng.wait_ge(out_sem, 16 * NB)

        @block.gpsimd
        def _(eng):
            for counts in (lo_ready, lo1p_ready):
                eng.sem_inc(counts, ONE)
            eng.memset(mhalf[:, :], -0.5).then_inc(pool_init, 1)

            def rstd_of(ready, value):
                eng.wait_ge(ready, value)
                return eng.tensor_tensor(rstd[:, :], ve[:, :], mhalf[:, :], ALU.pow)

            eng.wait_ge(pool_init, 1)
            for s, kind in enumerate(STAGES):
                with eng.Fori(0, NB) as c:
                    G = s * NB + c
                    rstd_of(ln_steps.sem, G * 13 + 9).then_inc(rstd_ready, 1)
                    if kind == "ffn0":
                        g = nth[s] * NB + c
                        for p in range(NPS):
                            n = g * NPS + p
                            eng.wait_ge(hi_ready, n + 1)
                            eng.tensor_tensor(h_lo[:, p % NH, :], hid[:, p % 3, :], h_hi[:, p % NH, :].bitcast(F32),
                                              ALU.subtract).then_inc(lo_ready, 1)
                    if kind == "ffn1":
                        g = nth[s] * NB + c
                        for j in range(0, NJ, 2):
                            eng.wait_ge(hi1a_ready, g * (NJ // 2) + j // 2 + 1)
                            eng.tensor_tensor(h_lo[:, j % NH, :], hid[:, j % 3, :], h_hi[:, j % NH, :].bitcast(F32),
                                              ALU.subtract).then_inc(lo1p_ready, 1)
                    if kind[:4] == "attn":
                        ga = nattn[s] * NB + c
                        eng.wait_ge(qkv_ready, 3 * ga + 2)
                        split_parts(eng, k_steps, ga, 1)
                        if kind == "attn1":
                            eng.wait_ge(tail_var, c + 1)
                            eng.tensor_tensor(rstd[:, :], ve[:, :], mhalf[:, :], ALU.pow).then_inc(tail_rstd, 1)

        @block.scalar
        def _(eng):
            for counts in (silu_ready, rb_ready, hid1_ready):
                eng.sem_inc(counts, ONE)
            eng.wait_ge(small_in, 64)
            eng.activation(ident[:, :], stage_c[:, C_ID:C_ID + P], ACT.Copy).then_inc(const_ready, 1)
            eng.activation(cbf[:, :], stage_c[:, :], ACT.Copy).then_inc(const_ready, 1)
            for n, (_, hi, _, cols) in enumerate(loads):
                eng.wait_ge(w_in[n % 4], 16 * (n // 4 + 1))
                eng.activation(hi, stage_w[:, n % 4, 0:cols], ACT.Copy).then_inc(w_hi_done, 1)

            for s, kind in enumerate(STAGES):
                with eng.Fori(0, NB) as c:
                    G = s * NB + c
                    eng.wait_ge(xnT_ps, ONE + G + 1)
                    eng.activation(xnT_hi[:, :], bank6[:, :], ACT.Copy).then_inc(xnT_hi_ready, 1)
                    if kind[:3] == "ffn":
                        router_act(eng, s, kind, c)
                    if kind == "ffn0":
                        ffn0_act(eng, nth[s] * NB + c)
                    if kind == "ffn1":
                        ffn1_act(eng, nth[s] * NB + c)
                    if kind[:4] == "attn":
                        attn_act(eng, kind, nattn[s] * NB + c, nth[s] * NB + c)

        @block.vector
        def _(eng):
            for counts in (prod_ready, hid_ready, ze_ready, acc_ready, x_done, lo1v_ready):
                eng.sem_inc(counts, ONE)
            eng.wait_ge(small_in, 64)
            ini = Steps(sem("dve_init"), 10)
            ini.begin(0)
            for j in range(NPART):
                src = stage_bd[:, 0, :] if j == 0 else stage_bd[:, 1, :]
                v = ini.mark(eng.tensor_copy(bd_parts[:, j, :], src))
                eng.wait_ge(ini.sem, v)
                if j < 2:
                    v = ini.mark(eng.tensor_tensor(stage_bd[:, 1, :], src, bd_parts[:, j, :], ALU.subtract))
                    eng.wait_ge(ini.sem, v)
            for _ in range(5):
                ini.mark(eng.memset(ve[:, :], 1.0))
                eng.wait_ge(ini.sem, ini.base + ini.k)
            ini.end()
            for n, (_, hi, lo, cols) in enumerate(loads):
                eng.wait_ge(w_hi_done, n + 1)
                eng.tensor_tensor(lo, stage_w[:, n % 4, 0:cols], hi.bitcast(F32), ALU.subtract).then_inc(w_lo_done, 1)
            eng.wait_ge(x_in_sem, 16)
            eng.wait_ge(w_lo_done, len(loads))

            for s, kind in enumerate(STAGES):
                if kind[:4] == "attn":
                    if kind == "attn0":
                        eng.memset(k_st[:, :, :], 1.0).then_inc(const_ready, 1)
                    else:
                        eng.memset(k_st[:, :, :], 1.0).then_inc(const_ready, 1)
                    eng.memset(v9[:, :, :, :], 1.0).then_inc(const_ready, 1)
                if kind == "ffn1":
                    for e in range(E1):
                        eng.memset(iota8[:, :, e], float(e)).then_inc(const_ready, 1)
                with eng.Fori(0, NB) as c:
                    G = s * NB + c
                    xs = x[:, bass.ds(c * NT, NT), :]
                    if s:
                        eng.wait_ge(x_done, ONE + G - NB + 1)
                    layernorm(eng, ln_steps, G, xs)
                    eng.wait_ge(xnT_hi_ready, G + 1)
                    eng.tensor_tensor(xnT_lo[:, :], bank6[:, :], xnT_hi[:, :].bitcast(F32), ALU.subtract).then_inc(xnT_lo_ready, 1)
                    if kind == "ffn0":
                        router0_dve(eng, s, c)
                        ffn0_dve(eng, nth[s] * NB + c)
                        eng.wait_ge(y_tok, nth[s] * NB + c + 1)
                    if kind == "ffn1":
                        router1_dve(eng, s, c)
                        ffn1_dve(eng, nth[s] * NB + c)
                        eng.wait_ge(y1_tok, ONE + nth[s] * NB + c + 1)
                    if kind[:3] == "ffn":
                        settle(eng)
                        eng.scalar_tensor_tensor(xs, bank6[:, :].rearrange("p (t d) -> p t d", d=D), 0.5, xs,
                                                 ALU.mult, ALU.add).then_inc(x_done, 1)
                    else:
                        attn_dve(eng, kind, s, c, xs)

        @block.tensor
        def _(eng):
            for counts in (h_used, h1_used, y1_tok, mT_ps, aT_ps, pv_done, xnT_ps):
                eng.sem_inc(counts, ONE)
            eng.wait_ge(const_ready, 2)
            eng.wait_ge(w_lo_done, len(loads))
            for s, kind in enumerate(STAGES):
                with eng.Fori(0, NB) as c:
                    G = s * NB + c
                    eng.wait_ge(ln_steps.sem, G * 13 + 13)
                    eng.wait_ge(x_done, ONE + G)
                    for t in range(NT):
                        ins = eng.transpose(bank6[:, t * P:(t + 1) * P], xn[:, t, :], ident[:, :])
                    ins.then_inc(xnT_ps, 1)
                    eng.wait_ge(xnT_lo_ready, G + 1)
                    if kind[:3] == "ffn":
                        router_pe(eng, s, kind, c)
                    if kind == "ffn0":
                        ffn0_pe(eng, nth[s] * NB + c, nffn[s] * NB + c)
                    if kind == "ffn1":
                        ffn1_pe(eng, nth[s] * NB + c, nffn[s] * NB + c)
                    if kind[:4] == "attn":
                        attn_pe(eng, kind, nattn[s] * NB + c, nth[s] * NB + c, G)


def _layout(i):
    pad = lambda a, n: np.concatenate([a, np.zeros(a.shape[:-1] + (n - a.shape[-1],), a.dtype)], -1)
    f = {k: np.asarray(v) for k, v in i.items()}
    cols = lambda w: np.moveaxis(w, 0, 1).reshape(D, -1)
    w0 = np.concatenate([
        cols(f["L0_ffn_Wg"]), pad(f["L0_ffn_Wg_s"], P), cols(f["L0_ffn_Wu"]), pad(f["L0_ffn_Wu_s"], P),
        f["L0_ffn_Wd"].reshape(NP, P, D).transpose(1, 0, 2).reshape(P, -1), pad(f["L0_ffn_Wd_s"].T, P).T,
        pad(f["L0_ffn_Wr"], P)], 1)
    w1 = np.concatenate([
        cols(f["L1_ffn_W1"]), f["L1_ffn_W2"].reshape(NJ, P, D).transpose(1, 0, 2).reshape(P, -1),
        pad(f["L1_ffn_Wr"], P)], 1)
    qkv1 = f["L1_attn_w_qkv"].reshape(D, H, 3, HD).transpose(0, 2, 1, 3).reshape(D, 3 * D)
    wa = np.concatenate([f["L0_attn_Wq"], f["L0_attn_Wk"], f["L0_attn_Wv"], f["L0_attn_Wo"], qkv1, f["L1_attn_w_out"]], 1)
    col = lambda v: pad(v.reshape(1, -1), -(-v.size // P) * P).reshape(-1, P).T
    biases = np.concatenate([
        col(f["L0_ffn_bg"]), col(f["L0_ffn_bg_s"]), col(f["L0_ffn_bu"]), col(f["L0_ffn_bu_s"]), col(f["L0_ffn_bd_s"]),
        col(f["L0_ffn_br"]), col(f["L1_ffn_b1"]), col(f["L1_ffn_b2"]), col(f["L1_ffn_br"])], 1)
    bd3 = np.tile(f["L0_ffn_bd"], (NPART, 1))
    rows = np.tile(np.stack([f["L0_attn_bo"], f["L1_attn_b_out"], f["L1_attn_gamma"], f["L1_attn_beta"]])[None], (P, 1, 1))
    r = np.arange(P)
    consts = np.zeros((P, NCONST), np.float32)
    consts[r, C_ID + r] = 1
    consts[:, C_NEG:C_NEG + P] = np.where(r[None, :] > r[:, None], -1e30, 0)
    consts[:, C_NEGT:C_NEGT + P] = consts[:, C_NEG:C_NEG + P].T
    for part in range(NPART):
        for e in range(E0):
            at = C_SEL0 + e * I0
            consts[part * E0 + e, at:at + I0] = 1
        for e in range(E1):
            consts[part * E1 + e, C_SEL1 + e * P:C_SEL1 + (e + 1) * P] = 1
    x = f["L0_attn_x"].reshape(NB * NT, P, D).transpose(1, 0, 2)
    return dict(x=x, w0=w0, w1=w1, wa=wa, biases=biases, bd3=bd3, rows=rows, consts=consts)


def kernel(**inputs):
    import concourse.bacc as _bacc
    from concourse.bass_utils import run_bass_kernel_spmd as _run

    nc = _bacc.Bacc("TRN2", target_bir_lowering=False, num_devices=1)
    arrays, args = {}, []
    for name, a in _layout(inputs).items():
        a = np.ascontiguousarray(a)
        arrays[f"in_{name}_dram"] = a
        args.append(nc.dram_tensor(f"in_{name}_dram", a.shape, mybir.dt.from_np(a.dtype), kind="ExternalInput").ap())
    out = nc.dram_tensor("out_0_dram", (P, NB * NT, D), F32, kind="ExternalOutput").ap()
    scratch = nc.dram_tensor("parts_dram", (2 * NB, 2, NPART, P, S), BF16, kind="Internal").ap()
    mixed = nc.dram_tensor("mixed_dram", (NB, P, S), F32, kind="Internal").ap()
    build(nc, *args, out, scratch, mixed)
    r = _run(nc, [arrays], core_ids=[0])
    o = r.results[0]["out_0_dram"]
    return o.transpose(1, 0, 2).reshape(NB, S, D)
```

```python
from contextlib import ExitStack

import numpy as np
import concourse.bass as bass
from concourse import mybir

ALU = mybir.AluOpType
ACT = mybir.ActivationFunctionType
AX_X = mybir.AxisListType.X
F32 = mybir.dt.float32
F32R = mybir.dt.float32r
BF16 = mybir.dt.bfloat16
U32 = mybir.dt.uint32

P = 128
D = 128
NB, S = 8, 512
NT = S // P
H, HD = 16, 8
E0, K0, I0 = 32, 8, 64
NP = E0 // 2
NPS = NP + 1
E1, I1 = 8, 512
HC = I1 // P
NJ = E1 * HC
LN_EPS = 1e-5
KERN_EPS = 1e-6
SCALE = float(HD) ** -0.5
NPART = 3
PAIRS = 6
Q_PART = (0, 0, 1, 1, 0, 2)
K_PART = (0, 1, 0, 1, 2, 0)
QK_ROWS = PAIRS * HD
MAX_ROW = QK_ROWS
STACK = 64
HALF = H // 2
GQ = D // HD

GATE0, UP0, DOWN0, WR0 = 0, NPS, 2 * NPS, 3 * NPS
NW0 = 3 * NPS + 1
UP1, DOWN1, WR1 = 0, NJ, 2 * NJ
NW1 = 2 * NJ + 1
WQ, WK, WV, WO = range(4)
BG, BU, BDS, BR0, B1, B2, BR1 = 0, NPS, 2 * NPS, 2 * NPS + 1, 2 * NPS + 2, 2 * NPS + 2 + NJ, 2 * NPS + 2 + NJ + E1
NBIAS = BR1 + 1
C_ID, C_NEG, C_NEGT, C_SEL0, C_SEL1 = 0, P, 2 * P, 3 * P, 3 * P + NP * P
NCONST = C_SEL1 + E1 * P
C_OSEL = NCONST
NCONST_ALL = C_OSEL + 4 * (HD + 1)

STAGES = ("ffn0", "attn0", "ffn0", "ffn1", "attn1", "ffn1")
FIRST1 = 3
NORM_AT = 12
W1_AT = 8
LAG = 3
NH = 4
ONE = 1
LOAD1 = NW1 * P // NB
VC = HD + 1
QUAD = 4
RING = 6
LOAD = 1024


class Steps:

    def __init__(self, sem, per):
        self.sem, self.per = sem, per

    def begin(self, visit):
        self.base, self.k = visit * self.per, 0

    def mark(self, ins):
        ins.then_inc(self.sem, 1)
        self.k += 1
        return self.base + self.k

    def end(self):
        assert self.k == self.per, (self.k, self.per)


class AttnMemory:

    def __init__(self, which, sb):
        self.q_st = sb(which + "_q_st", [P, H // 2, S], BF16)
        self.k_st = sb(which + "_k_st", [P, H // 2, S], BF16)
        self.qkv = sb(which + "_qkv", [P, 3, S], F32)
        self.res = sb(which + "_res", [P, 2, S], F32)
        self.parts = sb(which + "_parts", [P, 2, NPART, S], BF16)
        self.v_parts = sb(which + "_v_parts", [P, NT, H, 2, VC], F32R)
        self.rmax = sb(which + "_rmax", [P, NT, H], F32)
        self.nmax = sb(which + "_nmax", [P, 2, NT, HALF], F32)
        self.mparts = sb(which + "_mparts", [P, NT, NPART, HALF], BF16)
        self.mT = sb(which + "_mT", [NPART * HALF, 2, S], BF16)
        self.rden = sb(which + "_rden", [P, 2, NT * HALF], F32)
        self.attn = sb(which + "_attn", [P, NT, H, HD], F32)
        self.aT_hi, self.aT_lo = sb(which + "_aT_hi", [P, S], F32R), sb(which + "_aT_lo", [P, S], F32R)
        self.aT_perm, self.aT_mix = sb(which + "_aT_perm", [P, S], F32), sb(which + "_aT_mix", [P, S], F32)


def build(nc, x_in, w0, w1, wa, biases, bd3, rows, consts, out, scratch, mixed):
    nc.disable_value_cache = True
    ctx = ExitStack()
    with ctx:
        def sb(name, shape, dt, stack=ctx):
            return stack.enter_context(nc.sbuf_tensor(name, shape, dt))

        def sem(name):
            return ctx.enter_context(nc.semaphore(name))

        x = sb("x", [P, NB * NT, D], F32)
        wa_hi, wa_lo = sb("wa_hi", [P, 2, 4, P], F32R), sb("wa_lo", [P, 2, 4, P], F32R)
        bias = sb("bias", [P, NBIAS], F32)
        row = sb("row", [P, 4, D], F32)
        ident = sb("ident", [P, P], F32)
        osel = sb("osel", [P, QUAD * VC], F32)
        cbf = sb("cbf", [P, NCONST], BF16)
        bd_parts = sb("bd_parts", [96, NPART, D], BF16)
        xn = sb("xn", [P, NT, D], F32)
        xnT_hi, xnT_lo = sb("xnT_hi", [P, S], F32R), sb("xnT_lo", [P, S], F32R)
        stats, mv = sb("stats", [P, NT, 6], F32), sb("mv", [P, NT, 2], F32)
        ve, rstd = sb("ve", [P, NT], F32), sb("rstd", [P, NT], F32)
        mhalf = sb("mhalf", [P, NT], F32)
        wT = sb("wT", [96, S], BF16)
        lgT = sb("lgT", [E0, S], F32)
        aff, sel, wgt = (sb(n, [P, NT, E0], F32) for n in ("aff", "sel", "wgt"))
        m8 = sb("m8", [P, NT, 8], F32)
        i8 = sb("i8", [P, NT, 8], U32)
        i8f = sb("i8f", [P, NT, 8], F32)
        iota8 = sb("iota8", [P, NT, 8], F32)
        den = sb("den", [P, 2, NT], F32)
        wparts = sb("wparts", [P, NT, NPART * E0], BF16)

        with ExitStack() as part:
            mem1 = AttnMemory("attn1", lambda name, shape, dt: sb(name, shape, dt, part))
        w0_hi, w0_lo = sb("w0_hi", [P, NW0, P], F32R), sb("w0_lo", [P, NW0, P], F32R)
        with ExitStack() as part:
            mem0 = AttnMemory("attn0", lambda name, shape, dt: sb(name, shape, dt, part))
        w1_hi, w1_lo = sb("w1_hi", [P, NW1, P], F32R), sb("w1_lo", [P, NW1, P], F32R)

        with ExitStack() as part:
            stage_w = sb("stage_w", [P, 4, LOAD], F32, part)
            stage_c = sb("stage_c", [P, NCONST_ALL], F32, part)
            stage_bd = sb("stage_bd", [96, 2, D], F32, part)
        with ExitStack() as part:
            gate = sb("gate", [P, 2, S], F32, part)
            prod = sb("prod", [P, 2, S], F32, part)
            hid = sb("hid", [P, 3, S], F32, part)
            h_hi, h_lo = sb("h_hi", [P, NH, S], F32R, part), sb("h_lo", [P, NH, S], F32R, part)
            yT = sb("yT", [P, S], F32, part)
            stage_w1 = sb("stage_w1", [P, LOAD1], F32, part)
        rb, zed = gate, prod
        with ExitStack() as part:
            v_pad = sb("v_pad", [P, QUAD, NT, P], F32R, part)
            p_hi, p_lo = sb("p_hi", [P, RING, S], F32R, part), sb("p_lo", [P, RING, S], F32R, part)
            p_full = sb("p_full", [P, NT, S], F32, part)
            o_sb = sb("o_sb", [P, 2, S], F32, part)

        bank = [ctx.enter_context(nc.psum_tensor(f"bank{i}", [P, S], F32)) for i in range(8)]
        bank6, bank7 = bank[6], bank[7]
        bank7h = bank7[:, :].bitcast(BF16)
        identb = cbf[:, C_ID:C_ID + P]
        neg, negT = cbf[:, C_NEG:C_NEG + P], cbf[:, C_NEGT:C_NEGT + P]

        x_in_sem, small_in = sem("x_in_sem"), sem("small_in")
        w_in = [sem(f"w_in{i}") for i in range(4)]
        w_hi_done, w_lo_done = sem("w_hi_done"), sem("w_lo_done")
        w1_in, w1_hi_done, w1_lo_done = sem("w1_in"), sem("w1_hi_done"), sem("w1_lo_done")
        const_ready, pool_init = sem("const_ready"), sem("pool_init")
        ln_steps = Steps(sem("ln_steps"), 13)
        rstd_ready, xn_ready, xnT_ps, xnT_hi_ready, xnT_lo_ready = map(sem, (
            "rstd_ready", "xn_ready", "xnT_ps", "xnT_hi_ready", "xnT_lo_ready"))
        lgT_ps, lgT_ready, lg_ps, aff_ready, wparts_ready, wT_ps, wT_ready = map(sem, (
            "lgT_ps", "lgT_ready", "lg_ps", "aff_ready", "wparts_ready", "wT_ps", "wT_ready"))
        top0 = Steps(sem("top0_steps"), 18)
        top1 = Steps(sem("top1_steps"), 22)
        mx_ready, e_ready = sem("mask_ready"), sem("exp_ready")
        g_ready, u_ready, wb_ready = sem("g_ready"), sem("u_ready"), sem("wb_ready")
        silu_ready, prod_ready, hid_ready = sem("silu_ready"), sem("prod_ready"), sem("hid_ready")
        hi_ready, lo_ready, h_used = sem("hi_ready"), sem("lo_ready"), sem("h_used")
        y_ps, yT_ready, y_tok = sem("y_ps"), sem("yT_ready"), sem("y_tok")
        x_done = sem("x_done")
        u1_ready, hid1_ready, hi1a_ready, hi1v_ready, lo1p_ready, lo1v_ready, h1_used = map(sem, (
            "u1_ready", "hid1_ready", "hi1a_ready", "hi1v_ready", "lo1p_ready", "lo1v_ready", "h1_used"))
        rb_ps, rb_ready, ze_ready, acc_ready = map(sem, ("rb_ps", "rb_ready", "ze_ready", "acc_ready"))
        y1_tok = sem("y1_tok")
        qkv_ps, qkv_ready, vT_ps = map(sem, ("qkv_ps", "qkv_ready", "vT_ps"))
        q_steps, k_steps = Steps(sem("q_steps"), 5), Steps(sem("k_steps"), 5)
        scr_w, st_in = sem("scratch_written"), [sem("stack_in0"), sem("stack_in1")]
        s_ready, s_used, m_steps = sem("s_ready"), sem("s_used"), Steps(sem("m_steps"), 10)
        mT_ps, mT_ready = sem("mT_ps"), sem("mT_ready")
        m_in = [sem("m_in0"), sem("m_in1")]
        st_ready, v_hi_ready, v_lo_ready = sem("st_ready"), sem("v_hi_ready"), sem("v_lo_ready")
        v_pad_ready, pv_used, o_ready, o_tok = map(sem, ("v_pad_ready", "pv_used", "o_ready", "o_tok"))
        p0_full, p0_hi, p0_lo_dve, p0_lo_pool, p1_hi, p1_lo = map(sem, (
            "p0_full", "p0_hi", "p0_lo_dve", "p0_lo_pool", "p1_hi", "p1_lo"))
        attn_steps = Steps(sem("attn_steps"), 4)
        aT_ps, aT_hi_ready, aT_lo_ready, o_ps = map(sem, ("aT_ps", "aT_hi_ready", "aT_lo_ready", "o_ps"))
        tail = Steps(sem("tail_steps"), 17)
        x_mid = sem("x_mid")
        tail_var, tail_rstd, tail_eps = sem("tail_var"), sem("tail_rstd"), sem("tail_eps")
        perm_ready, perm_out, mix_in = sem("perm_ready"), sem("perm_out"), sem("mix_in")
        out_sem = sem("out_sem")

        loads = []
        for src, hi, lo, n in ((w0, w0_hi, w0_lo, NW0 * P), (wa, wa_hi, wa_lo, 8 * P)):
            hif = hi.rearrange("p a b -> p (a b)") if len(hi.shape) == 3 else hi.rearrange("p a b c -> p (a b c)")
            lof = lo.rearrange("p a b -> p (a b)") if len(lo.shape) == 3 else lo.rearrange("p a b c -> p (a b c)")
            for a in range(0, n, LOAD):
                b = min(n, a + LOAD)
                loads.append((src[:, a:b], hif[:, a:b], lof[:, a:b], b - a))

        w1_hif, w1_lof = (w.rearrange("p a b -> p (a b)") for w in (w1_hi, w1_lo))
        passed = {}

        def settle(eng):
            if eng.engine not in passed:
                passed[eng.engine] = sem(f"passed{len(passed)}")
            eng.sem_inc(passed[eng.engine], 1)

        def products(eng, o, w_hi_, w_lo_, v_hi, v_lo, start=True, stop=True, **kw):
            eng.matmul(o, w_hi_, v_hi, start=start, stop=False, **kw)
            eng.matmul(o, w_hi_, v_lo, start=False, stop=False, **kw)
            return eng.matmul(o, w_lo_, v_hi, start=False, stop=stop, **kw)

        nth = [STAGES[:s].count(STAGES[s]) for s in range(len(STAGES))]
        nffn = [sum(a[:3] == "ffn" for a in STAGES[:s]) for s in range(len(STAGES))]
        nattn = [sum(a[:4] == "attn" for a in STAGES[:s]) for s in range(len(STAGES))]
        ph_s = lambda: 0

        def chunks(eng, body):
            for s, kind in enumerate(STAGES):
                with eng.Fori(0, NB) as c:
                    body(s, kind, c)

        def split_parts(eng, mem, steps, ga, i):
            steps.begin(ga)
            settle(eng)
            v = steps.mark(eng.tensor_copy(mem.parts[:, i, 0, :], mem.qkv[:, i, :]))
            eng.wait_ge(steps.sem, v)
            v = steps.mark(eng.tensor_tensor(mem.res[:, i, :], mem.qkv[:, i, :], mem.parts[:, i, 0, :], ALU.subtract))
            eng.wait_ge(steps.sem, v)
            settle(eng)
            v = steps.mark(eng.tensor_copy(mem.parts[:, i, 1, :], mem.res[:, i, :]))
            eng.wait_ge(steps.sem, v)
            v = steps.mark(eng.tensor_tensor(mem.res[:, i, :], mem.res[:, i, :], mem.parts[:, i, 1, :], ALU.subtract))
            eng.wait_ge(steps.sem, v)
            settle(eng)
            steps.mark(eng.tensor_copy(mem.parts[:, i, 2, :], mem.res[:, i, :]))
            steps.end()

        def router_act(eng, s, kind, c):
            gr = nffn[s] * NB + c
            ne, br = (E0, BR0) if kind == "ffn0" else (E1, BR1)
            eng.wait_ge(lgT_ps, gr + 1)
            eng.activation(lgT[0:ne, :], bank7[0:ne, :], ACT.Identity, bias=bias[0:ne, br:br + 1]).then_inc(lgT_ready, 1)
            eng.wait_ge(lg_ps, gr + 1)
            src = bank7[:, 0:NT * ne].rearrange("p (t e) -> p t e", e=ne)
            eng.activation(aff[:, :, 0:ne], src, ACT.Sigmoid if kind == "ffn0" else ACT.Copy).then_inc(aff_ready, 1)
            if kind == "ffn1":
                g = nth[s] * NB + c
                eng.wait_ge(mx_ready, g + 1)
                eng.activation(wgt[:, :, 0:E1], sel[:, :, 0:E1], ACT.Exp).then_inc(e_ready, 1)
            eng.wait_ge(wT_ps, gr + 1)
            eng.activation(wT[0:NPART * ne, :], bank7h[0:NPART * ne, 0:S], ACT.Copy).then_inc(wT_ready, 1)

        def w1_piece(eng, c, part):
            cols = bass.ds(c * LOAD1, LOAD1)
            if part == 0:
                eng.wait_ge(w1_in, 16 * (c + 1))
                eng.activation(w1_hif[:, cols], stage_w1[:, :], ACT.Copy).then_inc(w1_hi_done, 1)
            else:
                eng.wait_ge(w1_hi_done, c + 1)
                eng.tensor_tensor(w1_lof[:, cols], stage_w1[:, :], w1_hif[:, cols].bitcast(F32), ALU.subtract).then_inc(w1_lo_done, 1)

        def ffn0_act(eng, g, s, c):
            def hi_part(p):
                eng.wait_ge(hid_ready, ONE + g * NPS + p + 1)
                if p >= NH:
                    eng.wait_ge(h_used, ONE + g * NPS + p - NH + 1)
                else:
                    eng.wait_ge(h_used, ONE + g * NPS)
                eng.activation(h_hi[:, p % NH, :], hid[:, p % 3, :], ACT.Copy).then_inc(hi_ready, 1)

            for p in range(NPS):
                eng.wait_ge(g_ready, g * NPS + p + 1)
                if p >= 2:
                    eng.wait_ge(prod_ready, ONE + g * NPS + p - 1)
                else:
                    eng.wait_ge(prod_ready, ONE + g * NPS)
                eng.activation(gate[:, p % 2, :], bank[p % 2][:, :], ACT.Silu, bias=bias[:, BG + p:BG + p + 1]).then_inc(silu_ready, 1)
                if p >= 1:
                    hi_part(p - 1)
                if s == FIRST1 - 1 and p == W1_AT:
                    w1_piece(eng, c, 0)
            hi_part(NPS - 1)
            eng.wait_ge(y_ps, g + 1)
            eng.activation(yT[:, :], bank[5][:, :], ACT.Identity, bias=bias[:, BDS:BDS + 1]).then_inc(yT_ready, 1)

        def ffn1_act(eng, g):
            def hi_part(j):
                eng.wait_ge(hid1_ready, ONE + g * NJ + j + 1)
                eng.wait_ge(h1_used, ONE + g * NJ + (j - NH + 1 if j >= NH else 0))
                eng.activation(h_hi[:, j % NH, :], hid[:, j % 3, :], ACT.Copy).then_inc(hi1a_ready, 1)

            for j in range(NJ):
                if j % HC == 0:
                    e = j // HC
                    eng.wait_ge(rb_ps, g * E1 + e + 1)
                    eng.wait_ge(ze_ready, ONE + g * E1 + (e - 1 if e >= 2 else 0))
                    eng.activation(rb[:, e % 2, :], bank[4][:, :], ACT.Copy).then_inc(rb_ready, 1)
                eng.wait_ge(u1_ready, g * NJ + j + 1)
                if j >= 3:
                    q = j - 3
                    if q % 2 == 0:
                        eng.wait_ge(lo1p_ready, ONE + g * (NJ // 2) + q // 2 + 1)
                    else:
                        eng.wait_ge(lo1v_ready, ONE + g * (NJ // 2) + q // 2 + 1)
                else:
                    eng.wait_ge(lo1p_ready, ONE + g * (NJ // 2))
                    eng.wait_ge(lo1v_ready, ONE + g * (NJ // 2))
                eng.activation(hid[:, j % 3, :], bank[j % 3][:, :], ACT.Relu, bias=bias[:, B1 + j:B1 + j + 1]).then_inc(hid1_ready, 1)
                if j % 2 == 0:
                    hi_part(j)

        def v_part(mem, i):
            return mem.v_parts[:, :, :, i, 0:HD].rearrange("p t h d -> p (t h) d")

        def attn_act(eng, kind, mem, ga, gk):
            causal = kind == "attn0"
            for i in range(3):
                eng.wait_ge(qkv_ps, 3 * ga + i + 1)
                eng.activation(mem.qkv[:, i, :], bank[i][:, :], ACT.Copy, scale=SCALE if i == 0 else 1.0).then_inc(qkv_ready, 1)
            eng.wait_ge(vT_ps, ga + 1)
            eng.activation(v_part(mem, 0), bank7[:, :].rearrange("p (n d) -> p n d", d=HD), ACT.Copy).then_inc(v_hi_ready, 1)
            if causal:
                for half in range(2):
                    eng.wait_ge(mT_ps, ONE + 2 * gk + half + 1)
                    eng.activation(mem.mT[:, half, :], bank7h[0:NPART * HALF, 0:S], ACT.Copy).then_inc(mT_ready, 1)

            def take_outputs(quad):
                eng.wait_ge(pv_used, ONE + (ga * H + (quad + 1) * QUAD) * NT)
                eng.activation(o_sb[:, quad % 2, :], bank[6 + quad % 2][:, :], ACT.Copy).then_inc(o_ready, 1)

            for h in range(H):
                if h >= QUAD and h % QUAD == 1:
                    take_outputs(h // QUAD - 1)
                for kb in range(NT):
                    i = h * NT + kb
                    n = ga * H * NT + i
                    eng.wait_ge(st_ready, n + 1)
                    if causal:
                        if kb % 2 == 0:
                            eng.wait_ge(p0_lo_dve, ONE + (gk * H + max(h - 1, 0)) * 2 + (kb // 2 + 1 if h else 0))
                        else:
                            eng.wait_ge(p0_lo_pool, ONE + (gk * H + max(h - 1, 0)) * 2 + (kb // 2 + 1 if h else 0))
                        eng.activation(p_full[:, kb, 0:S - kb * P], bank[kb][:, 0:S - kb * P], ACT.Exp).then_inc(p0_full, 1)
                    else:
                        eng.wait_ge(pv_used, ONE + ga * H * NT + (i - RING + 1 if i >= RING else 0))
                        eng.activation(p_hi[:, i % RING, :], bank[kb][:, :], ACT.Relu).then_inc(p1_hi, 1)
            take_outputs(H // QUAD - 1)
            eng.wait_ge(aT_ps, ONE + ga + 1)
            if causal:
                eng.activation(mem.aT_perm[:, :].rearrange("p (q r) -> p r q", q=GQ),
                               bank6[:, :].rearrange("p (r q) -> p r q", q=GQ), ACT.Copy).then_inc(perm_ready, 1)
                eng.wait_ge(mix_in, 16 * (gk + 1))
                eng.activation(mem.aT_hi[:, :], mem.aT_mix[:, :], ACT.Copy).then_inc(aT_hi_ready, 1)
            else:
                eng.activation(mem.aT_hi[:, :], bank6[:, :], ACT.Copy).then_inc(aT_hi_ready, 1)

        def layernorm(eng, steps, visit, src):
            steps.begin(visit)
            for t in range(NT):
                v = steps.mark(eng.bn_stats(stats[:, t, :], src[:, t, :]))
            eng.wait_ge(steps.sem, v)
            settle(eng)
            for t in range(NT):
                v = steps.mark(eng.bn_aggr(mv[:, t, :], stats[:, t, :]))
            eng.wait_ge(steps.sem, v)
            steps.mark(eng.tensor_scalar(ve[:, :], mv[:, :, 1], LN_EPS, None, ALU.add))
            eng.wait_ge(rstd_ready, visit + 1)
            eng.wait_ge(xnT_ps, ONE + visit)
            for t in range(NT):
                v = steps.mark(eng.tensor_scalar(xn[:, t, :], src[:, t, :], mv[:, t, 0:1], rstd[:, t:t + 1],
                                                 ALU.subtract, ALU.mult))
            steps.end()

        def split3(eng, steps, ne):
            for i in range(NPART):
                src = wgt if i == 0 else sel
                v = steps.mark(eng.tensor_copy(wparts[:, :, i * ne:(i + 1) * ne], src[:, :, 0:ne]))
                eng.wait_ge(steps.sem, v)
                if i < 2:
                    v = steps.mark(eng.tensor_tensor(sel[:, :, 0:ne], src[:, :, 0:ne], wparts[:, :, i * ne:(i + 1) * ne], ALU.subtract))
                    eng.wait_ge(steps.sem, v)

        def router0_dve(eng, s, c):
            st = top0
            st.begin(nth[s] * NB + c)
            eng.wait_ge(aff_ready, nffn[s] * NB + c + 1)
            settle(eng)
            for t in range(NT):
                v = st.mark(eng.max(m8[:, t, :], aff[:, t, :]))
            eng.wait_ge(st.sem, v)
            settle(eng)
            for t in range(NT):
                st.mark(eng.match_replace(sel[:, t, :], m8[:, t, :], aff[:, t, :], -1.0))
            v = st.mark(eng.tensor_reduce(den[:, 0, :], m8[:, :, :], AX_X, ALU.add))
            eng.wait_ge(st.sem, v)
            v = st.mark(eng.tensor_scalar(den[:, 0, :], den[:, 0, :], 1e-9, None, ALU.add))
            eng.wait_ge(st.sem, v)
            v = st.mark(eng.reciprocal(den[:, 1, :], den[:, 0, :]))
            v = st.mark(eng.tensor_tensor(sel[:, :, :], sel[:, :, :], aff[:, :, :], ALU.not_equal))
            eng.wait_ge(st.sem, v)
            v = st.mark(eng.tensor_tensor(aff[:, :, :], aff[:, :, :], den[:, 1, :].unsqueeze(2).broadcast_to([P, NT, E0]), ALU.mult))
            eng.wait_ge(st.sem, v)
            v = st.mark(eng.tensor_tensor(wgt[:, :, :], aff[:, :, :], sel[:, :, :], ALU.mult))
            eng.wait_ge(st.sem, v)
            split_tail(eng, st, E0)
            st.end()

        def split_tail(eng, st, ne):
            v = st.mark(eng.tensor_copy(wparts[:, :, 0:ne], wgt[:, :, 0:ne]))
            eng.wait_ge(st.sem, v)
            v = st.mark(eng.tensor_tensor(sel[:, :, 0:ne], wgt[:, :, 0:ne], wparts[:, :, 0:ne], ALU.subtract))
            eng.wait_ge(st.sem, v)
            v = st.mark(eng.tensor_copy(wparts[:, :, ne:2 * ne], sel[:, :, 0:ne]))
            eng.wait_ge(st.sem, v)
            v = st.mark(eng.tensor_tensor(wparts[:, :, 2 * ne:3 * ne], sel[:, :, 0:ne], wparts[:, :, ne:2 * ne], ALU.subtract))

        def router1_dve(eng, s, c):
            st = top1
            g = nth[s] * NB + c
            st.begin(g)
            a, r, w = aff[:, :, 0:E1], sel[:, :, 0:E1], wgt[:, :, 0:E1]
            bc = lambda v1: v1.broadcast_to([P, NT, E1])
            eng.wait_ge(aff_ready, nffn[s] * NB + c + 1)
            settle(eng)
            for t in range(NT):
                v = st.mark(eng.max(m8[:, t, :], aff[:, t, 0:E1]))
            eng.wait_ge(st.sem, v)
            settle(eng)
            for t in range(NT):
                v = st.mark(eng.max_index(i8[:, t, :], m8[:, t, :], aff[:, t, 0:E1]))
            eng.wait_ge(st.sem, v)
            v = st.mark(eng.tensor_copy(i8f[:, :, :], i8[:, :, :]))
            eng.wait_ge(st.sem, v)
            v = st.mark(eng.tensor_tensor(r, iota8[:, :, :], bc(i8f[:, :, 0:1]), ALU.is_equal))
            v = st.mark(eng.tensor_tensor(w, iota8[:, :, :], bc(i8f[:, :, 1:2]), ALU.is_equal))
            eng.wait_ge(st.sem, v)
            v = st.mark(eng.tensor_tensor(r, r, bc(m8[:, :, 0:1]), ALU.mult))
            v = st.mark(eng.tensor_tensor(w, w, bc(m8[:, :, 1:2]), ALU.mult))
            eng.wait_ge(st.sem, v)
            v = st.mark(eng.tensor_tensor(r, r, w, ALU.add))
            eng.wait_ge(st.sem, v)
            v = st.mark(eng.tensor_scalar(den[:, 0, :], m8[:, :, 0], 0.0, None, ALU.max))
            eng.wait_ge(st.sem, v)
            eng.tensor_tensor(r, r, bc(den[:, 0, :].unsqueeze(2)), ALU.subtract).then_inc(mx_ready, 1)
            eng.wait_ge(e_ready, g + 1)
            v = st.mark(eng.tensor_reduce(den[:, 0, :], w, AX_X, ALU.add))
            eng.wait_ge(st.sem, v)
            v = st.mark(eng.reciprocal(den[:, 1, :], den[:, 0, :]))
            eng.wait_ge(st.sem, v)
            v = st.mark(eng.tensor_tensor(w, w, bc(den[:, 1, :].unsqueeze(2)), ALU.mult))
            eng.wait_ge(st.sem, v)
            split_tail(eng, st, E1)
            assert st.k == 22, st.k

        def ffn0_dve(eng, g, s, c):
            for p in range(NPS):
                if s == FIRST1 - 1 and p == W1_AT + 2:
                    w1_piece(eng, c, 1)
                n = g * NPS + p
                eng.wait_ge(silu_ready, ONE + n + 1)
                eng.wait_ge(u_ready, n + 1)
                eng.wait_ge(hid_ready, ONE + g * NPS + (p - 1 if p >= 2 else 0))
                settle(eng)
                eng.scalar_tensor_tensor(prod[:, p % 2, :], bank[2 + p % 2][:, :], bias[:, BU + p:BU + p + 1],
                                         gate[:, p % 2, :], ALU.add, ALU.mult).then_inc(prod_ready, 1)
                eng.wait_ge(prod_ready, ONE + n + 1)
                eng.wait_ge(lo_ready, ONE + g * NPS + (p - 2 if p >= 3 else 0))
                if p < NP:
                    eng.wait_ge(wb_ready, g * NP + p + 1)
                    eng.tensor_tensor(hid[:, p % 3, :], bank[4][:, :], prod[:, p % 2, :], ALU.mult).then_inc(hid_ready, 1)
                else:
                    eng.tensor_copy(hid[:, p % 3, :], prod[:, p % 2, :]).then_inc(hid_ready, 1)

        def ffn1_dve(eng, g):
            def combine(e):
                n = g * E1 + e
                eng.wait_ge(h1_used, ONE + (n + 1) * HC)
                eng.wait_ge(rb_ready, ONE + n + 1)
                eng.wait_ge(acc_ready, ONE + g * E1 + e)
                ybank = bank[5 if e % 2 == 0 else 3]
                dst = yT[:, :] if e == 0 else zed[:, e % 2, :]
                if e == 0:
                    eng.wait_ge(y1_tok, ONE + g)
                settle(eng)
                eng.scalar_tensor_tensor(dst, ybank[:, :], bias[:, B2 + e:B2 + e + 1], rb[:, e % 2, :],
                                         ALU.add, ALU.mult).then_inc(ze_ready, 1)
                eng.wait_ge(ze_ready, ONE + n + 1)
                if e == 0:
                    eng.tensor_copy(den[:, 0, 0:1], yT[:, 0:1]).then_inc(acc_ready, 1)
                else:
                    eng.tensor_tensor(yT[:, :], yT[:, :], dst, ALU.add).then_inc(acc_ready, 1)

            for j in range(NJ + LAG + 1):
                if j < NJ and j % 2 == 1:
                    eng.wait_ge(hid1_ready, ONE + g * NJ + j + 1)
                    eng.wait_ge(h1_used, ONE + g * NJ + (j - NH + 1 if j >= NH else 0))
                    eng.tensor_copy(h_hi[:, j % NH, :], hid[:, j % 3, :]).then_inc(hi1v_ready, 1)
                    eng.wait_ge(hi1v_ready, g * (NJ // 2) + j // 2 + 1)
                    eng.tensor_tensor(h_lo[:, j % NH, :], hid[:, j % 3, :], h_hi[:, j % NH, :].bitcast(F32),
                                      ALU.subtract).then_inc(lo1v_ready, 1)
                d = j - LAG - 1
                if d >= 0 and d % HC == HC - 1:
                    combine(d // HC)

        def attn_dve(eng, kind, mem, s, c, xs):
            causal = kind == "attn0"
            ga, gk = nattn[s] * NB + c, nth[s] * NB + c

            def normalise(half):
                o = bank[4 + half][:, 0:NT * HALF * VC].rearrange("p (n c) -> p n c", c=VC)
                if half:
                    eng.wait_ge(attn_steps.sem, 4 * ga + 2)
                eng.wait_ge(o_tok, H // QUAD * ga + 2 * half + 2)
                if causal:
                    v = attn_steps.mark(eng.reciprocal(mem.rden[:, 1, :], o[:, :, HD]))
                else:
                    eng.tensor_scalar(mem.rden[:, 0, :], o[:, :, HD], KERN_EPS, None, ALU.add).then_inc(tail_eps, 1)
                    eng.wait_ge(tail_eps, 2 * gk + half + 1)
                    v = attn_steps.mark(eng.reciprocal(mem.rden[:, 1, :], mem.rden[:, 0, :]))
                eng.wait_ge(attn_steps.sem, v)
                if half == 0:
                    eng.wait_ge(aT_ps, ONE + ga)
                attn_steps.mark(eng.tensor_tensor(
                    mem.attn[:, :, half * HALF:(half + 1) * HALF, :],
                    o[:, :, 0:HD].rearrange("p (t h) d -> p t h d", h=HALF),
                    mem.rden[:, 1, :].rearrange("p (t h) -> p t h", h=HALF).unsqueeze(3).broadcast_to([P, NT, HALF, HD]), ALU.mult))

            eng.wait_ge(qkv_ready, 3 * ga + 1)
            split_parts(eng, mem, q_steps, ga, 0)
            eng.wait_ge(v_hi_ready, ga + 1)
            eng.tensor_tensor(v_part(mem, 1), bank7[:, :].rearrange("p (n d) -> p n d", d=HD), v_part(mem, 0).bitcast(F32),
                              ALU.subtract).then_inc(v_lo_ready, 1)
            if causal:
                m_steps.begin(gk)
                for half in range(2):
                    for hh in range(HALF):
                        h = half * HALF + hh
                        for qt in range(NT):
                            n = (gk * H + h) * NT + qt
                            eng.wait_ge(s_ready, n + 1)
                            eng.tensor_reduce(mem.rmax[:, qt, h:h + 1], bank[qt][:, 0:(qt + 1) * P], AX_X, ALU.max).then_inc(s_used, 1)
                    eng.wait_ge(s_used, (gk * H + (half + 1) * HALF) * NT)
                    eng.wait_ge(mT_ps, ONE + 2 * gk + half)
                    hs = slice(half * HALF, (half + 1) * HALF)
                    v = m_steps.mark(eng.tensor_scalar(mem.nmax[:, 0, :, :], mem.rmax[:, :, hs], -1.0, None, ALU.mult))
                    eng.wait_ge(m_steps.sem, v)
                    v = m_steps.mark(eng.tensor_copy(mem.mparts[:, :, 0, :], mem.nmax[:, 0, :, :]))
                    eng.wait_ge(m_steps.sem, v)
                    v = m_steps.mark(eng.tensor_tensor(mem.nmax[:, 1, :, :], mem.nmax[:, 0, :, :], mem.mparts[:, :, 0, :], ALU.subtract))
                    eng.wait_ge(m_steps.sem, v)
                    v = m_steps.mark(eng.tensor_copy(mem.mparts[:, :, 1, :], mem.nmax[:, 1, :, :]))
                    eng.wait_ge(m_steps.sem, v)
                    v = m_steps.mark(eng.tensor_tensor(mem.mparts[:, :, 2, :], mem.nmax[:, 1, :, :], mem.mparts[:, :, 1, :], ALU.subtract))
                m_steps.end()
            attn_steps.begin(ga)
            for h in range(H):
                if h == NORM_AT:
                    normalise(0)
                for kb in range(NT):
                    i = h * NT + kb
                    slot, w = i % RING, (S - kb * P if causal else S)
                    if causal:
                        eng.wait_ge(p0_full, gk * H * NT + i + 1)
                        eng.wait_ge(pv_used, ONE + ga * H * NT + (i - RING + 1 if i >= RING else 0))
                        eng.tensor_copy(p_hi[:, slot, 0:w], p_full[:, kb, 0:w]).then_inc(p0_hi, 1)
                        if kb % 2 == 0:
                            eng.wait_ge(p0_hi, gk * H * NT + i + 1)
                            eng.tensor_tensor(p_lo[:, slot, 0:w], p_full[:, kb, 0:w], p_hi[:, slot, 0:w].bitcast(F32),
                                              ALU.subtract).then_inc(p0_lo_dve, 1)
                    else:
                        eng.wait_ge(p1_hi, gk * H * NT + i + 1)
                        settle(eng)
                        eng.scalar_tensor_tensor(p_lo[:, slot, :], bank[kb][:, :], 0.0, p_hi[:, slot, :].bitcast(F32),
                                                 ALU.max, ALU.subtract).then_inc(p1_lo, 1)
            normalise(1)
            attn_steps.end()
            eng.wait_ge(aT_hi_ready, ga + 1)
            eng.tensor_tensor(mem.aT_lo[:, :], mem.aT_mix[:, :] if causal else bank6[:, :], mem.aT_hi[:, :].bitcast(F32), ALU.subtract).then_inc(aT_lo_ready, 1)
            eng.wait_ge(o_ps, ga + 1)
            ob = bank7[:, :].rearrange("p (t d) -> p t d", d=D)
            rbc = lambda i: row[:, i, :].unsqueeze(1).broadcast_to([P, NT, D])
            if causal:
                eng.tensor_tensor(xs, ob, xs, ALU.add).then_inc(x_mid, 1)
                eng.wait_ge(x_mid, gk + 1)
                eng.tensor_tensor(xs, xs, rbc(0), ALU.add).then_inc(x_done, 1)
            else:
                st = tail
                st.begin(gk)
                v = st.mark(eng.tensor_tensor(xn[:, :, :], ob, xn[:, :, :], ALU.add))
                eng.wait_ge(st.sem, v)
                v = st.mark(eng.tensor_tensor(xn[:, :, :], xn[:, :, :], rbc(1), ALU.add))
                eng.wait_ge(st.sem, v)
                for t in range(NT):
                    v = st.mark(eng.bn_stats(stats[:, t, :], xn[:, t, :]))
                eng.wait_ge(st.sem, v)
                settle(eng)
                for t in range(NT):
                    v = st.mark(eng.bn_aggr(mv[:, t, :], stats[:, t, :]))
                eng.wait_ge(st.sem, v)
                eng.tensor_scalar(ve[:, :], mv[:, :, 1], LN_EPS, None, ALU.add).then_inc(tail_var, 1)
                eng.wait_ge(tail_rstd, gk + 1)
                for t in range(NT):
                    v = st.mark(eng.tensor_scalar(xn[:, t, :], xn[:, t, :], mv[:, t, 0:1], rstd[:, t:t + 1],
                                                  ALU.subtract, ALU.mult))
                eng.wait_ge(st.sem, v)
                v = st.mark(eng.tensor_tensor(xn[:, :, :], xn[:, :, :], rbc(2), ALU.mult))
                eng.wait_ge(st.sem, v)
                v = st.mark(eng.tensor_tensor(xn[:, :, :], xn[:, :, :], rbc(3), ALU.add))
                eng.wait_ge(st.sem, v)
                v = st.mark(eng.tensor_tensor(xs, xs, xn[:, :, :], ALU.add))
                eng.wait_ge(st.sem, v)
                eng.tensor_copy(ve[:, 0:1], rstd[:, 0:1]).then_inc(x_done, 1)
                assert st.k == 17, st.k

        def router_pe(eng, s, kind, c):
            gr = nffn[s] * NB + c
            w_hi_, w_lo_, blk, ne = (w0_hi, w0_lo, WR0, E0) if kind == "ffn0" else (w1_hi, w1_lo, WR1, E1)
            products(eng, bank7[:, :], w_hi_[:, blk, :], w_lo_[:, blk, :], xnT_hi[:, :], xnT_lo[:, :]).then_inc(lgT_ps, 1)
            eng.wait_ge(lgT_ready, gr + 1)
            settle(eng)
            for t in range(NT):
                ins = eng.transpose(bank7[:, t * ne:(t + 1) * ne], lgT[0:ne, t * P:(t + 1) * P], ident[0:ne, 0:ne])
            ins.then_inc(lg_ps, 1)

        def router_pe2(eng, kind, gr):
            ne, st, per = (E0, top0, 18) if kind == "ffn0" else (E1, top1, 22)
            eng.wait_ge(st.sem, gr * per + per)
            for t in range(NT):
                ins = eng.transpose(bank7h[0:NPART * ne, t * P:(t + 1) * P], wparts[:, t, 0:NPART * ne], identb)
            ins.then_inc(wT_ps, 1)

        def ffn0_pe(eng, g, gr):
            def down(p):
                eng.wait_ge(hi_ready, g * NPS + p + 1)
                eng.wait_ge(lo_ready, ONE + g * NPS + p + 1)
                products(eng, bank[5][:, :], w0_hi[:, DOWN0 + p, :], w0_lo[:, DOWN0 + p, :],
                         h_hi[:, p % NH, :], h_lo[:, p % NH, :], start=(p == 0), stop=False).then_inc(h_used, 1)

            for p in range(NPS + LAG):
                if p < NPS:
                    eng.wait_ge(silu_ready, ONE + g * NPS + (p - 1 if p >= 2 else 0))
                    products(eng, bank[p % 2][:, :], w0_hi[:, GATE0 + p, :], w0_lo[:, GATE0 + p, :],
                             xnT_hi[:, :], xnT_lo[:, :]).then_inc(g_ready, 1)
                    eng.wait_ge(prod_ready, ONE + g * NPS + (p - 1 if p >= 2 else 0))
                    products(eng, bank[2 + p % 2][:, :], w0_hi[:, UP0 + p, :], w0_lo[:, UP0 + p, :],
                             xnT_hi[:, :], xnT_lo[:, :]).then_inc(u_ready, 1)
                if p == 1:
                    router_pe2(eng, "ffn0", g)
                    eng.wait_ge(wT_ready, gr + 1)
                    weight(eng, g, 0)
                    weight(eng, g, 1)
                if 1 < p < NP:
                    weight(eng, g, p)
                if p >= LAG:
                    down(p - LAG)
            for j in range(NPART):
                ins = eng.matmul(bank[5][:, :], bd_parts[:, j, :], wT[:, :], start=False, stop=(j == NPART - 1))
            ins.then_inc(y_ps, 1)
            eng.wait_ge(yT_ready, g + 1)
            for t in range(NT):
                ins = eng.transpose(bank6[:, t * P:(t + 1) * P], yT[:, t * P:(t + 1) * P], ident[:, :])
            ins.then_inc(y_tok, 1)

        def weight(eng, g, p):
            eng.wait_ge(hid_ready, ONE + g * NPS + p)
            eng.matmul(bank[4][:, :], cbf[0:NPART * E0, C_SEL0 + p * P:C_SEL0 + (p + 1) * P], wT[:, :],
                       start=True, stop=True).then_inc(wb_ready, 1)

        def ffn1_pe(eng, g, gr):
            def down(j):
                e = j // HC
                if j % 2 == 0:
                    eng.wait_ge(lo1p_ready, ONE + g * (NJ // 2) + j // 2 + 1)
                else:
                    eng.wait_ge(lo1v_ready, ONE + g * (NJ // 2) + j // 2 + 1)
                if j % HC == 0:
                    eng.wait_ge(ze_ready, ONE + g * E1 + (e - 1 if e >= 2 else 0))
                ybank = bank[5 if e % 2 == 0 else 3]
                ins = products(eng, ybank[:, :], w1_hi[:, DOWN1 + j, :], w1_lo[:, DOWN1 + j, :],
                               h_hi[:, j % NH, :], h_lo[:, j % NH, :], start=(j % HC == 0), stop=(j % HC == HC - 1))
                ins.then_inc(h1_used, 1)

            def spread(e):
                eng.wait_ge(rb_ready, ONE + g * E1 + e)
                eng.matmul(bank[4][:, :], cbf[0:NPART * E1, C_SEL1 + e * P:C_SEL1 + (e + 1) * P],
                           wT[0:NPART * E1, :], start=True, stop=True).then_inc(rb_ps, 1)

            for j in range(NJ + LAG):
                if j == 0:
                    router_pe2(eng, "ffn1", g)
                    eng.wait_ge(wT_ready, gr + 1)
                if j < NJ and j % HC == 0:
                    spread(j // HC)
                if j < NJ:
                    eng.wait_ge(hid1_ready, ONE + g * NJ + (j - 2 if j >= 3 else 0))
                    products(eng, bank[j % 3][:, :], w1_hi[:, UP1 + j, :], w1_lo[:, UP1 + j, :],
                             xnT_hi[:, :], xnT_lo[:, :]).then_inc(u1_ready, 1)
                if j >= LAG:
                    down(j - LAG)
            eng.wait_ge(acc_ready, ONE + g * E1 + E1)
            for t in range(NT):
                ins = eng.transpose(bank6[:, t * P:(t + 1) * P], yT[:, t * P:(t + 1) * P], ident[:, :])
            ins.then_inc(y1_tok, 1)

        def attn_pe(eng, kind, mem, ga, gk, G):
            causal = kind == "attn0"
            layer = 0 if causal else 1
            for i in range(3):
                products(eng, bank[i][:, :], wa_hi[:, layer, i, :], wa_lo[:, layer, i, :],
                         xnT_hi[:, :], xnT_lo[:, :]).then_inc(qkv_ps, 1)
            eng.wait_ge(qkv_ready, 3 * ga + 3)
            for t in range(NT):
                ins = eng.transpose(bank7[:, t * P:(t + 1) * P], mem.qkv[:, 2, t * P:(t + 1) * P], ident[:, :])
            ins.then_inc(vT_ps, 1)

            def head(st, h, rows):
                p0 = (h % 2) * STACK
                return st[p0:p0 + rows, h // 2, :]

            def maxima(half):
                eng.wait_ge(m_steps.sem, gk * 10 + 5 * half + 5)
                if half:
                    eng.wait_ge(mT_ready, 2 * gk + 1)
                else:
                    eng.wait_ge(v_lo_ready, ga + 1)
                for t in range(NT):
                    ins = eng.transpose(bank7h[0:NPART * HALF, t * P:(t + 1) * P],
                                        mem.mparts[:, t, :, :].rearrange("p a b -> p (a b)"), identb)
                ins.then_inc(mT_ps, 1)

            if causal:
                for half in range(2):
                    eng.wait_ge(st_in[half], 16 * 4 * (ga + 1))
                    for h in range(half * HALF, (half + 1) * HALF):
                        qs, ks = head(mem.q_st, h, QK_ROWS), head(mem.k_st, h, QK_ROWS)
                        for qt in range(NT):
                            n = (gk * H + h) * NT + qt
                            if h:
                                eng.wait_ge(s_used, n - NT + 1)
                            eng.matmul(bank[qt][:, 0:(qt + 1) * P], qs[:, qt * P:(qt + 1) * P], ks[:, 0:(qt + 1) * P],
                                       start=True, stop=True)
                            eng.matmul(bank[qt][:, qt * P:(qt + 1) * P], identb, neg, start=False, stop=True,
                                       skip_group_check=True).then_inc(s_ready, 1)
                    if half == 1:
                        maxima(0)
                maxima(1)
                rows_ = QK_ROWS + NPART
            else:
                rows_ = QK_ROWS

            def pv(h, kb):
                i = h * NT + kb
                quad, j = h // QUAD, h % QUAD
                slot, q0 = i % RING, (kb * P if causal else 0)
                if kb == 0:
                    eng.wait_ge(v_pad_ready, ga * H + h + 1)
                if j == 0 and kb == 0 and quad >= 2:
                    eng.wait_ge(o_ready, H // QUAD * ga + quad - 1)
                if not causal:
                    eng.wait_ge(p1_lo, gk * H * NT + i + 1)
                elif kb % 2 == 0:
                    eng.wait_ge(p0_lo_dve, ONE + (gk * H + h) * 2 + kb // 2 + 1)
                else:
                    eng.wait_ge(p0_lo_pool, ONE + (gk * H + h) * 2 + kb // 2 + 1)
                o = bank[6 + quad % 2][:, q0:S]
                eng.matmul(o, v_pad[:, j, kb, :], p_hi[:, slot, 0:S - q0], start=(j == 0 and kb == 0), stop=False, skip_group_check=True)
                eng.matmul(o, v_pad[:, j, kb, :], p_lo[:, slot, 0:S - q0], start=False, stop=(j == QUAD - 1 and kb == NT - 1),
                           skip_group_check=True).then_inc(pv_used, 1)

            def to_tokens(quad):
                eng.wait_ge(o_ready, H // QUAD * ga + quad + 1)
                for qt in range(NT):
                    at = (qt * HALF + (quad % 2) * QUAD) * VC
                    ins = eng.matmul(bank[4 + quad // 2][:, at:at + QUAD * VC], o_sb[:, quad % 2, qt * P:(qt + 1) * P], osel[:, :],
                                     start=True, stop=True)
                ins.then_inc(o_tok, 1)

            for h in range(H + 1):
                if h >= QUAD and h % QUAD == 2:
                    to_tokens(h // QUAD - 1)
                if h < H and h % HALF == 0:
                    half = h // HALF
                    if causal:
                        eng.wait_ge(m_in[half], 96 * (gk + 1))
                    else:
                        eng.wait_ge(st_in[half], 16 * 4 * (ga + 1))
                for kb in range(NT):
                    if h < H:
                        qs, ks = head(mem.q_st, h, rows_), head(mem.k_st, h, rows_)
                        n = (gk * H + h) * NT + kb
                        q0 = kb * P if causal else 0
                        if h and causal:
                            eng.wait_ge(p0_full, n - NT + 1)
                        elif h:
                            eng.wait_ge(p1_lo, n - NT + 1)
                        elif causal:
                            eng.wait_ge(s_used, (gk + 1) * H * NT)
                        ins = eng.matmul(bank[kb][:, 0:S - q0], ks[:, kb * P:(kb + 1) * P], qs[:, q0:S],
                                         start=True, stop=True)
                        if causal:
                            ins = eng.matmul(bank[kb][:, 0:P], identb, negT, start=False, stop=True, skip_group_check=True)
                        ins.then_inc(st_ready, 1)
                    if h >= 1:
                        pv(h - 1, kb)
            to_tokens(H // QUAD - 1)
            eng.wait_ge(attn_steps.sem, 4 * ga + 4)
            for t in range(NT):
                ins = eng.transpose(bank6[:, t * P:(t + 1) * P], mem.attn[:, t, :, :].rearrange("p h d -> p (h d)"), ident[:, :])
            ins.then_inc(aT_ps, 1)
            eng.wait_ge(aT_lo_ready, ga + 1)
            for t in range(NT):
                ts = slice(t * P, (t + 1) * P)
                ins = products(eng, bank7[:, ts], mem.aT_hi[:, ts], mem.aT_lo[:, ts], wa_hi[:, layer, WO, :], wa_lo[:, layer, WO, :])
            ins.then_inc(o_ps, 1)

        block = ctx.enter_context(nc.Block())

        @block.sync
        def _(eng):
            eng.dma_start(x[:, :, :], x_in).then_inc(x_in_sem, 16)
            eng.dma_start(stage_c[:, :], consts).then_inc(small_in, 16)
            eng.dma_start(bias[:, :], biases).then_inc(small_in, 16)
            eng.dma_start(row[:, :, :], rows).then_inc(small_in, 16)
            eng.dma_start(stage_bd[:, 0, :], bd3).then_inc(small_in, 16)
            for n, (src, _, _, cols) in enumerate(loads):
                if n >= 4:
                    eng.wait_ge(w_lo_done, n - 3)
                eng.dma_start(stage_w[:, n % 4, 0:cols], src).then_inc(w_in[n % 4], 16)

            for s, kind in enumerate(STAGES):
                if s == FIRST1 - 1:
                    eng.wait_ge(x_done, ONE + s * NB)
                    with eng.Fori(0, NB) as c:
                        eng.wait_ge(w1_lo_done, ONE + c)
                        eng.dma_start(stage_w1[:, :], w1[:, bass.ds(c * LOAD1, LOAD1)]).then_inc(w1_in, 16)
                if kind[:4] != "attn":
                    continue
                mem = mem0 if kind == "attn0" else mem1
                a = nattn[s]
                with eng.Fori(0, NB) as c:
                    ga = a * NB + c
                    eng.wait_ge(q_steps.sem, ga * 5 + 5)
                    eng.wait_ge(k_steps.sem, ga * 5 + 5)
                    for i, part_of in enumerate((Q_PART, K_PART)):
                        for r in range(PAIRS):
                            eng.dma_start(scratch[bass.ds(ga, 1), i, :, r * HD:(r + 1) * HD, :].rearrange("g h d s -> (g h) d s"),
                                          mem.parts[:, i, part_of[r], :]).then_inc(scr_w, 16)
                    eng.wait_ge(scr_w, ga * 192 + 192)
                    for half in range(2):
                        for i, st in enumerate((mem.q_st, mem.k_st)):
                            for par in range(2):
                                src = scratch[bass.ds(ga, 1), i, :, :, :].rearrange(
                                    "g (hf j two) p s -> g hf two p j s", hf=2, two=2)[0, half, par]
                                p0 = par * STACK
                                eng.dma_start(st[p0:p0 + QK_ROWS, half * 4:half * 4 + 4, :], src).then_inc(st_in[half], 16)
                    if kind == "attn0":
                        for half in range(2):
                            eng.wait_ge(mT_ready, 2 * ga + half + 1)
                            for i in range(NPART):
                                for par in range(2):
                                    p0 = par * STACK + MAX_ROW + i
                                    eng.dma_start(mem.q_st[p0:p0 + 1, half * 4:half * 4 + 4, :],
                                                  mem.mT[i * HALF + par:i * HALF + HALF:2, half, :]).then_inc(m_in[half], 16)
                        eng.wait_ge(perm_ready, ga + 1)
                        eng.dma_start(mixed[bass.ds(ga, 1), :, :].rearrange("g p s -> (g p) s"), mem.aT_perm[:, :]).then_inc(perm_out, 16)
                        eng.wait_ge(perm_out, 16 * (ga + 1))
                        eng.dma_start(mem.aT_mix.rearrange("p (h r) -> p h r", h=H),
                                      mixed[bass.ds(ga, 1), :, :].rearrange("g (h d) (q r) -> g (d q) h r", d=HD, q=GQ)[0]).then_inc(mix_in, 16)
            s = len(STAGES) - 1
            with eng.Fori(0, NB) as c:
                eng.wait_ge(x_done, ONE + s * NB + c + 1)
                eng.dma_start(out[:, bass.ds(c * NT, NT), :], x[:, bass.ds(c * NT, NT), :]).then_inc(out_sem, 16)
            eng.wait_ge(out_sem, 16 * NB)

        @block.gpsimd
        def _(eng):
            for counts in (lo_ready, lo1p_ready, p0_lo_pool):
                eng.sem_inc(counts, ONE)
            eng.memset(mhalf[:, :], -0.5).then_inc(pool_init, 1)

            def rstd_of(ready, value):
                eng.wait_ge(ready, value)
                return eng.tensor_tensor(rstd[:, :], ve[:, :], mhalf[:, :], ALU.pow)

            def p_lo_pool(c, h):
                for kb in range(1, NT, 2):
                    i = h * NT + kb
                    w = S - kb * P
                    eng.wait_ge(p0_hi, c * H * NT + i + 1)
                    eng.tensor_tensor(p_lo[:, i % RING, 0:w], p_full[:, kb, 0:w], p_hi[:, i % RING, 0:w].bitcast(F32),
                                      ALU.subtract).then_inc(p0_lo_pool, 1)

            eng.wait_ge(pool_init, 1)
            for s, kind in enumerate(STAGES):
                if kind[:4] == "attn":
                    mem = mem0 if kind == "attn0" else mem1
                    eng.wait_ge(x_done, ONE + s * NB)
                    eng.memset(v_pad[:, :, :, :].bitcast(F32), 0.0).then_inc(pool_init, 1)
                    eng.wait_ge(pool_init, 2 + nattn[s])
                with eng.Fori(0, NB) as c:
                    G = s * NB + c
                    rstd_of(ln_steps.sem, G * 13 + 9).then_inc(rstd_ready, 1)
                    if kind == "ffn0":
                        g = nth[s] * NB + c
                        for p in range(NPS):
                            n = g * NPS + p
                            eng.wait_ge(hi_ready, n + 1)
                            eng.tensor_tensor(h_lo[:, p % NH, :], hid[:, p % 3, :], h_hi[:, p % NH, :].bitcast(F32),
                                              ALU.subtract).then_inc(lo_ready, 1)
                    if kind == "ffn1":
                        g = nth[s] * NB + c
                        for j in range(0, NJ, 2):
                            eng.wait_ge(hi1a_ready, g * (NJ // 2) + j // 2 + 1)
                            eng.tensor_tensor(h_lo[:, j % NH, :], hid[:, j % 3, :], h_hi[:, j % NH, :].bitcast(F32),
                                              ALU.subtract).then_inc(lo1p_ready, 1)
                    if kind[:4] == "attn":
                        ga = nattn[s] * NB + c
                        eng.wait_ge(qkv_ready, 3 * ga + 2)
                        split_parts(eng, mem, k_steps, ga, 1)
                        eng.wait_ge(v_lo_ready, ga + 1)
                        for h in range(H):
                            eng.wait_ge(pv_used, ONE + ga * H * NT + (h - QUAD + 1 if h >= QUAD else 0) * NT)
                            settle(eng)
                            eng.tensor_copy(v_pad[:, h % QUAD, :, 32 * (h % QUAD):32 * (h % QUAD) + 2 * VC],
                                            mem.v_parts[:, :, h, :, :].rearrange("p t i c -> p t (i c)").bitcast(F32)).then_inc(v_pad_ready, 1)
                            if kind == "attn0" and h:
                                p_lo_pool(c, h - 1)
                        if kind == "attn0":
                            p_lo_pool(c, H - 1)
                        if kind == "attn1":
                            eng.wait_ge(tail_var, c + 1)
                            eng.tensor_tensor(rstd[:, :], ve[:, :], mhalf[:, :], ALU.pow).then_inc(tail_rstd, 1)

        @block.scalar
        def _(eng):
            for counts in (silu_ready, rb_ready, hid1_ready):
                eng.sem_inc(counts, ONE)
            eng.wait_ge(small_in, 64)
            eng.activation(ident[:, :], stage_c[:, C_ID:C_ID + P], ACT.Copy).then_inc(const_ready, 1)
            eng.activation(osel[:, :], stage_c[:, C_OSEL:C_OSEL + QUAD * VC], ACT.Copy).then_inc(const_ready, 1)
            eng.activation(cbf[:, :], stage_c[:, 0:NCONST], ACT.Copy).then_inc(const_ready, 1)
            for n, (_, hi, _, cols) in enumerate(loads):
                eng.wait_ge(w_in[n % 4], 16 * (n // 4 + 1))
                eng.activation(hi, stage_w[:, n % 4, 0:cols], ACT.Copy).then_inc(w_hi_done, 1)

            for s, kind in enumerate(STAGES):
                with eng.Fori(0, NB) as c:
                    G = s * NB + c
                    eng.wait_ge(xnT_ps, ONE + G + 1)
                    eng.activation(xnT_hi[:, :], bank6[:, :], ACT.Copy).then_inc(xnT_hi_ready, 1)
                    if kind[:3] == "ffn":
                        router_act(eng, s, kind, c)
                    if kind == "ffn0":
                        ffn0_act(eng, nth[s] * NB + c, s, c)
                    if kind == "ffn1":
                        ffn1_act(eng, nth[s] * NB + c)
                    if kind[:4] == "attn":
                        attn_act(eng, kind, mem0 if kind == "attn0" else mem1, nattn[s] * NB + c, nth[s] * NB + c)

        @block.vector
        def _(eng):
            for counts in (prod_ready, hid_ready, ze_ready, acc_ready, x_done, lo1v_ready, p0_lo_dve, w1_lo_done):
                eng.sem_inc(counts, ONE)
            eng.wait_ge(small_in, 64)
            ini = Steps(sem("dve_init"), 10)
            ini.begin(0)
            for j in range(NPART):
                src = stage_bd[:, 0, :] if j == 0 else stage_bd[:, 1, :]
                v = ini.mark(eng.tensor_copy(bd_parts[:, j, :], src))
                eng.wait_ge(ini.sem, v)
                if j < 2:
                    v = ini.mark(eng.tensor_tensor(stage_bd[:, 1, :], src, bd_parts[:, j, :], ALU.subtract))
                    eng.wait_ge(ini.sem, v)
            for _ in range(5):
                ini.mark(eng.memset(ve[:, :], 1.0))
                eng.wait_ge(ini.sem, ini.base + ini.k)
            ini.end()
            for n, (_, hi, lo, cols) in enumerate(loads):
                eng.wait_ge(w_hi_done, n + 1)
                eng.tensor_tensor(lo, stage_w[:, n % 4, 0:cols], hi.bitcast(F32), ALU.subtract).then_inc(w_lo_done, 1)
            eng.wait_ge(x_in_sem, 16)
            eng.wait_ge(w_lo_done, len(loads))

            for s, kind in enumerate(STAGES):
                mem = mem0 if kind == "attn0" else mem1
                if kind[:4] == "attn":
                    eng.memset(mem.k_st[:, :, :], 1.0).then_inc(const_ready, 1)
                    eng.memset(mem.v_parts[:, :, :, 0, HD:VC].bitcast(F32), 1.0).then_inc(const_ready, 1)
                    eng.memset(mem.v_parts[:, :, :, 1, HD:VC].bitcast(F32), 0.0).then_inc(const_ready, 1)
                if kind == "ffn1":
                    for e in range(E1):
                        eng.memset(iota8[:, :, e], float(e)).then_inc(const_ready, 1)
                with eng.Fori(0, NB) as c:
                    G = s * NB + c
                    xs = x[:, bass.ds(c * NT, NT), :]
                    if s:
                        eng.wait_ge(x_done, ONE + G - NB + 1)
                    layernorm(eng, ln_steps, G, xs)
                    eng.wait_ge(xnT_hi_ready, G + 1)
                    eng.tensor_tensor(xnT_lo[:, :], bank6[:, :], xnT_hi[:, :].bitcast(F32), ALU.subtract).then_inc(xnT_lo_ready, 1)
                    if kind == "ffn0":
                        router0_dve(eng, s, c)
                        ffn0_dve(eng, nth[s] * NB + c, s, c)
                        eng.wait_ge(y_tok, nth[s] * NB + c + 1)
                    if kind == "ffn1":
                        router1_dve(eng, s, c)
                        ffn1_dve(eng, nth[s] * NB + c)
                        eng.wait_ge(y1_tok, ONE + nth[s] * NB + c + 1)
                    if kind[:3] == "ffn":
                        settle(eng)
                        eng.scalar_tensor_tensor(xs, bank6[:, :].rearrange("p (t d) -> p t d", d=D), 0.5, xs,
                                                 ALU.mult, ALU.add).then_inc(x_done, 1)
                    else:
                        attn_dve(eng, kind, mem, s, c, xs)

        @block.tensor
        def _(eng):
            for counts in (h_used, h1_used, y1_tok, mT_ps, aT_ps, pv_used, xnT_ps):
                eng.sem_inc(counts, ONE)
            eng.wait_ge(const_ready, 3)
            eng.wait_ge(w_lo_done, len(loads))
            for s, kind in enumerate(STAGES):
                if s == FIRST1:
                    eng.wait_ge(w1_lo_done, ONE + NB)
                with eng.Fori(0, NB) as c:
                    G = s * NB + c
                    eng.wait_ge(ln_steps.sem, G * 13 + 13)
                    eng.wait_ge(x_done, ONE + G)
                    for t in range(NT):
                        ins = eng.transpose(bank6[:, t * P:(t + 1) * P], xn[:, t, :], ident[:, :])
                    ins.then_inc(xnT_ps, 1)
                    eng.wait_ge(xnT_lo_ready, G + 1)
                    if kind[:3] == "ffn":
                        router_pe(eng, s, kind, c)
                    if kind == "ffn0":
                        ffn0_pe(eng, nth[s] * NB + c, nffn[s] * NB + c)
                    if kind == "ffn1":
                        ffn1_pe(eng, nth[s] * NB + c, nffn[s] * NB + c)
                    if kind[:4] == "attn":
                        attn_pe(eng, kind, mem0 if kind == "attn0" else mem1, nattn[s] * NB + c, nth[s] * NB + c, G)


def _layout(i):
    pad = lambda a, n: np.concatenate([a, np.zeros(a.shape[:-1] + (n - a.shape[-1],), a.dtype)], -1)
    f = {k: np.asarray(v) for k, v in i.items()}
    cols = lambda w: np.moveaxis(w, 0, 1).reshape(D, -1)
    w0 = np.concatenate([
        cols(f["L0_ffn_Wg"]), pad(f["L0_ffn_Wg_s"], P), cols(f["L0_ffn_Wu"]), pad(f["L0_ffn_Wu_s"], P),
        f["L0_ffn_Wd"].reshape(NP, P, D).transpose(1, 0, 2).reshape(P, -1), pad(f["L0_ffn_Wd_s"].T, P).T,
        pad(f["L0_ffn_Wr"], P)], 1)
    w1 = np.concatenate([
        cols(f["L1_ffn_W1"]), f["L1_ffn_W2"].reshape(NJ, P, D).transpose(1, 0, 2).reshape(P, -1),
        pad(f["L1_ffn_Wr"], P)], 1)
    qkv1 = f["L1_attn_w_qkv"].reshape(D, H, 3, HD).transpose(0, 2, 1, 3).reshape(D, 3 * D)
    wa = np.concatenate([f["L0_attn_Wq"], f["L0_attn_Wk"], f["L0_attn_Wv"], f["L0_attn_Wo"].reshape(GQ, HD, D).transpose(1, 0, 2).reshape(D, D), qkv1, f["L1_attn_w_out"]], 1)
    col = lambda v: pad(v.reshape(1, -1), -(-v.size // P) * P).reshape(-1, P).T
    biases = np.concatenate([
        col(f["L0_ffn_bg"]), col(f["L0_ffn_bg_s"]), col(f["L0_ffn_bu"]), col(f["L0_ffn_bu_s"]), col(f["L0_ffn_bd_s"]),
        col(f["L0_ffn_br"]), col(f["L1_ffn_b1"]), col(f["L1_ffn_b2"]), col(f["L1_ffn_br"])], 1)
    bd3 = np.tile(f["L0_ffn_bd"], (NPART, 1))
    rows = np.tile(np.stack([f["L0_attn_bo"], f["L1_attn_b_out"], f["L1_attn_gamma"], f["L1_attn_beta"]])[None], (P, 1, 1))
    r = np.arange(P)
    consts = np.zeros((P, NCONST_ALL), np.float32)
    consts[r, C_ID + r] = 1
    consts[:, C_NEG:C_NEG + P] = np.where(r[None, :] > r[:, None], -1e30, 0)
    consts[:, C_NEGT:C_NEGT + P] = consts[:, C_NEG:C_NEG + P].T
    for j in range(QUAD):
        for c in range(2 * VC):
            consts[32 * j + c, C_OSEL + j * VC + c % VC] = 1
    for part in range(NPART):
        for e in range(E0):
            at = C_SEL0 + e * I0
            consts[part * E0 + e, at:at + I0] = 1
        for e in range(E1):
            consts[part * E1 + e, C_SEL1 + e * P:C_SEL1 + (e + 1) * P] = 1
    x = f["L0_attn_x"].reshape(NB * NT, P, D).transpose(1, 0, 2)
    return dict(x=x, w0=w0, w1=w1, wa=wa, biases=biases, bd3=bd3, rows=rows, consts=consts)


def kernel(**inputs):
    import concourse.bacc as _bacc
    from concourse.bass_utils import run_bass_kernel_spmd as _run

    nc = _bacc.Bacc("TRN2", target_bir_lowering=False, num_devices=1)
    arrays, args = {}, []
    for name, a in _layout(inputs).items():
        a = np.ascontiguousarray(a)
        arrays[f"in_{name}_dram"] = a
        args.append(nc.dram_tensor(f"in_{name}_dram", a.shape, mybir.dt.from_np(a.dtype), kind="ExternalInput").ap())
    out = nc.dram_tensor("out_0_dram", (P, NB * NT, D), F32, kind="ExternalOutput").ap()
    scratch = nc.dram_tensor("parts_dram", (2 * NB, 2, H, QK_ROWS, S), BF16, kind="Internal").ap()
    mixed = nc.dram_tensor("mixed_dram", (NB, P, S), F32, kind="Internal").ap()
    build(nc, *args, out, scratch, mixed)
    r = _run(nc, [arrays], core_ids=[0])
    o = r.results[0]["out_0_dram"]
    return o.transpose(1, 0, 2).reshape(NB, S, D)
```

```python
from contextlib import ExitStack

import numpy as np
import concourse.bass as bass
from concourse import mybir

ALU = mybir.AluOpType
ACT = mybir.ActivationFunctionType
AX_X = mybir.AxisListType.X
F32 = mybir.dt.float32
F32R = mybir.dt.float32r
BF16 = mybir.dt.bfloat16
U32 = mybir.dt.uint32

P = 128
D = 128
NB, S = 8, 512
NT = S // P
H, HD = 16, 8
E0, K0, I0 = 32, 8, 64
NP = E0 // 2
NPS = NP + 1
E1, I1 = 8, 512
HC = I1 // P
NJ = E1 * HC
LN_EPS = 1e-5
KERN_EPS = 1e-6
SCALE = float(HD) ** -0.5
NPART = 3
PAIRS = 6
Q_PART = (0, 0, 1, 1, 0, 2)
K_PART = (0, 1, 0, 1, 2, 0)
PART_OF = (Q_PART, K_PART)
QK_ROWS = PAIRS * HD
MAX_ROW = QK_ROWS
STACK = 64
HALF = H // 2
GQ = D // HD

GATE0, UP0, DOWN0, WR0 = 0, NPS, 2 * NPS, 3 * NPS
NW0 = 3 * NPS + 1
WR1, UP1, DOWN1 = 0, 1, 1 + NJ
NW1 = 2 * NJ + 1
WO = 3
BG, BU, BDS, BR0, B1, B2, BR1 = 0, NPS, 2 * NPS, 2 * NPS + 1, 2 * NPS + 2, 2 * NPS + 2 + NJ, 2 * NPS + 2 + NJ + E1
NBIAS = BR1 + 1
C_ID, C_NEG, C_NEGT, C_SEL0, C_SEL1 = 0, P, 2 * P, 3 * P, 3 * P + NP * P
NCONST = C_SEL1 + E1 * P
C_OSEL = NCONST
NCONST_ALL = C_OSEL + 4 * (HD + 1)

STAGES = ("ffn0", "attn0", "ffn0", "ffn1", "attn1", "ffn1")
FIRST1 = 3
LAG = 3
NH0, NH1 = 5, 4
NHID = 3
NW1_LOADS = 4
LOAD1 = NW1 * P // (NW1_LOADS * NB)
VC = HD + 1
QUAD = 4
NQ = H // QUAD
RING = 6
ONE = 1
ROUND = 16

DOWNS = ("down0", "down1", "down2")
TAIL = {
    ("ffn0", "ffn0"): ((0, "pe", "down0"), (1, "pe", "down1"), (2, "pe", "down2"), (3, "act", "y_out"), (4, "pe", "y_tok"), (5, "dve", "x_up")),
    ("attn0", "ffn0"): ((0, "pe", "down0"), (0, "pe", "down1"), (0, "pe", "down2"), (0, "act", "y_out"), (2, "pe", "y_tok"), (3, "dve", "x_up")),
    ("ffn1", "ffn0"): ((0, "pe", "down0"), (1, "pe", "down1"), (2, "pe", "down2"), (3, "act", "y_out"), (5, "pe", "y_tok"), (6, "dve", "x_up")),
    ("ffn1", "ffn1"): ((0, "pe", "down0"), (1, "pe", "down1"), (2, "pe", "down2"), (3, "dve", "combine"), (5, "pe", "y_tok"), (6, "dve", "x_up")),
    ("attn1", "ffn1"): ((0, "pe", "down0"), (0, "pe", "down1"), (0, "pe", "down2"), (0, "dve", "combine"), (0, "pe", "y_tok"), (0, "dve", "x_up")),
    ("attn0", "attn0"): ((1, "pe", "pv_last"), (2, "act", "o_last"), (3, "pe", "tok_last"), (4, "dve", "norm_last"), (5, "pe", "aT"), (5, "act", "perm"),
                         (12, "act", "aT_hi"), (12, "dve", "aT_lo"), (13, "pe", "proj"), (14, "dve", "res")),
    ("ffn0", "attn0"): ((0, "pe", "pv_last"), (0, "act", "o_last"), (0, "pe", "tok_last"), (0, "dve", "norm_last"), (1, "pe", "aT"), (2, "act", "perm"),
                        (7, "act", "aT_hi"), (7, "dve", "aT_lo"), (8, "pe", "proj"), (9, "dve", "res")),
    ("attn1", "attn1"): ((1, "act", "o_last"), (2, "pe", "tok_last"), (2, "dve", "norm_last"), (3, "pe", "aT"), (3, "act", "aT_hi"),
                         (3, "dve", "aT_lo"), (4, "pe", "proj"), (4, "dve", "y_norm"), (5, "pool", "y_rstd"), (5, "dve", "y_scale"), (6, "pool", "y_add")),
    ("ffn1", "attn1"): ((0, "pe", "pv_last"), (0, "act", "o_last"), (0, "pe", "tok_last"), (0, "dve", "norm_last"), (1, "pe", "aT"), (3, "act", "aT_hi"),
                        (3, "dve", "aT_lo"), (5, "pe", "proj"), (7, "dve", "y_norm"), (8, "pool", "y_rstd"), (10, "dve", "y_scale"), (11, "pool", "y_add")),
}
NORM_STEPS = (("dve", "ln"), ("pool", "rstd"), ("dve", "xn"), ("pe", "turn"), ("act", "hi"), ("dve", "lo"))
ROUTE_STEPS = (("pe", "logits"), ("act", "lgT"), ("pe", "lg"), ("act", "aff"), ("dve", "top_a"), ("act", "exp"), ("dve", "top_b"), ("pe", "wT"), ("act", "wT_out"))
QKV_STEPS = (("pe", "q"), ("act", "q_out"), ("pe", "k"), ("act", "k_out"), ("act", "cut0"), ("pe", "v"), ("act", "v_out"), ("pool", "rest0"),
             ("pe", "vT"), ("act", "v_hi"), ("dve", "v_lo"), ("act", "cut1"), ("pool", "rest1"), ("act", "cut2"))
PREP = {
    "ffn0": ((6, 7, 9, 10, 10, 10), (11, 11, 12, 12, 13, 14, 15, 16, 16), (11, 11, 12, 12, 12, 13, 13, 13, 14, 14, 14, 14, 15, 16)),
    "attn0": ((2, 3, 5, 15, 15, 15), (16, 16, 17, 17, 18, 19, 20, 22, 22), (16, 16, 17, 17, 17, 18, 18, 18, 19, 19, 19, 19, 20, 21)),
    "ffn1": ((9, 10, 12, 14, 14, 15), (17, 17, 19, 19, 20, 24, 25, 29, 29), (17, 17, 19, 19, 20, 21, 21, 21, 23, 23, 24, 24, 25, 27)),
    "attn1": ((3, 4, 8, 9, 9, 9), (10, 10, 11, 11, 12, 13, 13, 14, 14), (10, 10, 11, 11, 11, 12, 12, 11, 13, 13, 13, 12, 12, 14)),
}
W1_AT = (10, 12, 14, 16)
KEEP_AT = 6
PV_LAG = NT + 1
POOL_KB = NT - 1
FILL = range(3, H + 2)
NFILL = 2
MAX_AT = (10, 18)
LOAD = 1024


class Steps:

    def __init__(self, sem, per):
        self.sem, self.per = sem, per

    def begin(self, visit):
        self.base, self.k = visit * self.per, 0

    def mark(self, ins):
        ins.then_inc(self.sem, 1)
        self.k += 1
        return self.base + self.k

    def end(self):
        assert self.k == self.per, (self.k, self.per)


SLOTS = {"ffn0": NPS, "attn0": 2 * H, "ffn1": NJ, "attn1": H}
BIAS_AT = 10


class AttnMemory:

    def __init__(self, which, sb):
        self.q_st = sb(which + "_q_st", [P, H // 2, S], BF16)
        self.k_st = sb(which + "_k_st", [P, H // 2, S], BF16)
        self.qkv = sb(which + "_qkv", [P, 3, S], F32)
        self.res = sb(which + "_res", [P, 2, S], F32)
        self.parts = sb(which + "_parts", [P, 2, NPART, S], BF16)
        self.v_parts = sb(which + "_v_parts", [P, 2, NT * H, 2 * VC], F32R)
        self.rden = sb(which + "_rden", [P, 2, NT * QUAD], F32)
        self.attn = sb(which + "_attn", [P, NT, H, HD], F32)
        self.aT_hi, self.aT_lo = sb(which + "_aT_hi", [P, S], F32R), sb(which + "_aT_lo", [P, S], F32R)
        self.o_sb = sb(which + "_o_sb", [P, 2, S], F32)
        if which == "attn0":
            self.rmax = sb("rmax", [P, NT, H], F32)
            self.nmax = sb("nmax", [P, 2, NT, HALF], F32)
            self.mparts = sb("mparts", [P, NT, NPART, HALF], BF16)
            self.mT = sb("mT", [NPART * HALF, 2, S], BF16)
            self.p_full = sb("p_full", [P, NT, S], F32)
            self.aT_perm = sb("aT_perm", [P, S], F32)


def build(nc, x_in, w0, w1, wa, biases, bd3, rows, consts, out, scratch, mixed):
    nc.disable_value_cache = True
    ctx = ExitStack()
    with ctx:
        def sb(name, shape, dt, stack=ctx):
            return stack.enter_context(nc.sbuf_tensor(name, shape, dt))

        def sem(name):
            return ctx.enter_context(nc.semaphore(name))

        x = sb("x", [P, NB * NT, D], F32)
        wa_hi, wa_lo = sb("wa_hi", [P, 2, 4, P], F32R), sb("wa_lo", [P, 2, 4, P], F32R)
        bias = sb("bias", [P, NBIAS], F32)
        row = sb("row", [P, 4, D], F32)
        ident = sb("ident", [P, P], F32)
        osel = sb("osel", [P, QUAD * VC], F32)
        cbf = sb("cbf", [P, NCONST], BF16)
        bd_parts = sb("bd_parts", [96, NPART, D], BF16)
        xn = sb("xn", [P, NT, D], F32)
        xk = sb("xk", [P, NT, D], F32)
        xnT_hi, xnT_lo = sb("xnT_hi", [P, 2, S], F32R), sb("xnT_lo", [P, 2, S], F32R)
        stats, mv = sb("stats", [P, NT, 6], F32), sb("mv", [P, NT, 2], F32)
        ve, rstd = sb("ve", [P, NT], F32), sb("rstd", [P, NT], F32)
        y_mv = sb("y_mv", [P, NT, 2], F32)
        y_ve, y_rstd = sb("y_ve", [P, NT], F32), sb("y_rstd", [P, NT], F32)
        mhalf = sb("mhalf", [P, NT], F32)
        wT = sb("wT", [96, 2, S], BF16)
        yT = sb("yT", [P, S], F32)
        lgT = sb("lgT", [E0, S], F32)
        aff, sel, wgt = (sb(n, [P, NT, E0], F32) for n in ("aff", "sel", "wgt"))
        m8 = sb("m8", [P, NT, 8], F32)
        i8 = sb("i8", [P, NT, 8], U32)
        i8f = sel[:, :, E1:2 * E1]
        iota8 = sb("iota8", [P, NT, 8], F32)
        den = sb("den", [P, 2, NT], F32)
        wparts = sb("wparts", [P, NT, NPART * E0], BF16)

        with ExitStack() as part:
            mem1 = AttnMemory("attn1", lambda name, shape, dt: sb(name, shape, dt, part))
        w0_hi, w0_lo = sb("w0_hi", [P, NW0, P], F32R), sb("w0_lo", [P, NW0, P], F32R)
        aT_mix = xk.rearrange("p t d -> p (t d)")
        with ExitStack() as part:
            mem0 = AttnMemory("attn0", lambda name, shape, dt: sb(name, shape, dt, part))
        w1_hi, w1_lo = sb("w1_hi", [P, NW1, P], F32R), sb("w1_lo", [P, NW1, P], F32R)

        with ExitStack() as part:
            stage_w = sb("stage_w", [P, 4, LOAD], F32, part)
            stage_c = sb("stage_c", [P, NCONST_ALL], F32, part)
            stage_bd = sb("stage_bd", [96, 2, D], F32, part)
        with ExitStack() as part:
            gate = sb("gate", [P, 2, S], F32, part)
            prod = sb("prod", [P, 2, S], F32, part)
            hid = sb("hid", [P, NHID, S], F32, part)
            h_hi, h_lo = sb("h_hi", [P, NH0, S], F32R, part), sb("h_lo", [P, NH0, S], F32R, part)
            stage_w1 = sb("stage_w1", [P, LOAD1], F32, part)
        rb, zed = gate, prod
        with ExitStack() as part:
            v_pad = sb("v_pad", [P, QUAD, NT, P], F32R, part)
            p_hi, p_lo = sb("p_hi", [P, RING, S], F32R, part), sb("p_lo", [P, RING, S], F32R, part)
            p_copy = sb("p_copy", [P, S], F32, part)

        bank = [ctx.enter_context(nc.psum_tensor(f"bank{i}", [P, S], F32)) for i in range(8)]
        bank6, bank7 = bank[6], bank[7]
        bank6h = bank6[:, :].bitcast(BF16)
        bank7h = bank7[:, :].bitcast(BF16)
        identb = cbf[:, C_ID:C_ID + P]
        neg, negT = cbf[:, C_NEG:C_NEG + P], cbf[:, C_NEGT:C_NEGT + P]

        x_in_sem, small_in = sem("x_in_sem"), sem("small_in")
        w_in = [sem(f"w_in{i}") for i in range(4)]
        w_hi_done, w_lo_done = sem("w_hi_done"), sem("w_lo_done")
        w1_in, w1_hi_done, w1_lo_done = sem("w1_in"), sem("w1_hi_done"), sem("w1_lo_done")
        const_ready, pool_init = sem("const_ready"), sem("pool_init")
        ln_steps = Steps(sem("ln_steps"), 13)
        rstd_ready, xnT_ps, xnT_hi_ready, xnT_lo_ready = map(sem, ("rstd_ready", "xnT_ps", "xnT_hi_ready", "xnT_lo_ready"))
        lgT_ps, lgT_ready, lg_ps, aff_ready, wT_ps, wT_ready = map(sem, (
            "lgT_ps", "lgT_ready", "lg_ps", "aff_ready", "wT_ps", "wT_ready"))
        top0 = Steps(sem("top0_steps"), 18)
        top1 = Steps(sem("top1_steps"), 22)
        mx_ready, e_ready = sem("mask_ready"), sem("exp_ready")
        g_ready, u_ready, wb_ready = sem("g_ready"), sem("u_ready"), sem("wb_ready")
        silu_ready, prod_ready, hid_ready = sem("silu_ready"), sem("prod_ready"), sem("hid_ready")
        hi_ready, lo_ready, h_used = sem("hi_ready"), sem("lo_ready"), sem("h_used")
        y_ps, yT_ready, y_tok = sem("y_ps"), sem("yT_ready"), sem("y_tok")
        x_done = sem("x_done")
        u1_ready, hid1_ready, hi1a_ready, hi1v_ready, lo1p_ready, lo1v_ready, h1_used = map(sem, (
            "u1_ready", "hid1_ready", "hi1a_ready", "hi1v_ready", "lo1p_ready", "lo1v_ready", "h1_used"))
        rb_ps, rb_ready, ze_ready, acc_ready = map(sem, ("rb_ps", "rb_ready", "ze_ready", "acc_ready"))
        qkv_ps, qkv_ready, vT_ps = map(sem, ("qkv_ps", "qkv_ready", "vT_ps"))
        cut_ready, rest_ready = sem("cut_ready"), sem("rest_ready")
        scr_w, st_in = sem("scratch_written"), [sem("stack_in0"), sem("stack_in1")]
        s_ready, s_used, m_steps = sem("s_ready"), sem("s_used"), Steps(sem("m_steps"), 10)
        mT_ps, mT_ready = sem("mT_ps"), sem("mT_ready")
        m_in = [sem("m_in0"), sem("m_in1")]
        st_ready, v_hi_ready, v_lo_ready = sem("st_ready"), sem("v_hi_ready"), sem("v_lo_ready")
        v_pad_ready, pv_used, o_ready, o_tok = map(sem, ("v_pad_ready", "pv_used", "o_ready", "o_tok"))
        p0_full, p0_hi, p0_lo_dve, p0_lo_pool, p1_hi, p1_lo = map(sem, (
            "p0_full", "p0_hi", "p0_lo_dve", "p0_lo_pool", "p1_hi", "p1_lo"))
        p1_copy, p1_lo_pool = sem("p1_copy"), sem("p1_lo_pool")
        rden_ready, attn_ready = sem("rden_ready"), sem("attn_ready")
        aT_ps, aT_hi_ready, aT_lo_ready, o_ps = map(sem, ("aT_ps", "aT_hi_ready", "aT_lo_ready", "o_ps"))
        tail = Steps(sem("tail_steps"), 13)
        y_scaled, kept, x_biased, y_var, y_rstd_ready, eps_added = map(sem, ("y_scaled", "kept", "x_biased", "y_var", "y_rstd_ready", "eps_added"))
        perm_ready, perm_out, mix_in = sem("perm_ready"), sem("perm_out"), sem("mix_in")
        out_sem = sem("out_sem")

        loads = []
        for src, hi, lo, n in ((w0, w0_hi, w0_lo, NW0 * P), (wa, wa_hi, wa_lo, 8 * P)):
            hif = hi.rearrange("p a b -> p (a b)") if len(hi.shape) == 3 else hi.rearrange("p a b c -> p (a b c)")
            lof = lo.rearrange("p a b -> p (a b)") if len(lo.shape) == 3 else lo.rearrange("p a b c -> p (a b c)")
            for a in range(0, n, LOAD):
                b = min(n, a + LOAD)
                loads.append((src[:, a:b], hif[:, a:b], lof[:, a:b], b - a))

        w1_hif, w1_lof = (w.rearrange("p a b -> p (a b)") for w in (w1_hi, w1_lo))
        passed = {}

        class Chunk:

            def __init__(self, s, c):
                self.s, self.c, self.kind = s, c, STAGES[s]
                fixed = isinstance(c, int)
                self.first, self.last = fixed and c == 0, fixed and c == NB - 1
                self.very_first = self.first and s == 0
                self.causal = self.kind == "attn0"
                self.layer = 0 if self.causal else 1
                self.mem = {"attn0": mem0, "attn1": mem1}.get(self.kind)
                self.next_kind = STAGES[s + 1] if s + 1 < len(STAGES) else ""
                self.g_positive = not (self.first and STAGES[:s].count(self.kind) == 0)

            def stages_before(self, kind):
                return sum(a[:len(kind)] == kind for a in STAGES[:self.s])

            @property
            def G(self):
                return self.s * NB + self.c

            @property
            def g(self):
                return self.stages_before(self.kind) * NB + self.c

            @property
            def gf(self):
                return self.stages_before("ffn") * NB + (self.c if self.kind[:3] == "ffn" else 0)

            @property
            def ga(self):
                return self.stages_before("attn") * NB + self.c

            @property
            def parity(self):
                return self.c % 2

            def before(self):
                if self.first:
                    return Chunk(self.s - 1, NB - 1) if self.s else None
                return Chunk(self.s, self.c - 1)

            def after(self):
                if self.last:
                    return Chunk(self.s + 1, 0) if self.s + 1 < len(STAGES) else None
                return Chunk(self.s, self.c + 1)

        def settle(eng):
            if eng.engine not in passed:
                passed[eng.engine] = sem(f"passed{len(passed)}")
            eng.sem_inc(passed[eng.engine], 1)

        def products(eng, o, w_hi_, w_lo_, v_hi, v_lo, start=True, stop=True, **kw):
            eng.matmul(o, w_hi_, v_hi, start=start, stop=False, **kw)
            eng.matmul(o, w_hi_, v_lo, start=False, stop=False, **kw)
            return eng.matmul(o, w_lo_, v_hi, start=False, stop=stop, **kw)

        def reader(i, ring, n):
            if i >= ring:
                return i - ring + 1
            return max(r for r in range(n) if r % ring == i) + 1 - n

        def slot_steps(table, who, slot):
            return [step for at, engine, step in table if engine == who and at == slot]

        def prep_table(body_kind, kind):
            norm, route, qkv_at = PREP[body_kind]
            return ([(at, *step) for at, step in zip(norm, NORM_STEPS)]
                    + [(at, *step) for at, step in (zip(route, ROUTE_STEPS) if kind[:3] == "ffn" else zip(qkv_at, QKV_STEPS))])

        def run(eng, who, prep, tail_, main, between=None):
            def body(s, c):
                ch = Chunk(s, c)
                before, after = ch.before(), ch.after()
                for slot in range(SLOTS[ch.kind]):
                    if before is not None:
                        for step in slot_steps(TAIL[ch.kind, before.kind], who, slot):
                            tail_(eng, step, before)
                    if after is not None:
                        for step in slot_steps(prep_table(ch.kind, after.kind), who, slot):
                            prep(eng, step, after)
                    main(eng, ch, slot)

            for _, engine, step in prep_table("ffn0", STAGES[0]):
                if engine == who:
                    prep(eng, step, Chunk(0, 0))
            for s in range(len(STAGES)):
                body(s, 0)
                if between is not None:
                    between(s)
                with eng.Fori(1, NB - 1) as c:
                    body(s, c)
                body(s, NB - 1)
            ch = Chunk(len(STAGES) - 1, NB - 1)
            for _, engine, step in TAIL[ch.kind, ch.kind]:
                if engine == who:
                    tail_(eng, step, ch)

        def v_part(ch, i):
            return ch.mem.v_parts[:, ch.parity, :, i * VC:i * VC + HD]

        def xs_of(ch):
            return x[:, bass.ds(ch.c * NT, NT), :]

        def row_of(i):
            return row[:, i, :].unsqueeze(1).broadcast_to([P, NT, D])

        def heads_of(ap):
            return ap.rearrange("p (n d) -> p n d", d=HD)

        def pe_prep(eng, step, ch):
            w_hi_, w_lo_, blk, ne = (w0_hi, w0_lo, WR0, E0) if ch.kind == "ffn0" else (w1_hi, w1_lo, WR1, E1)
            if step == "turn":
                eng.wait_ge(ln_steps.sem, ch.G * 13 + 13)
                if not ch.very_first:
                    eng.wait_ge(x_done, ONE + ch.G - 1)
                for t in range(NT):
                    ins = eng.transpose(bank7[:, t * P:(t + 1) * P], xn[:, t, :], ident[:, :])
                ins.then_inc(xnT_ps, 1)
            if step == "logits":
                eng.wait_ge(xnT_lo_ready, ch.G + 1)
                if ch.s == FIRST1 and ch.first:
                    eng.wait_ge(w1_lo_done, ONE + 1)
                products(eng, bank7[:, :], w_hi_[:, blk, :], w_lo_[:, blk, :],
                         xnT_hi[:, ch.parity, :], xnT_lo[:, ch.parity, :]).then_inc(lgT_ps, 1)
            if step == "lg":
                eng.wait_ge(lgT_ready, ch.gf + 1)
                settle(eng)
                for t in range(NT):
                    ins = eng.transpose(bank7[:, t * ne:(t + 1) * ne], lgT[0:ne, t * P:(t + 1) * P], ident[0:ne, 0:ne])
                ins.then_inc(lg_ps, 1)
            if step == "wT":
                st = top0 if ch.kind == "ffn0" else top1
                eng.wait_ge(st.sem, ch.g * st.per + st.per)
                for t in range(NT):
                    ins = eng.transpose(bank7h[0:NPART * ne, t * P:(t + 1) * P], wparts[:, t, 0:NPART * ne], identb)
                ins.then_inc(wT_ps, 1)
            if step in ("q", "k", "v"):
                i = "qkv".index(step)
                if i == 0:
                    eng.wait_ge(xnT_lo_ready, ch.G + 1)
                else:
                    eng.wait_ge(qkv_ready, 3 * ch.ga + i)
                products(eng, bank7[:, :], wa_hi[:, ch.layer, i, :], wa_lo[:, ch.layer, i, :],
                         xnT_hi[:, ch.parity, :], xnT_lo[:, ch.parity, :]).then_inc(qkv_ps, 1)
            if step == "vT":
                eng.wait_ge(qkv_ready, 3 * ch.ga + 3)
                for t in range(NT):
                    ins = eng.transpose(bank7[:, t * P:(t + 1) * P], ch.mem.qkv[:, 2, t * P:(t + 1) * P], ident[:, :])
                ins.then_inc(vT_ps, 1)

        def down0(eng, ch, p):
            eng.wait_ge(hi_ready, ch.g * NPS + p + 1)
            eng.wait_ge(lo_ready, ROUND + ch.g * NPS + p + 1)
            if p == 0 and ch.g_positive:
                eng.wait_ge(yT_ready, ch.g)
            products(eng, bank[5][:, :], w0_hi[:, DOWN0 + p, :], w0_lo[:, DOWN0 + p, :],
                     h_hi[:, p % NH0, :], h_lo[:, p % NH0, :], start=(p == 0), stop=False).then_inc(h_used, 1)
            if p == NPS - 1:
                for j in range(NPART):
                    ins = eng.matmul(bank[5][:, :], bd_parts[:, j, :], wT[:, ch.parity, :], start=False, stop=(j == NPART - 1))
                ins.then_inc(y_ps, 1)

        def down1(eng, ch, j):
            e = j // HC
            if j % 2 == 0:
                eng.wait_ge(lo1p_ready, ROUND + ch.g * (NJ // 2) + j // 2 + 1)
            else:
                eng.wait_ge(lo1v_ready, ROUND + ch.g * (NJ // 2) + j // 2 + 1)
            if j % HC == 0:
                eng.wait_ge(ze_ready, ROUND + ch.g * E1 + reader(e, 2, E1))
                if j == 0 and ch.s == FIRST1 and ch.first:
                    eng.wait_ge(yT_ready, ch.gf)
            ybank = bank[5 if e % 2 == 0 else 3]
            products(eng, ybank[:, :], w1_hi[:, DOWN1 + j, :], w1_lo[:, DOWN1 + j, :], h_hi[:, j % NH1, :], h_lo[:, j % NH1, :],
                     start=(j % HC == 0), stop=(j % HC == HC - 1)).then_inc(h1_used, 1)

        def pv(eng, ch, h, kb):
            i = h * NT + kb
            quad, j = h // QUAD, h % QUAD
            slot, q0 = i % RING, (kb * P if ch.causal else 0)
            if kb == 0:
                eng.wait_ge(v_pad_ready, ch.ga * H + h + 1)
            if j == 0 and kb == 0 and quad >= 2:
                eng.wait_ge(o_ready, NQ * ch.ga + quad - 1)
            if not ch.causal and kb == POOL_KB:
                eng.wait_ge(p1_lo_pool, ROUND + ch.g * H + h + 1)
            elif not ch.causal:
                eng.wait_ge(p1_lo, (ch.g * H + h) * (NT - 1) + kb + 1)
            elif kb % 2 == 0:
                eng.wait_ge(p0_lo_dve, ROUND + (ch.g * H + h) * 2 + kb // 2 + 1)
            else:
                eng.wait_ge(p0_lo_pool, ROUND + (ch.g * H + h) * 2 + kb // 2 + 1)
            o = bank[5 + quad % 2][:, q0:S]
            eng.matmul(o, v_pad[:, j, kb, :], p_hi[:, slot, 0:S - q0], start=(j == 0 and kb == 0), stop=False, skip_group_check=True)
            eng.matmul(o, v_pad[:, j, kb, :], p_lo[:, slot, 0:S - q0], start=False, stop=(j == QUAD - 1 and kb == NT - 1),
                       skip_group_check=True).then_inc(pv_used, 1)

        def to_tokens(eng, ch, quad):
            eng.wait_ge(o_ready, NQ * ch.ga + quad + 1)
            if quad:
                eng.wait_ge(attn_ready, NQ * ch.ga + quad)
            for qt in range(NT):
                at = qt * QUAD * VC
                ins = eng.matmul(bank[4][:, at:at + QUAD * VC], ch.mem.o_sb[:, quad % 2, qt * P:(qt + 1) * P], osel[:, :],
                                 start=True, stop=True)
            ins.then_inc(o_tok, 1)

        def pe_tail(eng, step, ch):
            mem = ch.mem
            if step in DOWNS:
                if ch.kind == "ffn0":
                    down0(eng, ch, NPS - LAG + DOWNS.index(step))
                else:
                    down1(eng, ch, NJ - LAG + DOWNS.index(step))
            if step == "y_tok":
                if ch.kind == "ffn0":
                    eng.wait_ge(yT_ready, ch.g + 1)
                else:
                    eng.wait_ge(acc_ready, ROUND + ch.g * E1 + E1)
                eng.wait_ge(x_done, ONE + ch.G)
                for t in range(NT):
                    ins = eng.transpose(bank6[:, t * P:(t + 1) * P], yT[:, t * P:(t + 1) * P], ident[:, :])
                ins.then_inc(y_tok, 1)
            if step == "pv_last":
                for tile in range(H * NT - PV_LAG, H * NT):
                    pv(eng, ch, tile // NT, tile % NT)
            if step == "tok_last":
                to_tokens(eng, ch, NQ - 1)
            if step == "aT":
                eng.wait_ge(attn_ready, NQ * ch.ga + NQ)
                if ch.last and ch.next_kind[:3] == "ffn":
                    eng.wait_ge(wT_ready, ch.gf + 1)
                for t in range(NT):
                    ins = eng.transpose(bank7[:, t * P:(t + 1) * P], mem.attn[:, t, :, :].rearrange("p h d -> p (h d)"), ident[:, :])
                ins.then_inc(aT_ps, 1)
            if step == "proj":
                eng.wait_ge(aT_lo_ready, ch.ga + 1)
                for t in range(NT):
                    ts = slice(t * P, (t + 1) * P)
                    ins = products(eng, bank7[:, ts], mem.aT_hi[:, ts], mem.aT_lo[:, ts],
                                   wa_hi[:, ch.layer, WO, :], wa_lo[:, ch.layer, WO, :])
                ins.then_inc(o_ps, 1)

        def pe_ffn0(eng, ch, p):
            base = ROUND + ch.g * NPS
            eng.wait_ge(silu_ready, base + reader(p, 2, NPS))
            xh, xl = xnT_hi[:, ch.parity, :], xnT_lo[:, ch.parity, :]
            products(eng, bank[p % 2][:, :], w0_hi[:, GATE0 + p, :], w0_lo[:, GATE0 + p, :], xh, xl).then_inc(g_ready, 1)
            if p:
                weight(eng, ch, p - 1)
            eng.wait_ge(prod_ready, ROUND + ch.g * NPS + reader(p, 2, NPS))
            products(eng, bank[2 + p % 2][:, :], w0_hi[:, UP0 + p, :], w0_lo[:, UP0 + p, :],
                     xnT_hi[:, ch.parity, :], xnT_lo[:, ch.parity, :]).then_inc(u_ready, 1)
            if p >= LAG:
                down0(eng, ch, p - LAG)

        def weight(eng, ch, p):
            if p == 0:
                eng.wait_ge(wT_ready, ch.gf + 1)
            eng.wait_ge(hid_ready, ROUND + ch.g * NPS + (p if p else -1))
            eng.matmul(bank[4][:, :], cbf[0:NPART * E0, C_SEL0 + p * P:C_SEL0 + (p + 1) * P], wT[:, ch.parity, :],
                       start=True, stop=True).then_inc(wb_ready, 1)

        def pe_ffn1(eng, ch, j):
            if j == 0 and ch.s == FIRST1 and ch.first:
                eng.wait_ge(w1_lo_done, ONE + NW1_LOADS * NB)
                eng.wait_ge(silu_ready, ROUND + ch.gf * NPS)
                eng.wait_ge(prod_ready, ROUND + ch.gf * NPS)
                eng.wait_ge(hid_ready, ROUND + ch.gf * NPS)
            eng.wait_ge(hid1_ready, ROUND + ch.g * NJ + reader(j, 3, NJ))
            products(eng, bank[j % 3][:, :], w1_hi[:, UP1 + j, :], w1_lo[:, UP1 + j, :],
                     xnT_hi[:, ch.parity, :], xnT_lo[:, ch.parity, :]).then_inc(u1_ready, 1)
            if j % HC == 1:
                e = j // HC
                if e == 0:
                    eng.wait_ge(wT_ready, ch.gf + 1)
                eng.wait_ge(rb_ready, ROUND + ch.g * E1 + e)
                eng.matmul(bank[4][:, :], cbf[0:NPART * E1, C_SEL1 + e * P:C_SEL1 + (e + 1) * P],
                           wT[0:NPART * E1, ch.parity, :], start=True, stop=True).then_inc(rb_ps, 1)
            if j >= LAG:
                down1(eng, ch, j - LAG)

        def pe_attn(eng, ch, slot):
            mem = ch.mem

            def head(st, h, rows):
                p0 = (h % 2) * STACK
                return st[p0:p0 + rows, h // 2, :]

            if ch.causal and slot in MAX_AT:
                half = MAX_AT.index(slot)
                eng.wait_ge(m_steps.sem, ch.g * 10 + 5 * half + 5)
                if half:
                    eng.wait_ge(mT_ready, 2 * ch.g + 1)
                for t in range(NT):
                    ins = eng.transpose(bank6h[0:NPART * HALF, t * P:(t + 1) * P],
                                        mem.mparts[:, t, :, :].rearrange("p a b -> p (a b)"), identb)
                ins.then_inc(mT_ps, 1)
            if ch.causal and slot < H:
                h = slot
                if h % HALF == 0:
                    eng.wait_ge(st_in[h // HALF], 64 * (ch.ga + 1))
                if h == 0 and ch.first:
                    eng.wait_ge(silu_ready, ROUND + ch.gf * NPS)
                    eng.wait_ge(prod_ready, ROUND + ch.gf * NPS)
                elif h == 0:
                    eng.wait_ge(p0_full, ch.g * H * NT)
                qs, ks = head(mem.q_st, h, QK_ROWS), head(mem.k_st, h, QK_ROWS)
                for qt in range(NT):
                    if h:
                        eng.wait_ge(s_used, ch.g * H * NT + (h - 1) * NT + qt + 1)
                    eng.matmul(bank[qt][:, 0:(qt + 1) * P], qs[:, qt * P:(qt + 1) * P], ks[:, 0:(qt + 1) * P],
                               start=True, stop=True)
                    eng.matmul(bank[qt][:, qt * P:(qt + 1) * P], identb, neg, start=False, stop=True,
                               skip_group_check=True).then_inc(s_ready, 1)
                if slot in FILL:
                    for _ in range(NFILL):
                        eng.matmul(bank[5][:, :], identb, cbf[:, 0:S], start=True, stop=True)
                return
            h = slot - (H if ch.causal else 0)
            if h >= QUAD and h % QUAD == 2:
                to_tokens(eng, ch, h // QUAD - 1)
            if h % HALF == 0:
                if ch.causal:
                    eng.wait_ge(m_in[h // HALF], 96 * (ch.g + 1))
                else:
                    eng.wait_ge(st_in[h // HALF], 64 * (ch.ga + 1))
            rows_ = QK_ROWS + NPART if ch.causal else QK_ROWS
            qs, ks = head(mem.q_st, h, rows_), head(mem.k_st, h, rows_)
            for kb in range(NT):
                q0 = kb * P if ch.causal else 0
                if ch.causal and h:
                    eng.wait_ge(p0_full, ch.g * H * NT + (h - 1) * NT + kb + 1)
                elif ch.causal:
                    eng.wait_ge(s_used, (ch.g + 1) * H * NT)
                elif h == 0 and ch.first:
                    eng.wait_ge(ze_ready, ROUND + ch.stages_before("ffn1") * NB * E1)
                elif kb == POOL_KB:
                    eng.wait_ge(p1_copy, ch.g * H + h)
                else:
                    eng.wait_ge(p1_lo, (ch.g * H + h - 1) * (NT - 1) + kb + 1)
                ins = eng.matmul(bank[kb][:, 0:S - q0], ks[:, kb * P:(kb + 1) * P], qs[:, q0:S], start=True, stop=True)
                if ch.causal:
                    ins = eng.matmul(bank[kb][:, 0:P], identb, negT, start=False, stop=True, skip_group_check=True)
                ins.then_inc(st_ready, 1)
                tile = h * NT + kb - PV_LAG
                if tile >= 0:
                    pv(eng, ch, tile // NT, tile % NT)
                elif not ch.causal and not ch.first:
                    tile += H * NT
                    pv(eng, ch.before(), tile // NT, tile % NT)

        def act_prep(eng, step, ch):
            ne, br = (E0, BR0) if ch.kind == "ffn0" else (E1, BR1)
            if step == "hi":
                eng.wait_ge(xnT_ps, ONE + ch.G + 1)
                eng.activation(xnT_hi[:, ch.parity, :], bank7[:, :], ACT.Copy).then_inc(xnT_hi_ready, 1)
            if step == "lgT":
                eng.wait_ge(lgT_ps, ch.gf + 1)
                eng.activation(lgT[0:ne, :], bank7[0:ne, :], ACT.Identity, bias=bias[0:ne, br:br + 1]).then_inc(lgT_ready, 1)
            if step == "aff":
                eng.wait_ge(lg_ps, ch.gf + 1)
                src = bank7[:, 0:NT * ne].rearrange("p (t e) -> p t e", e=ne)
                eng.activation(aff[:, :, 0:ne], src, ACT.Sigmoid if ch.kind == "ffn0" else ACT.Copy).then_inc(aff_ready, 1)
            if step == "exp" and ch.kind == "ffn1":
                eng.wait_ge(mx_ready, ch.g + 1)
                eng.activation(wgt[:, :, 0:E1], sel[:, :, 0:E1], ACT.Exp).then_inc(e_ready, 1)
            if step == "wT_out":
                eng.wait_ge(wT_ps, ch.gf + 1)
                eng.activation(wT[0:NPART * ne, ch.parity, :], bank7h[0:NPART * ne, 0:S], ACT.Copy).then_inc(wT_ready, 1)
            if step in ("q_out", "k_out", "v_out"):
                i = "qkv".index(step[0])
                eng.wait_ge(qkv_ps, 3 * ch.ga + i + 1)
                eng.activation(ch.mem.qkv[:, i, :], bank7[:, :], ACT.Copy, scale=SCALE if i == 0 else 1.0).then_inc(qkv_ready, 1)
            if step == "v_hi":
                eng.wait_ge(vT_ps, ch.ga + 1)
                eng.activation(v_part(ch, 0), heads_of(bank7[:, :]), ACT.Copy).then_inc(v_hi_ready, 1)
            if step in ("cut0", "cut1", "cut2"):
                n = int(step[3])
                for i in range(2):
                    if n == 0:
                        eng.wait_ge(qkv_ready, 3 * ch.ga + 2)
                    else:
                        eng.wait_ge(rest_ready, 4 * ch.ga + 2 * (n - 1) + i + 1)
                    src = ch.mem.qkv[:, i, :] if n == 0 else ch.mem.res[:, i, :]
                    eng.activation(ch.mem.parts[:, i, n, :], src, ACT.Copy).then_inc(cut_ready, 1)

        def take_outputs(eng, ch, quad):
            eng.wait_ge(pv_used, ROUND + (ch.ga * H + (quad + 1) * QUAD) * NT)
            eng.activation(ch.mem.o_sb[:, quad % 2, :], bank[5 + quad % 2][:, :], ACT.Copy).then_inc(o_ready, 1)

        def act_tail(eng, step, ch):
            mem = ch.mem
            if step == "y_out":
                eng.wait_ge(y_ps, ch.g + 1)
                eng.activation(yT[:, :], bank[5][:, :], ACT.Identity, bias=bias[:, BDS:BDS + 1]).then_inc(yT_ready, 1)
            if step == "o_last":
                take_outputs(eng, ch, NQ - 1)
            if step == "perm":
                eng.wait_ge(aT_ps, ONE + ch.ga + 1)
                eng.activation(mem.aT_perm[:, :].rearrange("p (q r) -> p r q", q=GQ),
                               bank7[:, :].rearrange("p (r q) -> p r q", q=GQ), ACT.Copy).then_inc(perm_ready, 1)
            if step == "aT_hi":
                if ch.causal:
                    eng.wait_ge(mix_in, 16 * (ch.g + 1))
                else:
                    eng.wait_ge(aT_ps, ONE + ch.ga + 1)
                eng.activation(mem.aT_hi[:, :], aT_mix[:, :] if ch.causal else bank7[:, :], ACT.Copy).then_inc(aT_hi_ready, 1)

        def act_ffn0(eng, ch, p):
            def hi_part(q):
                eng.wait_ge(hid_ready, ROUND + ch.g * NPS + q + 1)
                eng.wait_ge(h_used, ROUND + ch.g * NPS + reader(q, NH0, NPS))
                eng.activation(h_hi[:, q % NH0, :], hid[:, q % NHID, :], ACT.Copy).then_inc(hi_ready, 1)

            eng.wait_ge(g_ready, ch.g * NPS + p + 1)
            eng.wait_ge(prod_ready, ROUND + ch.g * NPS + reader(p, 2, NPS))
            eng.activation(gate[:, p % 2, :], bank[p % 2][:, :], ACT.Silu, bias=bias[:, BG + p:BG + p + 1]).then_inc(silu_ready, 1)
            if p >= 1:
                hi_part(p - 1)
            if ch.s == FIRST1 - 1 and p in W1_AT:
                i = W1_AT.index(p)
                eng.wait_ge(w1_in, 16 * (NW1_LOADS * ch.c + i + 1))
                eng.activation(w1_hif[:, bass.ds((NW1_LOADS * ch.c + i) * LOAD1, LOAD1)], stage_w1[:, :], ACT.Copy).then_inc(w1_hi_done, 1)
            if p == NPS - 1:
                hi_part(p)

        def act_ffn1(eng, ch, j):
            if j == 0 and ch.s == FIRST1 and ch.first:
                eng.wait_ge(lo_ready, ROUND + ch.gf * NPS)
                eng.wait_ge(h_used, ROUND + ch.gf * NPS - LAG)
            if j % HC == 2:
                e = j // HC
                eng.wait_ge(rb_ps, ch.g * E1 + e + 1)
                eng.wait_ge(ze_ready, ROUND + ch.g * E1 + reader(e, 2, E1))
                eng.activation(rb[:, e % 2, :], bank[4][:, :], ACT.Copy).then_inc(rb_ready, 1)
            eng.wait_ge(u1_ready, ch.g * NJ + j + 1)
            q = reader(j, NHID, NJ) - 1
            if q % 2 == 0:
                eng.wait_ge(lo1p_ready, ROUND + ch.g * (NJ // 2) + q // 2 + 1)
            else:
                eng.wait_ge(lo1v_ready, ROUND + ch.g * (NJ // 2) + q // 2 + 1)
            eng.activation(hid[:, j % NHID, :], bank[j % 3][:, :], ACT.Relu, bias=bias[:, B1 + j:B1 + j + 1]).then_inc(hid1_ready, 1)
            if j % 2 == 0:
                if j == 0 and ch.s == FIRST1 and ch.first:
                    eng.wait_ge(h_used, ROUND + ch.gf * NPS)
                eng.wait_ge(hid1_ready, ROUND + ch.g * NJ + j + 1)
                eng.wait_ge(h1_used, ROUND + ch.g * NJ + reader(j, NH1, NJ))
                eng.activation(h_hi[:, j % NH1, :], hid[:, j % NHID, :], ACT.Copy).then_inc(hi1a_ready, 1)

        def act_attn(eng, ch, slot):
            if ch.causal and slot in MAX_AT:
                half = MAX_AT.index(slot)
                eng.wait_ge(mT_ps, ONE + 2 * ch.g + half + 1)
                eng.activation(ch.mem.mT[:, half, :], bank6h[0:NPART * HALF, 0:S], ACT.Copy).then_inc(mT_ready, 1)
            if ch.causal and slot < H:
                return
            h = slot - (H if ch.causal else 0)
            if h == 0 and ch.first:
                eng.wait_ge(x_done, ONE + ch.s * NB)
            if h >= QUAD and h % QUAD == 1:
                take_outputs(eng, ch, h // QUAD - 1)
            for kb in range(NT):
                i = h * NT + kb
                eng.wait_ge(st_ready, ch.ga * H * NT + i + 1)
                if ch.causal:
                    eng.wait_ge(p0_lo_pool if kb % 2 else p0_lo_dve, ROUND + (ch.g * H + h - 1) * 2 + kb // 2 + 1)
                    eng.activation(mem0.p_full[:, kb, 0:S - kb * P], bank[kb][:, 0:S - kb * P], ACT.Exp).then_inc(p0_full, 1)
                else:
                    eng.wait_ge(pv_used, ROUND + ch.ga * H * NT + reader(i, RING, H * NT))
                    eng.activation(p_hi[:, i % RING, :], bank[kb][:, :], ACT.Relu).then_inc(p1_hi, 1)
                    if kb == POOL_KB:
                        eng.wait_ge(p1_lo_pool, ROUND + ch.g * H + h)
                        eng.activation(p_copy[:, :], bank[kb][:, :], ACT.Relu).then_inc(p1_copy, 1)

        def dve_prep(eng, step, ch):
            if step == "ln":
                st = ln_steps
                st.begin(ch.G)
                if ch.s:
                    eng.wait_ge(x_done, ONE + ch.G - NB + 1)
                for t in range(NT):
                    v = st.mark(eng.bn_stats(stats[:, t, :], xs_of(ch)[:, t, :]))
                eng.wait_ge(st.sem, v)
                settle(eng)
                for t in range(NT):
                    v = st.mark(eng.bn_aggr(mv[:, t, :], stats[:, t, :]))
                eng.wait_ge(st.sem, v)
                st.mark(eng.tensor_scalar(ve[:, :], mv[:, :, 1], LN_EPS, None, ALU.add))
            if step == "xn":
                st = ln_steps
                eng.wait_ge(rstd_ready, ch.G + 1)
                eng.wait_ge(xnT_ps, ONE + ch.G)
                before = ch.before()
                if before is not None and before.kind == "attn1":
                    eng.wait_ge(kept, before.g + 1)
                for t in range(NT):
                    st.mark(eng.tensor_scalar(xn[:, t, :], xs_of(ch)[:, t, :], mv[:, t, 0:1], rstd[:, t:t + 1],
                                              ALU.subtract, ALU.mult))
                st.end()
            if step == "lo":
                eng.wait_ge(xnT_hi_ready, ch.G + 1)
                eng.tensor_tensor(xnT_lo[:, ch.parity, :], bank7[:, :], xnT_hi[:, ch.parity, :].bitcast(F32),
                                  ALU.subtract).then_inc(xnT_lo_ready, 1)
            if step == "top_a":
                if ch.kind == "ffn0":
                    top0_a(eng, ch)
                else:
                    top1_a(eng, ch)
            if step == "top_b":
                if ch.kind == "ffn0":
                    top0_b(eng, ch)
                else:
                    top1_b(eng, ch)
            if step == "v_lo":
                eng.wait_ge(v_hi_ready, ch.ga + 1)
                eng.tensor_tensor(v_part(ch, 1), heads_of(bank7[:, :]), v_part(ch, 0).bitcast(F32), ALU.subtract).then_inc(v_lo_ready, 1)

        def top0_a(eng, ch):
            st = top0
            st.begin(ch.g)
            eng.wait_ge(aff_ready, ch.gf + 1)
            settle(eng)
            for t in range(NT):
                v = st.mark(eng.max(m8[:, t, :], aff[:, t, :]))
            eng.wait_ge(st.sem, v)
            settle(eng)
            for t in range(NT):
                st.mark(eng.match_replace(sel[:, t, :], m8[:, t, :], aff[:, t, :], -1.0))
            v = st.mark(eng.tensor_reduce(den[:, 0, :], m8[:, :, :], AX_X, ALU.add))
            eng.wait_ge(st.sem, v)
            v = st.mark(eng.tensor_scalar(den[:, 0, :], den[:, 0, :], 1e-9, None, ALU.add))
            eng.wait_ge(st.sem, v)
            st.mark(eng.reciprocal(den[:, 1, :], den[:, 0, :]))

        def top0_b(eng, ch):
            st = top0
            v = st.mark(eng.tensor_tensor(sel[:, :, :], sel[:, :, :], aff[:, :, :], ALU.not_equal))
            eng.wait_ge(st.sem, v)
            v = st.mark(eng.tensor_tensor(aff[:, :, :], aff[:, :, :], den[:, 1, :].unsqueeze(2).broadcast_to([P, NT, E0]), ALU.mult))
            eng.wait_ge(st.sem, v)
            v = st.mark(eng.tensor_tensor(wgt[:, :, :], aff[:, :, :], sel[:, :, :], ALU.mult))
            eng.wait_ge(st.sem, v)
            weight_parts(eng, st, E0)
            st.end()

        def weight_parts(eng, st, ne):
            v = st.mark(eng.tensor_copy(wparts[:, :, 0:ne], wgt[:, :, 0:ne]))
            eng.wait_ge(st.sem, v)
            v = st.mark(eng.tensor_tensor(sel[:, :, 0:ne], wgt[:, :, 0:ne], wparts[:, :, 0:ne], ALU.subtract))
            eng.wait_ge(st.sem, v)
            v = st.mark(eng.tensor_copy(wparts[:, :, ne:2 * ne], sel[:, :, 0:ne]))
            eng.wait_ge(st.sem, v)
            st.mark(eng.tensor_tensor(wparts[:, :, 2 * ne:3 * ne], sel[:, :, 0:ne], wparts[:, :, ne:2 * ne], ALU.subtract))

        def over_experts(ap):
            return ap.broadcast_to([P, NT, E1])

        def top1_a(eng, ch):
            st = top1
            st.begin(ch.g)
            r, w, bc = sel[:, :, 0:E1], wgt[:, :, 0:E1], over_experts
            eng.wait_ge(aff_ready, ch.gf + 1)
            settle(eng)
            for t in range(NT):
                v = st.mark(eng.max(m8[:, t, :], aff[:, t, 0:E1]))
            eng.wait_ge(st.sem, v)
            settle(eng)
            for t in range(NT):
                v = st.mark(eng.max_index(i8[:, t, :], m8[:, t, :], aff[:, t, 0:E1]))
            eng.wait_ge(st.sem, v)
            v = st.mark(eng.tensor_copy(i8f[:, :, :], i8[:, :, :]))
            eng.wait_ge(st.sem, v)
            v = st.mark(eng.tensor_tensor(r, iota8[:, :, :], bc(i8f[:, :, 0:1]), ALU.is_equal))
            v = st.mark(eng.tensor_tensor(w, iota8[:, :, :], bc(i8f[:, :, 1:2]), ALU.is_equal))
            eng.wait_ge(st.sem, v)
            v = st.mark(eng.tensor_tensor(r, r, bc(m8[:, :, 0:1]), ALU.mult))
            v = st.mark(eng.tensor_tensor(w, w, bc(m8[:, :, 1:2]), ALU.mult))
            eng.wait_ge(st.sem, v)
            v = st.mark(eng.tensor_tensor(r, r, w, ALU.add))
            eng.wait_ge(st.sem, v)
            v = st.mark(eng.tensor_scalar(den[:, 0, :], m8[:, :, 0], 0.0, None, ALU.max))
            eng.wait_ge(st.sem, v)
            eng.tensor_tensor(r, r, bc(den[:, 0, :].unsqueeze(2)), ALU.subtract).then_inc(mx_ready, 1)

        def top1_b(eng, ch):
            st = top1
            w = wgt[:, :, 0:E1]
            eng.wait_ge(e_ready, ch.g + 1)
            v = st.mark(eng.tensor_reduce(den[:, 0, :], w, AX_X, ALU.add))
            eng.wait_ge(st.sem, v)
            v = st.mark(eng.reciprocal(den[:, 1, :], den[:, 0, :]))
            eng.wait_ge(st.sem, v)
            v = st.mark(eng.tensor_tensor(w, w, over_experts(den[:, 1, :].unsqueeze(2)), ALU.mult))
            eng.wait_ge(st.sem, v)
            weight_parts(eng, st, E1)
            st.end()

        def combine(eng, ch, e):
            n = ch.g * E1 + e
            eng.wait_ge(h1_used, ROUND + (ch.g * E1 + e + 1) * HC)
            eng.wait_ge(rb_ready, ROUND + ch.g * E1 + e + 1)
            eng.wait_ge(acc_ready, ROUND + ch.g * E1 + e)
            ybank = bank[5 if e % 2 == 0 else 3]
            dst = yT[:, :] if e == 0 else zed[:, e % 2, :]
            if e == 0:
                eng.wait_ge(y_tok, ch.gf)
            settle(eng)
            eng.scalar_tensor_tensor(dst, ybank[:, :], bias[:, B2 + e:B2 + e + 1], rb[:, e % 2, :],
                                     ALU.add, ALU.mult).then_inc(ze_ready, 1)
            eng.wait_ge(ze_ready, ROUND + ch.g * E1 + e + 1)
            if e == 0:
                eng.sem_inc(acc_ready, 1)
            else:
                eng.tensor_tensor(yT[:, :], yT[:, :], dst, ALU.add).then_inc(acc_ready, 1)

        def dve_ffn0(eng, ch, p):
            if ch.s == FIRST1 - 1 and p in W1_AT:
                i = W1_AT.index(p)
                cols = bass.ds((NW1_LOADS * ch.c + i) * LOAD1, LOAD1)
                eng.wait_ge(w1_hi_done, NW1_LOADS * ch.c + i + 1)
                eng.tensor_tensor(w1_lof[:, cols], stage_w1[:, :], w1_hif[:, cols].bitcast(F32), ALU.subtract).then_inc(w1_lo_done, 1)
            eng.wait_ge(silu_ready, ROUND + ch.g * NPS + p + 1)
            eng.wait_ge(u_ready, ch.g * NPS + p + 1)
            eng.wait_ge(hid_ready, ROUND + ch.g * NPS + reader(p, 2, NPS))
            settle(eng)
            eng.scalar_tensor_tensor(prod[:, p % 2, :], bank[2 + p % 2][:, :], bias[:, BU + p:BU + p + 1],
                                     gate[:, p % 2, :], ALU.add, ALU.mult).then_inc(prod_ready, 1)
            eng.wait_ge(prod_ready, ROUND + ch.g * NPS + p + 1)
            eng.wait_ge(lo_ready, ROUND + ch.g * NPS + reader(p, NHID, NPS))
            if p < NP:
                eng.wait_ge(wb_ready, ch.g * NP + p + 1)
                eng.tensor_tensor(hid[:, p % NHID, :], bank[4][:, :], prod[:, p % 2, :], ALU.mult).then_inc(hid_ready, 1)
            else:
                eng.tensor_copy(hid[:, p % NHID, :], prod[:, p % 2, :]).then_inc(hid_ready, 1)

        def dve_ffn1(eng, ch, j):
            if j % 2 == 1:
                if j == 1 and ch.s == FIRST1 and ch.first:
                    eng.wait_ge(h_used, ROUND + ch.gf * NPS)
                eng.wait_ge(hid1_ready, ROUND + ch.g * NJ + j + 1)
                eng.wait_ge(h1_used, ROUND + ch.g * NJ + reader(j, NH1, NJ))
                eng.tensor_copy(h_hi[:, j % NH1, :], hid[:, j % NHID, :]).then_inc(hi1v_ready, 1)
                eng.wait_ge(hi1v_ready, ch.g * (NJ // 2) + j // 2 + 1)
                eng.tensor_tensor(h_lo[:, j % NH1, :], hid[:, j % NHID, :], h_hi[:, j % NH1, :].bitcast(F32),
                                  ALU.subtract).then_inc(lo1v_ready, 1)
            d = j - LAG - 1
            if d >= 0 and d % HC == HC - 1:
                combine(eng, ch, d // HC)

        def normalise(eng, ch, quad):
            rden = ch.mem.rden
            o = bank[4][:, 0:NT * QUAD * VC].rearrange("p (n c) -> p n c", c=VC)
            eng.wait_ge(o_tok, NQ * ch.ga + quad + 1)
            if ch.causal:
                eng.reciprocal(rden[:, 1, :], o[:, :, HD]).then_inc(rden_ready, 1)
            else:
                eng.tensor_scalar(rden[:, 0, :], o[:, :, HD], KERN_EPS, None, ALU.add).then_inc(eps_added, 1)
                eng.wait_ge(eps_added, NQ * ch.g + quad + 1)
                eng.reciprocal(rden[:, 1, :], rden[:, 0, :]).then_inc(rden_ready, 1)
            eng.wait_ge(rden_ready, NQ * ch.ga + quad + 1)
            if quad == 0:
                eng.wait_ge(aT_ps, ONE + ch.ga)
            eng.tensor_tensor(
                ch.mem.attn[:, :, quad * QUAD:(quad + 1) * QUAD, :],
                o[:, :, 0:HD].rearrange("p (t h) d -> p t h d", h=QUAD),
                rden[:, 1, :].rearrange("p (t h) -> p t h", h=QUAD).unsqueeze(3).broadcast_to([P, NT, QUAD, HD]),
                ALU.mult).then_inc(attn_ready, 1)

        def maxima(eng, ch, half):
            st, m = m_steps, ch.mem
            if half == 0:
                st.begin(ch.g)
            eng.wait_ge(s_used, (ch.g * H + (half + 1) * HALF) * NT)
            eng.wait_ge(mT_ps, ONE + 2 * ch.g + half)
            v = st.mark(eng.tensor_scalar(m.nmax[:, 0, :, :], m.rmax[:, :, half * HALF:(half + 1) * HALF], -1.0, None, ALU.mult))
            eng.wait_ge(st.sem, v)
            v = st.mark(eng.tensor_copy(m.mparts[:, :, 0, :], m.nmax[:, 0, :, :]))
            eng.wait_ge(st.sem, v)
            v = st.mark(eng.tensor_tensor(m.nmax[:, 1, :, :], m.nmax[:, 0, :, :], m.mparts[:, :, 0, :], ALU.subtract))
            eng.wait_ge(st.sem, v)
            v = st.mark(eng.tensor_copy(m.mparts[:, :, 1, :], m.nmax[:, 1, :, :]))
            eng.wait_ge(st.sem, v)
            st.mark(eng.tensor_tensor(m.mparts[:, :, 2, :], m.nmax[:, 1, :, :], m.mparts[:, :, 1, :], ALU.subtract))
            if half:
                st.end()

        def dve_attn(eng, ch, slot):
            if ch.causal and slot < H:
                for qt in range(NT):
                    eng.wait_ge(s_ready, ch.g * H * NT + slot * NT + qt + 1)
                    eng.tensor_reduce(ch.mem.rmax[:, qt, slot:slot + 1], bank[qt][:, 0:(qt + 1) * P], AX_X, ALU.max).then_inc(s_used, 1)
                if slot % HALF == HALF - 1:
                    maxima(eng, ch, slot // HALF)
                return
            h = slot - (H if ch.causal else 0)
            if h >= QUAD and h % QUAD == QUAD - 1:
                normalise(eng, ch, h // QUAD - 1)
            for kb in range(NT):
                i = h * NT + kb
                slot_, w = i % RING, (S - kb * P if ch.causal else S)
                if ch.causal:
                    eng.wait_ge(p0_full, ch.g * H * NT + i + 1)
                    eng.wait_ge(pv_used, ROUND + ch.ga * H * NT + reader(i, RING, H * NT))
                    eng.tensor_copy(p_hi[:, slot_, 0:w], mem0.p_full[:, kb, 0:w]).then_inc(p0_hi, 1)
                    if kb % 2 == 0:
                        eng.wait_ge(p0_hi, ch.g * H * NT + i + 1)
                        eng.tensor_tensor(p_lo[:, slot_, 0:w], mem0.p_full[:, kb, 0:w], p_hi[:, slot_, 0:w].bitcast(F32),
                                          ALU.subtract).then_inc(p0_lo_dve, 1)
                elif kb != POOL_KB:
                    eng.wait_ge(p1_hi, ch.g * H * NT + i + 1)
                    settle(eng)
                    eng.scalar_tensor_tensor(p_lo[:, slot_, :], bank[kb][:, :], 0.0, p_hi[:, slot_, :].bitcast(F32),
                                             ALU.max, ALU.subtract).then_inc(p1_lo, 1)

        def dve_tail(eng, step, ch):
            if step == "combine":
                combine(eng, ch, E1 - 1)
            if step == "x_up":
                eng.wait_ge(y_tok, ch.gf + 1)
                settle(eng)
                eng.scalar_tensor_tensor(xs_of(ch), bank6[:, :].rearrange("p (t d) -> p t d", d=D), 0.5, xs_of(ch),
                                         ALU.mult, ALU.add).then_inc(x_done, 1)
            if step == "norm_last":
                normalise(eng, ch, NQ - 1)
            if step == "aT_lo":
                eng.wait_ge(aT_hi_ready, ch.ga + 1)
                eng.tensor_tensor(ch.mem.aT_lo[:, :], aT_mix[:, :] if ch.causal else bank7[:, :],
                                  ch.mem.aT_hi[:, :].bitcast(F32), ALU.subtract).then_inc(aT_lo_ready, 1)
            ob = bank7[:, :].rearrange("p (t d) -> p t d", d=D)
            if step == "res" and ch.causal:
                eng.wait_ge(o_ps, ch.ga + 1)
                eng.wait_ge(x_biased, ch.ga + 1)
                eng.tensor_tensor(xs_of(ch), ob, xs_of(ch), ALU.add).then_inc(x_done, 1)
            if step == "y_norm":
                st = tail
                st.begin(ch.g)
                eng.wait_ge(o_ps, ch.ga + 1)
                eng.wait_ge(kept, ch.g + 1)
                v = st.mark(eng.tensor_tensor(xk[:, :, :], ob, xk[:, :, :], ALU.add))
                eng.wait_ge(st.sem, v)
                for t in range(NT):
                    v = st.mark(eng.bn_stats(stats[:, t, :], xk[:, t, :]))
                eng.wait_ge(st.sem, v)
                settle(eng)
                for t in range(NT):
                    v = st.mark(eng.bn_aggr(y_mv[:, t, :], stats[:, t, :]))
                eng.wait_ge(st.sem, v)
                eng.tensor_scalar(y_ve[:, :], y_mv[:, :, 1], LN_EPS, None, ALU.add).then_inc(y_var, 1)
            if step == "y_scale":
                eng.wait_ge(y_rstd_ready, ch.g + 1)
                for t in range(NT):
                    v = tail.mark(eng.tensor_scalar(xk[:, t, :], xk[:, t, :], y_mv[:, t, 0:1], y_rstd[:, t:t + 1],
                                                    ALU.subtract, ALU.mult))
                tail.end()

        def pool_prep(eng, step, ch):
            if step == "rstd":
                eng.wait_ge(ln_steps.sem, ch.G * 13 + 9)
                eng.tensor_tensor(rstd[:, :], ve[:, :], mhalf[:, :], ALU.pow).then_inc(rstd_ready, 1)
            if step in ("rest0", "rest1"):
                n = int(step[4])
                mem = ch.mem
                for i in range(2):
                    eng.wait_ge(cut_ready, 6 * ch.ga + 2 * n + i + 1)
                    src = mem.qkv[:, i, :] if n == 0 else mem.res[:, i, :]
                    eng.tensor_tensor(mem.res[:, i, :], src, mem.parts[:, i, n, :], ALU.subtract).then_inc(rest_ready, 1)

        def pool_tail(eng, step, ch):
            if step == "y_rstd":
                eng.wait_ge(y_var, ch.g + 1)
                eng.tensor_tensor(y_rstd[:, :], y_ve[:, :], mhalf[:, :], ALU.pow).then_inc(y_rstd_ready, 1)
            if step == "y_add":
                eng.wait_ge(tail.sem, 13 * ch.g + 13)
                eng.tensor_tensor(xk[:, :, :], xk[:, :, :], row_of(2), ALU.mult).then_inc(y_scaled, 1)
                eng.wait_ge(y_scaled, ch.g + 1)
                eng.wait_ge(x_biased, ch.ga + 1)
                eng.tensor_tensor(xs_of(ch), xs_of(ch), xk[:, :, :], ALU.add).then_inc(x_done, 1)

        def pool_attn(eng, ch, slot):
            def p_lo_pool(h):
                for kb in range(1, NT, 2):
                    i = h * NT + kb
                    w = S - kb * P
                    eng.wait_ge(p0_hi, ch.g * H * NT + i + 1)
                    eng.tensor_tensor(p_lo[:, i % RING, 0:w], mem0.p_full[:, kb, 0:w], p_hi[:, i % RING, 0:w].bitcast(F32),
                                      ALU.subtract).then_inc(p0_lo_pool, 1)

            def p_lo_last(h):
                slot_ = (h * NT + POOL_KB) % RING
                eng.wait_ge(p1_copy, ch.g * H + h + 1)
                eng.tensor_tensor(p_lo[:, slot_, :], p_copy[:, :], p_hi[:, slot_, :].bitcast(F32), ALU.subtract).then_inc(p1_lo_pool, 1)

            h = slot - (H if ch.causal else 0)
            if slot == BIAS_AT:
                eng.wait_ge(ln_steps.sem, ch.G * 13 + 13)
                eng.tensor_tensor(xs_of(ch), xs_of(ch), row_of(0 if ch.causal else 3), ALU.add).then_inc(x_biased, 1)
            if h < 0:
                return
            if h == 0 and ch.first:
                eng.wait_ge(x_done, ONE + ch.s * NB)
                eng.memset(v_pad[:, :, :, :].bitcast(F32), 0.0).then_inc(pool_init, 1)
                eng.wait_ge(pool_init, 2 + ch.stages_before("attn"))
            if h == 0:
                eng.wait_ge(v_lo_ready, ch.ga + 1)
            for n in (0, 1) if h == 0 else (h + 1,):
                if n < H:
                    eng.wait_ge(pv_used, ROUND + (ch.ga * H + n - QUAD + 1) * NT)
                    settle(eng)
                    at = 32 * (n % QUAD)
                    eng.tensor_copy(v_pad[:, n % QUAD, :, at:at + 2 * VC],
                                    ch.mem.v_parts[:, ch.parity, n:NT * H:H, :].bitcast(F32)).then_inc(v_pad_ready, 1)
            if ch.causal:
                if h:
                    p_lo_pool(h - 1)
                if h == H - 1:
                    p_lo_pool(h)
            else:
                p_lo_last(h)
            if not ch.causal and slot == KEEP_AT:
                eng.wait_ge(ln_steps.sem, ch.G * 13 + 13)
                if not ch.first:
                    eng.wait_ge(x_done, ONE + ch.G)
                eng.tensor_tensor(xk[:, :, :], xn[:, :, :], row_of(1), ALU.add).then_inc(kept, 1)

        def pool_main(eng, ch, slot):
            if ch.kind == "ffn0":
                p = slot
                eng.wait_ge(hi_ready, ch.g * NPS + p + 1)
                eng.tensor_tensor(h_lo[:, p % NH0, :], hid[:, p % NHID, :], h_hi[:, p % NH0, :].bitcast(F32),
                                  ALU.subtract).then_inc(lo_ready, 1)
            elif ch.kind == "ffn1":
                j = slot
                if j % 2 == 0:
                    eng.wait_ge(hi1a_ready, ch.g * (NJ // 2) + j // 2 + 1)
                    eng.tensor_tensor(h_lo[:, j % NH1, :], hid[:, j % NHID, :], h_hi[:, j % NH1, :].bitcast(F32),
                                      ALU.subtract).then_inc(lo1p_ready, 1)
            else:
                pool_attn(eng, ch, slot)

        def stack_parts(eng, ch):
            mem, ga = ch.mem, ch.ga
            for i, r in sorted(((i, r) for i in range(2) for r in range(PAIRS)), key=lambda at: PART_OF[at[0]][at[1]]):
                    part_of = PART_OF[i]
                    eng.wait_ge(cut_ready, 6 * ch.ga + 2 * part_of[r] + i + 1)
                    eng.dma_start(scratch[bass.ds(ch.ga, 1), i, :, r * HD:(r + 1) * HD, :].rearrange("g h d s -> (g h) d s"),
                                  mem.parts[:, i, part_of[r], :]).then_inc(scr_w, 16)
            eng.wait_ge(scr_w, ch.ga * 192 + 192)
            for half in range(2):
                if not ch.first:
                    eng.wait_ge(st_ready, (ch.ga * H - H + (half + 1) * HALF) * NT)
                for i, st in enumerate((mem.q_st, mem.k_st)):
                    for par in range(2):
                        src = scratch[bass.ds(ch.ga, 1), i, :, :, :].rearrange(
                            "g (hf j two) p s -> g hf two p j s", hf=2, two=2)[0, half, par]
                        p0 = par * STACK
                        eng.dma_start(st[p0:p0 + QK_ROWS, half * 4:half * 4 + 4, :], src).then_inc(st_in[half], 16)

        def mix_heads(eng, ch):
            eng.wait_ge(perm_ready, ch.ga + 1)
            eng.dma_start(mixed[bass.ds(ch.ga, 1), :, :].rearrange("g p s -> (g p) s"), ch.mem.aT_perm[:, :]).then_inc(perm_out, 16)
            eng.wait_ge(perm_out, 16 * (ch.ga + 1))
            eng.dma_start(aT_mix[:, :].rearrange("p (h r) -> p h r", h=H),
                          mixed[bass.ds(ch.ga, 1), :, :].rearrange("g (h d) (q r) -> g (d q) h r", d=HD, q=GQ)[0]).then_inc(mix_in, 16)

        def max_rows(eng, ch):
            for half in range(2):
                eng.wait_ge(mT_ready, 2 * ch.g + half + 1)
                for i in range(NPART):
                    for par in range(2):
                        p0 = par * STACK + MAX_ROW + i
                        eng.dma_start(ch.mem.q_st[p0:p0 + 1, half * 4:half * 4 + 4, :],
                                      ch.mem.mT[i * HALF + par:i * HALF + HALF:2, half, :]).then_inc(m_in[half], 16)

        def dma_body(eng, s, c):
            ch = Chunk(s, c)
            before, after = ch.before(), ch.after()
            if before is not None and before.kind == "attn0":
                mix_heads(eng, before)
            if s == FIRST1 - 1:
                if ch.first:
                    eng.wait_ge(x_done, ONE + s * NB)
                for i in range(NW1_LOADS):
                    eng.wait_ge(w1_lo_done, ONE + NW1_LOADS * ch.c + i)
                    eng.dma_start(stage_w1[:, :], w1[:, bass.ds((NW1_LOADS * ch.c + i) * LOAD1, LOAD1)]).then_inc(w1_in, 16)
            if ch.kind == "attn0":
                max_rows(eng, ch)
            if after is not None and after.kind[:4] == "attn":
                stack_parts(eng, after)

        block = ctx.enter_context(nc.Block())

        @block.sync
        def _(eng):
            eng.dma_start(x[:, :, :], x_in).then_inc(x_in_sem, 16)
            eng.dma_start(stage_c[:, :], consts).then_inc(small_in, 16)
            eng.dma_start(bias[:, :], biases).then_inc(small_in, 16)
            eng.dma_start(row[:, :, :], rows).then_inc(small_in, 16)
            eng.dma_start(stage_bd[:, 0, :], bd3).then_inc(small_in, 16)
            for n, (src, _, _, cols) in enumerate(loads):
                if n >= 4:
                    eng.wait_ge(w_lo_done, n - 3)
                eng.dma_start(stage_w[:, n % 4, 0:cols], src).then_inc(w_in[n % 4], 16)
            for s in range(len(STAGES)):
                dma_body(eng, s, 0)
                with eng.Fori(1, NB - 1) as c:
                    dma_body(eng, s, c)
                dma_body(eng, s, NB - 1)
            s = len(STAGES) - 1
            with eng.Fori(0, NB) as c:
                eng.wait_ge(x_done, ONE + s * NB + c + 1)
                eng.dma_start(out[:, bass.ds(c * NT, NT), :], x[:, bass.ds(c * NT, NT), :]).then_inc(out_sem, 16)
            eng.wait_ge(out_sem, 16 * NB)

        @block.gpsimd
        def _(eng):
            for counts in (lo_ready, lo1p_ready, p0_lo_pool, p1_lo_pool):
                eng.sem_inc(counts, ROUND)
            eng.memset(mhalf[:, :], -0.5).then_inc(pool_init, 1)
            eng.wait_ge(pool_init, 1)
            run(eng, "pool", pool_prep, pool_tail, pool_main)

        @block.scalar
        def _(eng):
            for counts in (silu_ready, rb_ready, hid1_ready):
                eng.sem_inc(counts, ROUND)
            eng.wait_ge(small_in, 64)
            eng.activation(ident[:, :], stage_c[:, C_ID:C_ID + P], ACT.Copy).then_inc(const_ready, 1)
            eng.activation(osel[:, :], stage_c[:, C_OSEL:C_OSEL + QUAD * VC], ACT.Copy).then_inc(const_ready, 1)
            eng.activation(cbf[:, :], stage_c[:, 0:NCONST], ACT.Copy).then_inc(const_ready, 1)
            for n, (_, hi, _, cols) in enumerate(loads):
                eng.wait_ge(w_in[n % 4], 16 * (n // 4 + 1))
                eng.activation(hi, stage_w[:, n % 4, 0:cols], ACT.Copy).then_inc(w_hi_done, 1)
            eng.wait_ge(w_lo_done, len(loads))

            def main(eng, ch, slot):
                if ch.kind == "ffn0":
                    act_ffn0(eng, ch, slot)
                elif ch.kind == "ffn1":
                    act_ffn1(eng, ch, slot)
                else:
                    act_attn(eng, ch, slot)

            run(eng, "act", act_prep, act_tail, main)

        @block.vector
        def _(eng):
            for counts in (x_done, w1_lo_done):
                eng.sem_inc(counts, ONE)
            for counts in (prod_ready, hid_ready, ze_ready, acc_ready, lo1v_ready, p0_lo_dve):
                eng.sem_inc(counts, ROUND)
            eng.wait_ge(small_in, 64)
            bd_steps = Steps(sem("bd_steps"), 2 * NPART - 1)
            bd_steps.begin(0)
            for j in range(NPART):
                src = stage_bd[:, 0, :] if j == 0 else stage_bd[:, 1, :]
                v = bd_steps.mark(eng.tensor_copy(bd_parts[:, j, :], src))
                eng.wait_ge(bd_steps.sem, v)
                if j < NPART - 1:
                    v = bd_steps.mark(eng.tensor_tensor(stage_bd[:, 1, :], src, bd_parts[:, j, :], ALU.subtract))
                    eng.wait_ge(bd_steps.sem, v)
            bd_steps.end()
            for e in range(E1):
                eng.memset(iota8[:, :, e], float(e)).then_inc(const_ready, 1)
            for n, (_, hi, lo, cols) in enumerate(loads):
                eng.wait_ge(w_hi_done, n + 1)
                eng.tensor_tensor(lo, stage_w[:, n % 4, 0:cols], hi.bitcast(F32), ALU.subtract).then_inc(w_lo_done, 1)
            eng.wait_ge(x_in_sem, 16)
            eng.wait_ge(w_lo_done, len(loads))

            def ones(s):
                if s + 1 < len(STAGES) and STAGES[s + 1][:4] == "attn":
                    mem = mem0 if STAGES[s + 1] == "attn0" else mem1
                    eng.wait_ge(x_done, ONE + s * NB)
                    eng.memset(mem.k_st[:, :, :], 1.0).then_inc(const_ready, 1)
                    eng.memset(mem.v_parts[:, :, :, HD:VC].bitcast(F32), 1.0).then_inc(const_ready, 1)
                    eng.memset(mem.v_parts[:, :, :, VC + HD:2 * VC].bitcast(F32), 0.0).then_inc(const_ready, 1)

            def main(eng, ch, slot):
                if ch.kind == "ffn0":
                    dve_ffn0(eng, ch, slot)
                elif ch.kind == "ffn1":
                    dve_ffn1(eng, ch, slot)
                else:
                    dve_attn(eng, ch, slot)

            run(eng, "dve", dve_prep, dve_tail, main, ones)

        @block.tensor
        def _(eng):
            for counts in (mT_ps, aT_ps, xnT_ps):
                eng.sem_inc(counts, ONE)
            for counts in (h_used, h1_used, pv_used):
                eng.sem_inc(counts, ROUND)
            eng.wait_ge(const_ready, 3 + E1)
            eng.wait_ge(w_lo_done, len(loads))

            def main(eng, ch, slot):
                if ch.kind == "ffn0":
                    pe_ffn0(eng, ch, slot)
                elif ch.kind == "ffn1":
                    pe_ffn1(eng, ch, slot)
                else:
                    pe_attn(eng, ch, slot)

            run(eng, "pe", pe_prep, pe_tail, main)


def _layout(i):
    pad = lambda a, n: np.concatenate([a, np.zeros(a.shape[:-1] + (n - a.shape[-1],), a.dtype)], -1)
    f = {k: np.asarray(v) for k, v in i.items()}
    cols = lambda w: np.moveaxis(w, 0, 1).reshape(D, -1)
    w0 = np.concatenate([
        cols(f["L0_ffn_Wg"]), pad(f["L0_ffn_Wg_s"], P), cols(f["L0_ffn_Wu"]), pad(f["L0_ffn_Wu_s"], P),
        f["L0_ffn_Wd"].reshape(NP, P, D).transpose(1, 0, 2).reshape(P, -1), pad(f["L0_ffn_Wd_s"].T, P).T,
        pad(f["L0_ffn_Wr"], P)], 1)
    w1 = np.concatenate([
        pad(f["L1_ffn_Wr"], P), cols(f["L1_ffn_W1"]), f["L1_ffn_W2"].reshape(NJ, P, D).transpose(1, 0, 2).reshape(P, -1)], 1)
    qkv1 = f["L1_attn_w_qkv"].reshape(D, H, 3, HD).transpose(0, 2, 1, 3).reshape(D, 3 * D)
    wa = np.concatenate([f["L0_attn_Wq"], f["L0_attn_Wk"], f["L0_attn_Wv"], f["L0_attn_Wo"].reshape(GQ, HD, D).transpose(1, 0, 2).reshape(D, D), qkv1, f["L1_attn_w_out"]], 1)
    col = lambda v: pad(v.reshape(1, -1), -(-v.size // P) * P).reshape(-1, P).T
    biases = np.concatenate([
        col(f["L0_ffn_bg"]), col(f["L0_ffn_bg_s"]), col(f["L0_ffn_bu"]), col(f["L0_ffn_bu_s"]), col(f["L0_ffn_bd_s"]),
        col(f["L0_ffn_br"]), col(f["L1_ffn_b1"]), col(f["L1_ffn_b2"]), col(f["L1_ffn_br"])], 1)
    bd3 = np.tile(f["L0_ffn_bd"], (NPART, 1))
    rows = np.tile(np.stack([f["L0_attn_bo"], f["L1_attn_b_out"], f["L1_attn_gamma"], f["L1_attn_beta"]])[None], (P, 1, 1))
    r = np.arange(P)
    consts = np.zeros((P, NCONST_ALL), np.float32)
    consts[r, C_ID + r] = 1
    consts[:, C_NEG:C_NEG + P] = np.where(r[None, :] > r[:, None], -1e30, 0)
    consts[:, C_NEGT:C_NEGT + P] = consts[:, C_NEG:C_NEG + P].T
    for j in range(QUAD):
        for c in range(2 * VC):
            consts[32 * j + c, C_OSEL + j * VC + c % VC] = 1
    for part in range(NPART):
        for e in range(E0):
            at = C_SEL0 + e * I0
            consts[part * E0 + e, at:at + I0] = 1
        for e in range(E1):
            consts[part * E1 + e, C_SEL1 + e * P:C_SEL1 + (e + 1) * P] = 1
    x = f["L0_attn_x"].reshape(NB * NT, P, D).transpose(1, 0, 2)
    return dict(x=x, w0=w0, w1=w1, wa=wa, biases=biases, bd3=bd3, rows=rows, consts=consts)


def kernel(**inputs):
    import concourse.bacc as _bacc
    from concourse.bass_utils import run_bass_kernel_spmd as _run

    nc = _bacc.Bacc("TRN2", target_bir_lowering=False, num_devices=1)
    arrays, args = {}, []
    for name, a in _layout(inputs).items():
        a = np.ascontiguousarray(a)
        arrays[f"in_{name}_dram"] = a
        args.append(nc.dram_tensor(f"in_{name}_dram", a.shape, mybir.dt.from_np(a.dtype), kind="ExternalInput").ap())
    out = nc.dram_tensor("out_0_dram", (P, NB * NT, D), F32, kind="ExternalOutput").ap()
    scratch = nc.dram_tensor("parts_dram", (2 * NB, 2, H, QK_ROWS, S), BF16, kind="Internal").ap()
    mixed = nc.dram_tensor("mixed_dram", (NB, P, S), F32, kind="Internal").ap()
    build(nc, *args, out, scratch, mixed)
    r = _run(nc, [arrays], core_ids=[0])
    o = r.results[0]["out_0_dram"]
    return o.transpose(1, 0, 2).reshape(NB, S, D)
```
